# Optimizing a Trainium2 kernel written in Bass

```python
import numpy as np
import jax
import jax.numpy as jnp

def _softmax(x, axis=-1):
    return jax.nn.softmax(x, axis=axis)

def _gelu(x):
    return jax.nn.gelu(x, approximate=True)

def _silu(x):
    return jax.nn.silu(x)

def _sigmoid(x):
    return jax.nn.sigmoid(x)

def _layernorm(x, axis=-1, eps=1e-05):
    m = jnp.mean(x, axis=axis, keepdims=True)
    v = jnp.var(x, axis=axis, keepdims=True)
    return (x - m) / jnp.sqrt(v + eps)

def _scatter_add(tgt, idx, src, axis=0):
    return tgt.at[idx].add(src)

def _segment_sum(src, seg, n):
    return jax.ops.segment_sum(src, seg, n)
kernel_name = 'mk_seq_preln_d4_jaxref_r8_8fc7a2'

def setup_inputs(seed: int=0):
    np.random.seed(seed)
    _w = jnp.asarray

    def _L0_attn_setup():
        import jax, jax.numpy as jnp
        import numpy as np
        B, L, D, H, W = (2, 512, 128, 16, 128)
        E = D // H

        def _ln(x, g, b):
            m = jnp.mean(x, axis=-1, keepdims=True)
            v = jnp.mean((x - m) ** 2, axis=-1, keepdims=True)
            return (x - m) / jnp.sqrt(v + 1e-05) * g + b

        def _swa(xn, Wqkv, bqkv, Wp, bp):
            b_, l_, d_ = xn.shape
            nb = l_ // W
            qkv = xn @ Wqkv + bqkv
            q, k, v = jnp.split(qkv, 3, axis=-1)

            def heads(t):
                return t.reshape(b_, l_, H, E).transpose(0, 2, 1, 3)
            q, k, v = (heads(q), heads(k), heads(v))

            def blk(t):
                return t.reshape(b_, H, nb, W, E)
            qb, kb, vb = (blk(q), blk(k), blk(v))
            kprev = jnp.pad(kb, ((0, 0), (0, 0), (1, 0), (0, 0), (0, 0)))[:, :, :nb]
            vprev = jnp.pad(vb, ((0, 0), (0, 0), (1, 0), (0, 0), (0, 0)))[:, :, :nb]
            kc = jnp.concatenate([kprev, kb], axis=3)
            vc = jnp.concatenate([vprev, vb], axis=3)
            scores = jnp.einsum('bhnre,bhnse->bhnrs', qb, kc) / np.float32(np.sqrt(E))
            r = jnp.arange(W)[:, None]
            s = jnp.arange(2 * W)[None, :]
            band = (s >= r + 1) & (s <= r + W)
            first = band & (s >= W)
            mask = jnp.concatenate([first[None], jnp.broadcast_to(band, (nb - 1, W, 2 * W))], axis=0)
            scores = jnp.where(mask[None, None], scores, jnp.float32(-1e+30))
            attn = jax.nn.softmax(scores, axis=-1)
            out = jnp.einsum('bhnrs,bhnse->bhnre', attn, vc)
            out = out.reshape(b_, H, l_, E).transpose(0, 2, 1, 3).reshape(b_, l_, d_)
            return out @ Wp + bp

        def _linattn(xn, Wqkv, bqkv, Wo, bo):
            b_, l_, d_ = xn.shape
            C = 128
            nc = l_ // C
            qkv = xn @ Wqkv + bqkv
            q, k, v = jnp.split(qkv, 3, axis=-1)
            q = q.reshape(b_, l_, H, E)
            k = k.reshape(b_, l_, H, E)
            v = v.reshape(b_, l_, H, E)
            q = jax.nn.elu(q * np.float32(E ** (-0.5))) + np.float32(1.0001)
            k = jax.nn.elu(k) + np.float32(1.0001)

            def chunks(t):
                return t.reshape(b_, nc, C, H, E).transpose(1, 0, 3, 2, 4)
            qc, kc, vc = (chunks(q), chunks(k), chunks(v))
            tril = jnp.tril(jnp.ones((C, C), jnp.float32))

            def step(carry, inp):
                S, z = carry
                qi, ki, vi = inp
                A = jnp.einsum('bhce,bhde->bhcd', qi, ki) * tril
                num = jnp.einsum('bhce,bhef->bhcf', qi, S) + jnp.einsum('bhcd,bhdf->bhcf', A, vi)
                den = jnp.einsum('bhce,bhe->bhc', qi, z) + A.sum(-1)
                o = num / (den[..., None] + 1e-06)
                S = S + jnp.einsum('bhce,bhcf->bhef', ki, vi)
                z = z + ki.sum(2)
                return ((S, z), o)
            S0 = jnp.zeros((b_, H, E, E), jnp.float32)
            z0 = jnp.zeros((b_, H, E), jnp.float32)
            _, out = jax.lax.scan(step, (S0, z0), (qc, kc, vc))
            out = out.transpose(1, 0, 3, 2, 4).reshape(b_, l_, d_)
            return out @ Wo + bo
        key = jax.random.key(seed)
        ks = jax.random.split(key, 9)

        def w(k, shape, s=0.02):
            return jax.random.normal(k, shape, jnp.float32) * s
        return {'x': jax.random.normal(ks[0], (B, L, D), jnp.float32), 'g1': jnp.ones((D,), jnp.float32), 'b1': jnp.zeros((D,), jnp.float32), 'Wqkv_a': w(ks[1], (D, 3 * D)), 'bqkv_a': jnp.zeros((3 * D,), jnp.float32), 'Wp_a': w(ks[2], (D, D)), 'bp_a': jnp.zeros((D,), jnp.float32), 'Wqkv_s': w(ks[3], (D, 3 * D)), 'bqkv_s': jnp.zeros((3 * D,), jnp.float32), 'Wo_s': w(ks[4], (D, D)), 'bo_s': jnp.zeros((D,), jnp.float32), 'Wo': w(ks[5], (D, D)), 'bo': jnp.zeros((D,), jnp.float32), 'gm': jnp.ones((D,), jnp.float32), 'bm': jnp.zeros((D,), jnp.float32), 'W1': w(ks[6], (D, 4 * D)), 'b1m': jnp.zeros((4 * D,), jnp.float32), 'W2': w(ks[7], (4 * D, D)), 'b2m': jnp.zeros((D,), jnp.float32)}
    _L0_attn_in = _L0_attn_setup()

    def _L0_ffn_setup():
        import jax, jax.numpy as jnp
        import numpy as np
        HIDDEN_SIZE = 128
        NUM_EXPERTS = 8
        MOE_INTERMEDIATE_SIZE = 176
        NUM_EXPERTS_PER_TOK = 2
        SHARED_EXPERT_INTERMEDIATE_SIZE = 352
        B, T = (2, 128)
        W_SCALE = 0.02
        key = jax.random.key(seed)
        ks = jax.random.split(key, 8)
        H, E, I, SI = (HIDDEN_SIZE, NUM_EXPERTS, MOE_INTERMEDIATE_SIZE, SHARED_EXPERT_INTERMEDIATE_SIZE)
        return {'x': jax.random.normal(ks[0], (B, T, H), jnp.float32), 'gate_w': jax.random.normal(ks[1], (E, H), jnp.float32) * W_SCALE, 'experts_gate_up': jax.random.normal(ks[2], (E, 2 * I, H), jnp.float32) * W_SCALE, 'experts_down': jax.random.normal(ks[3], (E, H, I), jnp.float32) * W_SCALE, 'shared_gate_w': jax.random.normal(ks[4], (SI, H), jnp.float32) * W_SCALE, 'shared_up_w': jax.random.normal(ks[5], (SI, H), jnp.float32) * W_SCALE, 'shared_down_w': jax.random.normal(ks[6], (H, SI), jnp.float32) * W_SCALE, 'shared_expert_gate_w': jax.random.normal(ks[7], (1, H), jnp.float32) * W_SCALE}
    _L0_ffn_in = _L0_ffn_setup()

    def _L1_attn_setup():
        import jax, jax.numpy as jnp
        import numpy as np
        D_MODEL = 128
        N_HEADS = 16
        D_HEAD = D_MODEL // N_HEADS
        EPS_LN = 1e-05
        EPS_GATE = 1e-05
        EPS_DEN = 1e-05

        def _linear(x, w, b):
            return jnp.einsum('btd,od->bto', x, w) + b
        key = jax.random.key(seed)
        ks = jax.random.split(key, 4)
        B, T, D = (1, 256, D_MODEL)
        x = jax.random.normal(ks[0], (B, T, D), dtype=jnp.float32)
        s = 1.0 / np.sqrt(D)
        qkv_w = jax.random.normal(ks[1], (3 * D, D), dtype=jnp.float32) * s
        gate_w = jax.random.normal(ks[2], (D, D), dtype=jnp.float32) * s
        proj_w = jax.random.normal(ks[3], (D, D), dtype=jnp.float32) * s
        return {'x': x, 'ln_g': jnp.ones((D,), jnp.float32), 'ln_b': jnp.zeros((D,), jnp.float32), 'qkv_w': qkv_w, 'qkv_b': jnp.zeros((3 * D,), jnp.float32), 'gate_w': gate_w, 'gate_b': jnp.zeros((D,), jnp.float32), 'proj_w': proj_w, 'proj_b': jnp.zeros((D,), jnp.float32)}
    _L1_attn_in = _L1_attn_setup()

    def _L1_ffn_setup():
        import jax, jax.numpy as jnp
        import numpy as np
        E = 16
        K = 4
        NG = 4
        TG = 2
        SCALE = 2.5
        NORM_TOPK = True
        H = 128
        I = 64
        SH_I = I * 2
        B, S = (2, 256)
        key = jax.random.key(seed)
        ks = jax.random.split(key, 9)

        def w(k, shape, fan_in):
            return jax.random.normal(k, shape, jnp.float32) * (1.0 / np.sqrt(fan_in))
        return {'hidden_states': jax.random.normal(ks[0], (B, S, H), jnp.float32), 'gate_w': w(ks[1], (E, H), H), 'gate_bias': jnp.zeros((E,), jnp.float32), 'Wg': w(ks[2], (E, I, H), H), 'Wu': w(ks[3], (E, I, H), H), 'Wd': w(ks[4], (E, H, I), I), 'Ws_g': w(ks[5], (SH_I, H), H), 'Ws_u': w(ks[6], (SH_I, H), H), 'Ws_d': w(ks[7], (H, SH_I), SH_I)}
    _L1_ffn_in = _L1_ffn_setup()

    def _L2_attn_setup():
        import jax, jax.numpy as jnp
        import numpy as np
        B, S, D, N = (8, 512, 128, 64)
        EPS = 1e-05
        key = jax.random.key(seed)
        ks = jax.random.split(key, 6)
        sD = 1.0 / np.sqrt(D)
        sN = 1.0 / np.sqrt(N)
        return {'x': jax.random.normal(ks[0], (B, S, D), dtype=jnp.float32), 'ln_w': jnp.ones((D,), jnp.float32), 'ln_b': jnp.zeros((D,), jnp.float32), 'Wi': jax.random.normal(ks[1], (N, D), jnp.float32) * sD, 'bi': jnp.zeros((N,), jnp.float32), 'Wf': jax.random.normal(ks[2], (N, D), jnp.float32) * sD, 'bf': jnp.zeros((N,), jnp.float32), 'Wz': jax.random.normal(ks[3], (N, D), jnp.float32) * sD, 'bz': jnp.zeros((N,), jnp.float32), 'Wo': jax.random.normal(ks[4], (N, D), jnp.float32) * sD, 'bo': jnp.zeros((N,), jnp.float32), 'Wp': jax.random.normal(ks[5], (D, N), jnp.float32) * sN, 'bp': jnp.zeros((D,), jnp.float32)}
    _L2_attn_in = _L2_attn_setup()

    def _L2_ffn_setup():
        import jax, jax.numpy as jnp
        import numpy as np
        import math
        BETA = 0.9
        THRESHOLD = 1.0
        NUM_STEPS = 5
        ALPHA = 2.0

        @jax.custom_vjp
        def spike_fn(u):
            return (u > 0).astype(u.dtype)

        def _spike_fwd(u):
            return (spike_fn(u), u)

        def _spike_bwd(u, g):
            s = jnp.pi / 2.0 * ALPHA * u
            return (g * (ALPHA / 2.0) / (1.0 + s * s),)
        spike_fn.defvjp(_spike_fwd, _spike_bwd)
        key = jax.random.key(seed)
        k1, k2, k3 = jax.random.split(key, 3)
        n_embd = 128
        x = jax.random.normal(k1, (4, 256, n_embd), dtype=jnp.float32)
        W_fc = jax.random.normal(k2, (4 * n_embd, n_embd), dtype=jnp.float32) / math.sqrt(n_embd)
        W_proj = jax.random.normal(k3, (n_embd, 4 * n_embd), dtype=jnp.float32) / math.sqrt(4 * n_embd)
        return {'x': x, 'W_fc': W_fc, 'W_proj': W_proj}
    _L2_ffn_in = _L2_ffn_setup()

    def _L3_attn_setup():
        import jax, jax.numpy as jnp
        import numpy as np
        D_MODEL = 128
        NUM_HEADS = 16
        DEPTH = D_MODEL // NUM_HEADS

        def _split_heads(x):
            B, S, _ = x.shape
            return x.reshape(B, S, NUM_HEADS, DEPTH).transpose(0, 2, 1, 3)
        key = jax.random.key(seed)
        ks = jax.random.split(key, 9)
        B, S = (2, 256)
        scale = 1.0 / np.sqrt(D_MODEL)
        inputs = jax.random.normal(ks[0], (B, S, D_MODEL), dtype=jnp.float32)
        wq = jax.random.normal(ks[1], (D_MODEL, D_MODEL), dtype=jnp.float32) * scale
        wk = jax.random.normal(ks[2], (D_MODEL, D_MODEL), dtype=jnp.float32) * scale
        wv = jax.random.normal(ks[3], (D_MODEL, D_MODEL), dtype=jnp.float32) * scale
        wo = jax.random.normal(ks[4], (D_MODEL, D_MODEL), dtype=jnp.float32) * scale
        bq = jnp.zeros((D_MODEL,), jnp.float32)
        bk = jnp.zeros((D_MODEL,), jnp.float32)
        bv = jnp.zeros((D_MODEL,), jnp.float32)
        bo = jnp.zeros((D_MODEL,), jnp.float32)
        return {'inputs': inputs, 'wq': wq, 'bq': bq, 'wk': wk, 'bk': bk, 'wv': wv, 'bv': bv, 'wo': wo, 'bo': bo}
    _L3_attn_in = _L3_attn_setup()

    def _L3_ffn_setup():
        import jax, jax.numpy as jnp
        import numpy as np
        E = 8
        K = 2
        LN_EPS = 1e-05

        def _expert_ffn(x, w1, b1, gate, w2, b2):
            h = jax.nn.gelu((x @ w1 + b1) * gate, approximate=False)
            return h @ w2 + b2
        key = jax.random.key(seed)
        B, S, D, F = (4, 256, 128, 512)
        F2 = F // 2
        ks = jax.random.split(key, 8)
        s = 0.02
        return {'hidden_states': jax.random.normal(ks[0], (B, S, D), jnp.float32), 'router_w': jax.random.normal(ks[1], (D, E), jnp.float32) * s, 'router_b': jnp.zeros((E,), jnp.float32), 'w1': jax.random.normal(ks[2], (E, D, F), jnp.float32) * s, 'b1': jnp.zeros((E, F), jnp.float32), 'gate': jnp.ones((E, F), jnp.float32), 'w2': jax.random.normal(ks[3], (E, F, D), jnp.float32) * s, 'b2': jnp.zeros((E, D), jnp.float32), 'sw1': jax.random.normal(ks[4], (D, F2), jnp.float32) * s, 'sb1': jnp.zeros((F2,), jnp.float32), 'sgate': jnp.ones((F2,), jnp.float32), 'sw2': jax.random.normal(ks[5], (F2, D), jnp.float32) * s, 'sb2': jnp.zeros((D,), jnp.float32), 'shared_weight': jnp.float32(0.5), 'ln_g': jnp.ones((D,), jnp.float32), 'ln_b': jnp.zeros((D,), jnp.float32)}
    _L3_ffn_in = _L3_ffn_setup()
    _d = {'L0_attn_x': _L0_attn_in['x'], 'L0_attn_g1': _L0_attn_in['g1'], 'L0_attn_b1': _L0_attn_in['b1'], 'L0_attn_Wqkv_a': _L0_attn_in['Wqkv_a'], 'L0_attn_bqkv_a': _L0_attn_in['bqkv_a'], 'L0_attn_Wp_a': _L0_attn_in['Wp_a'], 'L0_attn_bp_a': _L0_attn_in['bp_a'], 'L0_attn_Wqkv_s': _L0_attn_in['Wqkv_s'], 'L0_attn_bqkv_s': _L0_attn_in['bqkv_s'], 'L0_attn_Wo_s': _L0_attn_in['Wo_s'], 'L0_attn_bo_s': _L0_attn_in['bo_s'], 'L0_attn_Wo': _L0_attn_in['Wo'], 'L0_attn_bo': _L0_attn_in['bo'], 'L0_attn_gm': _L0_attn_in['gm'], 'L0_attn_bm': _L0_attn_in['bm'], 'L0_attn_W1': _L0_attn_in['W1'], 'L0_attn_b1m': _L0_attn_in['b1m'], 'L0_attn_W2': _L0_attn_in['W2'], 'L0_attn_b2m': _L0_attn_in['b2m'], 'L0_ffn_gate_w': _L0_ffn_in['gate_w'], 'L0_ffn_experts_gate_up': _L0_ffn_in['experts_gate_up'], 'L0_ffn_experts_down': _L0_ffn_in['experts_down'], 'L0_ffn_shared_gate_w': _L0_ffn_in['shared_gate_w'], 'L0_ffn_shared_up_w': _L0_ffn_in['shared_up_w'], 'L0_ffn_shared_down_w': _L0_ffn_in['shared_down_w'], 'L0_ffn_shared_expert_gate_w': _L0_ffn_in['shared_expert_gate_w'], 'L1_attn_ln_g': _L1_attn_in['ln_g'], 'L1_attn_ln_b': _L1_attn_in['ln_b'], 'L1_attn_qkv_w': _L1_attn_in['qkv_w'], 'L1_attn_qkv_b': _L1_attn_in['qkv_b'], 'L1_attn_gate_w': _L1_attn_in['gate_w'], 'L1_attn_gate_b': _L1_attn_in['gate_b'], 'L1_attn_proj_w': _L1_attn_in['proj_w'], 'L1_attn_proj_b': _L1_attn_in['proj_b'], 'L1_ffn_gate_w': _L1_ffn_in['gate_w'], 'L1_ffn_gate_bias': _L1_ffn_in['gate_bias'], 'L1_ffn_Wg': _L1_ffn_in['Wg'], 'L1_ffn_Wu': _L1_ffn_in['Wu'], 'L1_ffn_Wd': _L1_ffn_in['Wd'], 'L1_ffn_Ws_g': _L1_ffn_in['Ws_g'], 'L1_ffn_Ws_u': _L1_ffn_in['Ws_u'], 'L1_ffn_Ws_d': _L1_ffn_in['Ws_d'], 'L2_attn_ln_w': _L2_attn_in['ln_w'], 'L2_attn_ln_b': _L2_attn_in['ln_b'], 'L2_attn_Wi': _L2_attn_in['Wi'], 'L2_attn_bi': _L2_attn_in['bi'], 'L2_attn_Wf': _L2_attn_in['Wf'], 'L2_attn_bf': _L2_attn_in['bf'], 'L2_attn_Wz': _L2_attn_in['Wz'], 'L2_attn_bz': _L2_attn_in['bz'], 'L2_attn_Wo': _L2_attn_in['Wo'], 'L2_attn_bo': _L2_attn_in['bo'], 'L2_attn_Wp': _L2_attn_in['Wp'], 'L2_attn_bp': _L2_attn_in['bp'], 'L2_ffn_W_fc': _L2_ffn_in['W_fc'], 'L2_ffn_W_proj': _L2_ffn_in['W_proj'], 'L3_attn_wq': _L3_attn_in['wq'], 'L3_attn_bq': _L3_attn_in['bq'], 'L3_attn_wk': _L3_attn_in['wk'], 'L3_attn_bk': _L3_attn_in['bk'], 'L3_attn_wv': _L3_attn_in['wv'], 'L3_attn_bv': _L3_attn_in['bv'], 'L3_attn_wo': _L3_attn_in['wo'], 'L3_attn_bo': _L3_attn_in['bo'], 'L3_ffn_router_w': _L3_ffn_in['router_w'], 'L3_ffn_router_b': _L3_ffn_in['router_b'], 'L3_ffn_w1': _L3_ffn_in['w1'], 'L3_ffn_b1': _L3_ffn_in['b1'], 'L3_ffn_gate': _L3_ffn_in['gate'], 'L3_ffn_w2': _L3_ffn_in['w2'], 'L3_ffn_b2': _L3_ffn_in['b2'], 'L3_ffn_sw1': _L3_ffn_in['sw1'], 'L3_ffn_sb1': _L3_ffn_in['sb1'], 'L3_ffn_sgate': _L3_ffn_in['sgate'], 'L3_ffn_sw2': _L3_ffn_in['sw2'], 'L3_ffn_sb2': _L3_ffn_in['sb2'], 'L3_ffn_shared_weight': _L3_ffn_in['shared_weight'], 'L3_ffn_ln_g': _L3_ffn_in['ln_g'], 'L3_ffn_ln_b': _L3_ffn_in['ln_b']}
    _x0 = _d['L0_attn_x']
    _d['L0_attn_x'] = jax.random.normal(jax.random.fold_in(jax.random.key(seed), 1), (4, 512, 128), dtype=_x0.dtype)
    del _x0
    return _d

def reference(L0_attn_x, L0_attn_g1, L0_attn_b1, L0_attn_Wqkv_a, L0_attn_bqkv_a, L0_attn_Wp_a, L0_attn_bp_a, L0_attn_Wqkv_s, L0_attn_bqkv_s, L0_attn_Wo_s, L0_attn_bo_s, L0_attn_Wo, L0_attn_bo, L0_attn_gm, L0_attn_bm, L0_attn_W1, L0_attn_b1m, L0_attn_W2, L0_attn_b2m, L0_ffn_gate_w, L0_ffn_experts_gate_up, L0_ffn_experts_down, L0_ffn_shared_gate_w, L0_ffn_shared_up_w, L0_ffn_shared_down_w, L0_ffn_shared_expert_gate_w, L1_attn_ln_g, L1_attn_ln_b, L1_attn_qkv_w, L1_attn_qkv_b, L1_attn_gate_w, L1_attn_gate_b, L1_attn_proj_w, L1_attn_proj_b, L1_ffn_gate_w, L1_ffn_gate_bias, L1_ffn_Wg, L1_ffn_Wu, L1_ffn_Wd, L1_ffn_Ws_g, L1_ffn_Ws_u, L1_ffn_Ws_d, L2_attn_ln_w, L2_attn_ln_b, L2_attn_Wi, L2_attn_bi, L2_attn_Wf, L2_attn_bf, L2_attn_Wz, L2_attn_bz, L2_attn_Wo, L2_attn_bo, L2_attn_Wp, L2_attn_bp, L2_ffn_W_fc, L2_ffn_W_proj, L3_attn_wq, L3_attn_bq, L3_attn_wk, L3_attn_bk, L3_attn_wv, L3_attn_bv, L3_attn_wo, L3_attn_bo, L3_ffn_router_w, L3_ffn_router_b, L3_ffn_w1, L3_ffn_b1, L3_ffn_gate, L3_ffn_w2, L3_ffn_b2, L3_ffn_sw1, L3_ffn_sb1, L3_ffn_sgate, L3_ffn_sw2, L3_ffn_sb2, L3_ffn_shared_weight, L3_ffn_ln_g, L3_ffn_ln_b):

    def _L0_attn_ref(x, g1, b1, Wqkv_a, bqkv_a, Wp_a, bp_a, Wqkv_s, bqkv_s, Wo_s, bo_s, Wo, bo, gm, bm, W1, b1m, W2, b2m):
        import jax, jax.numpy as jnp
        import numpy as np
        B, L, D, H, W = (2, 512, 128, 16, 128)
        E = D // H

        def _ln(x, g, b):
            m = jnp.mean(x, axis=-1, keepdims=True)
            v = jnp.mean((x - m) ** 2, axis=-1, keepdims=True)
            return (x - m) / jnp.sqrt(v + 1e-05) * g + b

        def _swa(xn, Wqkv, bqkv, Wp, bp):
            b_, l_, d_ = xn.shape
            nb = l_ // W
            qkv = xn @ Wqkv + bqkv
            q, k, v = jnp.split(qkv, 3, axis=-1)

            def heads(t):
                return t.reshape(b_, l_, H, E).transpose(0, 2, 1, 3)
            q, k, v = (heads(q), heads(k), heads(v))

            def blk(t):
                return t.reshape(b_, H, nb, W, E)
            qb, kb, vb = (blk(q), blk(k), blk(v))
            kprev = jnp.pad(kb, ((0, 0), (0, 0), (1, 0), (0, 0), (0, 0)))[:, :, :nb]
            vprev = jnp.pad(vb, ((0, 0), (0, 0), (1, 0), (0, 0), (0, 0)))[:, :, :nb]
            kc = jnp.concatenate([kprev, kb], axis=3)
            vc = jnp.concatenate([vprev, vb], axis=3)
            scores = jnp.einsum('bhnre,bhnse->bhnrs', qb, kc) / np.float32(np.sqrt(E))
            r = jnp.arange(W)[:, None]
            s = jnp.arange(2 * W)[None, :]
            band = (s >= r + 1) & (s <= r + W)
            first = band & (s >= W)
            mask = jnp.concatenate([first[None], jnp.broadcast_to(band, (nb - 1, W, 2 * W))], axis=0)
            scores = jnp.where(mask[None, None], scores, jnp.float32(-1e+30))
            attn = jax.nn.softmax(scores, axis=-1)
            out = jnp.einsum('bhnrs,bhnse->bhnre', attn, vc)
            out = out.reshape(b_, H, l_, E).transpose(0, 2, 1, 3).reshape(b_, l_, d_)
            return out @ Wp + bp

        def _linattn(xn, Wqkv, bqkv, Wo, bo):
            b_, l_, d_ = xn.shape
            C = 128
            nc = l_ // C
            qkv = xn @ Wqkv + bqkv
            q, k, v = jnp.split(qkv, 3, axis=-1)
            q = q.reshape(b_, l_, H, E)
            k = k.reshape(b_, l_, H, E)
            v = v.reshape(b_, l_, H, E)
            q = jax.nn.elu(q * np.float32(E ** (-0.5))) + np.float32(1.0001)
            k = jax.nn.elu(k) + np.float32(1.0001)

            def chunks(t):
                return t.reshape(b_, nc, C, H, E).transpose(1, 0, 3, 2, 4)
            qc, kc, vc = (chunks(q), chunks(k), chunks(v))
            tril = jnp.tril(jnp.ones((C, C), jnp.float32))

            def step(carry, inp):
                S, z = carry
                qi, ki, vi = inp
                A = jnp.einsum('bhce,bhde->bhcd', qi, ki) * tril
                num = jnp.einsum('bhce,bhef->bhcf', qi, S) + jnp.einsum('bhcd,bhdf->bhcf', A, vi)
                den = jnp.einsum('bhce,bhe->bhc', qi, z) + A.sum(-1)
                o = num / (den[..., None] + 1e-06)
                S = S + jnp.einsum('bhce,bhcf->bhef', ki, vi)
                z = z + ki.sum(2)
                return ((S, z), o)
            S0 = jnp.zeros((b_, H, E, E), jnp.float32)
            z0 = jnp.zeros((b_, H, E), jnp.float32)
            _, out = jax.lax.scan(step, (S0, z0), (qc, kc, vc))
            out = out.transpose(1, 0, 3, 2, 4).reshape(b_, l_, d_)
            return out @ Wo + bo
        xn = _ln(x, g1, b1)
        attn_out = _swa(xn, Wqkv_a, bqkv_a, Wp_a, bp_a)
        ssm_out = _linattn(xn, Wqkv_s, bqkv_s, Wo_s, bo_s)
        mixed = (attn_out + ssm_out) @ Wo + bo
        x1 = x + mixed
        h = _ln(x1, gm, bm)
        mlp = jax.nn.gelu(h @ W1 + b1m, approximate=False) @ W2 + b2m
        return x1 + mlp

    def _L0_ffn_ref(x, gate_w, experts_gate_up, experts_down, shared_gate_w, shared_up_w, shared_down_w, shared_expert_gate_w):
        import jax, jax.numpy as jnp
        import numpy as np
        HIDDEN_SIZE = 128
        NUM_EXPERTS = 8
        MOE_INTERMEDIATE_SIZE = 176
        NUM_EXPERTS_PER_TOK = 2
        SHARED_EXPERT_INTERMEDIATE_SIZE = 352
        B, T = (2, 128)
        W_SCALE = 0.02
        Bx, Tx, H = x.shape
        E = gate_w.shape[0]
        I = experts_down.shape[2]
        x_flat = x.reshape(Bx * Tx, H)
        logits = x_flat @ gate_w.T
        scores = jax.nn.softmax(logits, axis=-1)
        _, topk_ids = jax.lax.top_k(scores, NUM_EXPERTS_PER_TOK)
        in_topk = jax.nn.one_hot(topk_ids, E, dtype=x.dtype).sum(axis=1)
        w = scores * in_topk
        gu = jnp.einsum('nh,eih->nei', x_flat, experts_gate_up)
        g, u = (gu[..., :I], gu[..., I:])
        h = jax.nn.silu(g) * u
        expert_out = jnp.einsum('nei,ehi->neh', h, experts_down)
        out = jnp.einsum('neh,ne->nh', expert_out, w)
        shared = jax.nn.silu(x_flat @ shared_gate_w.T) * (x_flat @ shared_up_w.T) @ shared_down_w.T
        shared_weight = jax.nn.sigmoid(x_flat @ shared_expert_gate_w.T)
        out = out + shared_weight * shared
        return out.reshape(Bx, Tx, H)

    def _L1_attn_ref(x, ln_g, ln_b, qkv_w, qkv_b, gate_w, gate_b, proj_w, proj_b):
        import jax, jax.numpy as jnp
        import numpy as np
        D_MODEL = 128
        N_HEADS = 16
        D_HEAD = D_MODEL // N_HEADS
        EPS_LN = 1e-05
        EPS_GATE = 1e-05
        EPS_DEN = 1e-05

        def _linear(x, w, b):
            return jnp.einsum('btd,od->bto', x, w) + b
        B, T, D = x.shape
        H, Dh = (N_HEADS, D_HEAD)
        mu = jnp.mean(x, axis=-1, keepdims=True)
        var = jnp.mean((x - mu) ** 2, axis=-1, keepdims=True)
        x_norm = (x - mu) / jnp.sqrt(var + EPS_LN) * ln_g + ln_b
        qkv = _linear(x_norm, qkv_w, qkv_b)
        q, k, v = jnp.split(qkv, 3, axis=-1)
        gate_sig = jax.nn.sigmoid(_linear(x, gate_w, gate_b))
        gate_norm = gate_sig / (jnp.mean(gate_sig, axis=-1, keepdims=True) + EPS_GATE)
        q = q * gate_norm
        k = k * gate_norm

        def heads(t):
            return t.reshape(B, T, H, Dh).transpose(0, 2, 1, 3)
        q, k, v = (heads(q).astype(jnp.float32), heads(k).astype(jnp.float32), heads(v).astype(jnp.float32))
        q = jax.nn.elu(q) + 1.0
        k = jax.nn.elu(k) + 1.0
        kv = jnp.einsum('bhtd,bhtm->bhtdm', k, v)
        kv_cum = jnp.cumsum(kv, axis=2)
        out_num = jnp.einsum('bhtd,bhtdm->bhtm', q, kv_cum)
        k_cum = jnp.cumsum(k, axis=2)
        out_den = jnp.einsum('bhtd,bhtd->bht', q, k_cum)[..., None] + EPS_DEN
        out = out_num / out_den
        out = out.astype(x_norm.dtype).transpose(0, 2, 1, 3).reshape(B, T, D)
        return _linear(out, proj_w, proj_b)

    def _L1_ffn_ref(hidden_states, gate_w, gate_bias, Wg, Wu, Wd, Ws_g, Ws_u, Ws_d):
        import jax, jax.numpy as jnp
        import numpy as np
        E = 16
        K = 4
        NG = 4
        TG = 2
        SCALE = 2.5
        NORM_TOPK = True
        H = 128
        I = 64
        SH_I = I * 2
        B, S = (2, 256)
        x = hidden_states
        b, s, h = x.shape
        n = b * s
        xf = x.reshape(n, h)
        logits = xf @ gate_w.T
        scores = jax.nn.sigmoid(logits)
        sfc = scores + gate_bias
        epg = E // NG
        grp = sfc.reshape(n, NG, epg)
        g_scores = jax.lax.top_k(grp, 2)[0].sum(-1)
        _, gidx = jax.lax.top_k(g_scores, TG)
        gmask = jax.nn.one_hot(gidx, NG, dtype=sfc.dtype).sum(1)
        emask = jnp.repeat(gmask, epg, axis=1)
        masked = jnp.where(emask > 0, sfc, -jnp.inf)
        _, topk_idx = jax.lax.top_k(masked, K)
        topk_w = jnp.take_along_axis(scores, topk_idx, axis=1)
        if K > 1 and NORM_TOPK:
            topk_w = topk_w / (topk_w.sum(-1, keepdims=True) + 1e-20)
        topk_w = topk_w * SCALE
        cw = (jax.nn.one_hot(topk_idx, E, dtype=topk_w.dtype) * topk_w[..., None]).sum(1)
        hg = jnp.einsum('nh,eih->nei', xf, Wg)
        hu = jnp.einsum('nh,eih->nei', xf, Wu)
        act = jax.nn.silu(hg) * hu
        y = jnp.einsum('nei,ne,ehi->nh', act, cw, Wd)
        shared = jax.nn.silu(xf @ Ws_g.T) * (xf @ Ws_u.T) @ Ws_d.T
        y = y + shared
        return (x + y.reshape(b, s, h)).astype(hidden_states.dtype)

    def _L2_attn_ref(x, ln_w, ln_b, Wi, bi, Wf, bf, Wz, bz, Wo, bo, Wp, bp):
        import jax, jax.numpy as jnp
        import numpy as np
        B, S, D, N = (8, 512, 128, 64)
        EPS = 1e-05
        mu = jnp.mean(x, axis=-1, keepdims=True)
        var = jnp.mean(jnp.square(x - mu), axis=-1, keepdims=True)
        xn = (x - mu) * jax.lax.rsqrt(var + EPS) * ln_w + ln_b
        log_i = jnp.clip(jnp.einsum('bsd,nd->bsn', xn, Wi) + bi, -20.0, 20.0)
        log_f = jnp.clip(jnp.einsum('bsd,nd->bsn', xn, Wf) + bf, -20.0, 20.0)
        z = jnp.tanh(jnp.einsum('bsd,nd->bsn', xn, Wz) + bz)
        o = jax.nn.sigmoid(jnp.einsum('bsd,nd->bsn', xn, Wo) + bo)

        def step(carry, inp):
            c, m = carry
            li, lf, zt, ot = inp
            m_new = jnp.maximum(m + lf, li)
            i_s = jnp.exp(li - m_new)
            f_s = jnp.exp(m + lf - m_new)
            c = f_s * c + i_s * zt
            h = ot * jnp.tanh(c)
            return ((c, m_new), h)
        c0 = jnp.zeros((x.shape[0], log_i.shape[-1]), x.dtype)
        m0 = jnp.zeros_like(c0)
        tm = lambda a: jnp.swapaxes(a, 0, 1)
        _, h_seq = jax.lax.scan(step, (c0, m0), (tm(log_i), tm(log_f), tm(z), tm(o)))
        h_seq = jnp.swapaxes(h_seq, 0, 1)
        return jnp.einsum('bsn,dn->bsd', h_seq, Wp) + bp

    def _L2_ffn_ref(x, W_fc, W_proj):
        import jax, jax.numpy as jnp
        import numpy as np
        import math
        BETA = 0.9
        THRESHOLD = 1.0
        NUM_STEPS = 5
        ALPHA = 2.0

        @jax.custom_vjp
        def spike_fn(u):
            return (u > 0).astype(u.dtype)

        def _spike_fwd(u):
            return (spike_fn(u), u)

        def _spike_bwd(u, g):
            s = jnp.pi / 2.0 * ALPHA * u
            return (g * (ALPHA / 2.0) / (1.0 + s * s),)
        spike_fn.defvjp(_spike_fwd, _spike_bwd)
        h = jnp.square(jax.nn.relu(jnp.einsum('bsd,fd->bsf', x, W_fc)))
        y = jnp.einsum('bsf,df->bsd', h, W_proj)

        def step(mem, _):
            reset = jax.lax.stop_gradient(spike_fn(mem - THRESHOLD))
            mem_new = BETA * mem + y - reset * THRESHOLD
            spk = spike_fn(mem_new - THRESHOLD)
            return (mem_new, spk)
        mem0 = jnp.zeros_like(y)
        _, spks = jax.lax.scan(step, mem0, None, length=NUM_STEPS)
        return jnp.sum(spks, axis=0) / NUM_STEPS

    def _L3_attn_ref(inputs, wq, bq, wk, bk, wv, bv, wo, bo):
        import jax, jax.numpy as jnp
        import numpy as np
        D_MODEL = 128
        NUM_HEADS = 16
        DEPTH = D_MODEL // NUM_HEADS

        def _split_heads(x):
            B, S, _ = x.shape
            return x.reshape(B, S, NUM_HEADS, DEPTH).transpose(0, 2, 1, 3)
        B, S, _ = inputs.shape
        q = _split_heads(inputs @ wq + bq)
        k = _split_heads(inputs @ wk + bk)
        v = _split_heads(inputs @ wv + bv)
        scale = 1.0 / jnp.sqrt(jnp.float32(DEPTH))
        logits = jnp.einsum('bhqd,bhkd->bhqk', q, k) * scale
        attn = jax.nn.softmax(logits, axis=-1)
        out = jnp.einsum('bhqk,bhkd->bhqd', attn, v)
        out = out.transpose(0, 2, 1, 3).reshape(B, S, D_MODEL)
        return out @ wo + bo

    def _L3_ffn_ref(hidden_states, router_w, router_b, w1, b1, gate, w2, b2, sw1, sb1, sgate, sw2, sb2, shared_weight, ln_g, ln_b):
        import jax, jax.numpy as jnp
        import numpy as np
        E = 8
        K = 2
        LN_EPS = 1e-05

        def _expert_ffn(x, w1, b1, gate, w2, b2):
            h = jax.nn.gelu((x @ w1 + b1) * gate, approximate=False)
            return h @ w2 + b2
        x = hidden_states
        logits = jnp.einsum('bsd,de->bse', x, router_w) + router_b
        probs = jax.nn.softmax(logits, axis=-1)
        topk_p, topk_i = jax.lax.top_k(probs, K)
        topk_p = topk_p / jnp.sum(topk_p, axis=-1, keepdims=True)
        combine = jnp.sum(jax.nn.one_hot(topk_i, E, dtype=x.dtype) * topk_p[..., None], axis=-2)
        moe = jnp.zeros_like(x)
        for e in range(E):
            moe = moe + combine[..., e:e + 1] * _expert_ffn(x, w1[e], b1[e], gate[e], w2[e], b2[e])
        shared = _expert_ffn(x, sw1, sb1, sgate, sw2, sb2) * jax.nn.sigmoid(shared_weight)
        y = moe + shared
        mu = jnp.mean(y, axis=-1, keepdims=True)
        var = jnp.var(y, axis=-1, keepdims=True)
        return (y - mu) * jax.lax.rsqrt(var + LN_EPS) * ln_g + ln_b
    x = L0_attn_x
    x = x + _L0_attn_ref(_layernorm(x, axis=-1), L0_attn_g1, L0_attn_b1, L0_attn_Wqkv_a, L0_attn_bqkv_a, L0_attn_Wp_a, L0_attn_bp_a, L0_attn_Wqkv_s, L0_attn_bqkv_s, L0_attn_Wo_s, L0_attn_bo_s, L0_attn_Wo, L0_attn_bo, L0_attn_gm, L0_attn_bm, L0_attn_W1, L0_attn_b1m, L0_attn_W2, L0_attn_b2m)
    x = x + _L0_ffn_ref(_layernorm(x, axis=-1), L0_ffn_gate_w, L0_ffn_experts_gate_up, L0_ffn_experts_down, L0_ffn_shared_gate_w, L0_ffn_shared_up_w, L0_ffn_shared_down_w, L0_ffn_shared_expert_gate_w)
    x = x + _L1_attn_ref(_layernorm(x, axis=-1), L1_attn_ln_g, L1_attn_ln_b, L1_attn_qkv_w, L1_attn_qkv_b, L1_attn_gate_w, L1_attn_gate_b, L1_attn_proj_w, L1_attn_proj_b)
    x = x + _L1_ffn_ref(_layernorm(x, axis=-1), L1_ffn_gate_w, L1_ffn_gate_bias, L1_ffn_Wg, L1_ffn_Wu, L1_ffn_Wd, L1_ffn_Ws_g, L1_ffn_Ws_u, L1_ffn_Ws_d)
    x = x + _L2_attn_ref(_layernorm(x, axis=-1), L2_attn_ln_w, L2_attn_ln_b, L2_attn_Wi, L2_attn_bi, L2_attn_Wf, L2_attn_bf, L2_attn_Wz, L2_attn_bz, L2_attn_Wo, L2_attn_bo, L2_attn_Wp, L2_attn_bp)
    x = x + _L2_ffn_ref(_layernorm(x, axis=-1), L2_ffn_W_fc, L2_ffn_W_proj)
    x = x + _L3_attn_ref(_layernorm(x, axis=-1), L3_attn_wq, L3_attn_bq, L3_attn_wk, L3_attn_bk, L3_attn_wv, L3_attn_bv, L3_attn_wo, L3_attn_bo)
    x = x + _L3_ffn_ref(_layernorm(x, axis=-1), L3_ffn_router_w, L3_ffn_router_b, L3_ffn_w1, L3_ffn_b1, L3_ffn_gate, L3_ffn_w2, L3_ffn_b2, L3_ffn_sw1, L3_ffn_sb1, L3_ffn_sgate, L3_ffn_sw2, L3_ffn_sb2, L3_ffn_shared_weight, L3_ffn_ln_g, L3_ffn_ln_b)
    return x

_drawn_inputs = setup_inputs


def setup_inputs(seed=0):
    import zlib

    import numpy as np

    out = dict(_drawn_inputs(seed))
    spreads = {'L0_attn_g1': (1.0, 0.6),
     'L0_attn_b1': (0.0, 0.336),
     'L0_attn_bqkv_a': (0.0, 0.293),
     'L0_attn_bp_a': (0.0, 0.1),
     'L0_attn_bqkv_s': (0.0, 0.292),
     'L0_attn_bo_s': (0.0, 0.1),
     'L0_attn_bo': (0.0, 0.1),
     'L0_attn_gm': (1.0, 0.2),
     'L0_attn_bm': (0.0, 0.281),
     'L0_attn_b1m': (0.0, 0.1),
     'L0_attn_b2m': (0.0, 0.1),
     'L1_attn_ln_g': (1.0, 0.2),
     'L1_attn_ln_b': (0.0, 0.1),
     'L1_attn_qkv_b': (0.0, 0.1),
     'L1_attn_gate_b': (0.0, 1.168),
     'L1_attn_proj_b': (0.0, 0.1),
     'L1_ffn_gate_bias': (0.0, 0.1),
     'L2_attn_ln_w': (1.0, 0.2),
     'L2_attn_ln_b': (0.0, 0.1),
     'L2_attn_bi': (0.0, 2.0),
     'L2_attn_bf': (0.0, 0.1),
     'L2_attn_bz': (0.0, 0.1),
     'L2_attn_bo': (0.0, 0.455),
     'L2_attn_bp': (0.0, 0.1),
     'L3_attn_bq': (0.0, 0.677),
     'L3_attn_bk': (0.0, 2.0),
     'L3_attn_bv': (0.0, 0.1),
     'L3_attn_bo': (0.0, 0.1),
     'L3_ffn_router_b': (0.0, 0.1),
     'L3_ffn_b1': (0.0, 0.1),
     'L3_ffn_gate': (1.0, 0.564),
     'L3_ffn_b2': (0.0, 0.1),
     'L3_ffn_sb1': (0.0, 0.299),
     'L3_ffn_sgate': (1.0, 0.6),
     'L3_ffn_sb2': (0.0, 0.1),
     'L3_ffn_ln_g': (1.0, 0.2),
     'L3_ffn_ln_b': (0.0, 0.282)}
    factors = {'L0_attn_Wqkv_a': 3.494,
     'L0_attn_Wqkv_s': 3.639,
     'L0_ffn_gate_w': 4.506,
     'L0_ffn_experts_gate_up': 4.727,
     'L0_ffn_experts_down': 5.001,
     'L0_ffn_shared_gate_w': 3.458,
     'L0_ffn_shared_up_w': 3.521,
     'L0_ffn_shared_down_w': 3.667,
     'L0_ffn_shared_expert_gate_w': 6.587}
    for name, (base, spread) in spreads.items():
        noise = np.random.default_rng([zlib.crc32(name.encode()), seed]).standard_normal(out[name].shape)
        drawn = base * np.exp(spread * noise) if base else spread * noise
        out[name] = jnp.asarray(drawn.astype(out[name].dtype))
    for name, factor in factors.items():
        out[name] = (out[name] * factor).astype(out[name].dtype)
    return out
```

```python
from contextlib import ExitStack

import numpy as np
import concourse.bass as bass
from concourse import mybir

F32 = mybir.dt.float32
BF16 = mybir.dt.bfloat16
ALU = mybir.AluOpType
ACT = mybir.ActivationFunctionType
AX = mybir.AxisListType

P = 128
B, L, D, H = 2, 512, 128, 16
E = D // H
NT = B * L // P
TPB = L // P
TOK = B * L
PASSES = 2
HALF = 512
VW = 32
PICK = 4 * E + 4
GROUPS = H // 4
SCALE = float(E) ** -0.5
NEG = -1e30
EPS = 1e-5

Q_PARTS = (0, 0, 1, 1, 0, 2)
K_PARTS = (0, 1, 0, 1, 2, 0)
STACK = 96
M_ROW = 96

MOE = {"L0": dict(blocks=14, experts=8, table=9, topk=2, glu=True),
       "L1": dict(blocks=9, experts=16, table=17, topk=4, glu=True),
       "L3": dict(blocks=34, experts=8, table=9, topk=2, glu=False)}

HEAD_ORDER = np.array([h * E + e for e in range(E) for h in range(H)])


class Wall:

    def __init__(self):
        self.at, self.parts, self.n = {}, [], 0

    def put(self, name, array):
        array = np.asarray(array)
        if array.ndim == 1:
            array = array[:, None]
        self.at[name] = (self.n, array.shape[1], array.shape[0])
        self.parts.append(array)
        self.n += array.shape[1]

    def array(self, rows, dtype):
        out = np.zeros((rows, self.n), dtype)
        for (at, n, r), a in zip(self.at.values(), self.parts):
            out[:r, at:at + n] = a
        return out


def columns(n_rows, x):
    return np.asarray(x).reshape(-1, n_rows).T


def bf16_bits(constant):
    return (np.ascontiguousarray(constant).view(np.uint32) >> 16).astype(np.uint16)


def constants():
    f = Wall()
    f.put("ident", np.eye(P, dtype=np.float32))
    r, c = np.arange(P)[:, None], np.arange(P)[None, :]
    f.put("causal", (r <= c).astype(np.float32))
    block = np.zeros((P, H, VW), np.float32)
    for row in range(P):
        block[row, row % H, :] = 1.0
    f.put("block", block.reshape(P, H * VW))
    pick = np.zeros((P, PICK), np.float32)
    for j in range(4):
        for e in range(E):
            pick[32 * j + e, j * E + e] = 1.0
        pick[32 * j + E, 4 * E + j] = 1.0
    f.put("pick", pick)
    f.put("ones", np.full((P, 1), 1.0 / P, np.float32))
    for n in (4, 8, 16):
        below = (np.arange(n)[None, :] < np.arange(n)[:, None]).astype(np.float32)
        f.put(f"before{n}", np.broadcast_to(below.reshape(1, n * n), (P, n * n)))
    b = Wall()
    b.put("ident", np.eye(P))
    q, k = r, c
    previous = np.where(k > q, 0.0, NEG)
    current = np.where(k <= q, 0.0, NEG)
    nothing = np.full((P, P), NEG)
    b.put("mask_q", np.tile(np.concatenate([previous, current], 1), 2))
    b.put("mask_q0", np.tile(np.concatenate([nothing, current], 1), 2))
    b.put("mask_k", np.tile(np.concatenate([previous.T, current.T], 1), 2))
    b.put("mask_k0", np.tile(np.concatenate([nothing, current.T], 1), 2))
    return f.array(P, np.float32), f.at, bf16_bits(b.array(P, np.float32)), b.at


def expanders():
    out = {}
    for name, m in MOE.items():
        t = m["table"]
        if name == "L0":
            owner = np.concatenate([np.repeat(np.arange(8), 176), np.full(352, 8), np.full(32, -1)])
        elif name == "L1":
            owner = np.concatenate([np.repeat(np.arange(16), 64), np.full(128, 16)])
        else:
            owner = np.concatenate([np.repeat(np.arange(8), 512), np.full(256, 8)])
        hot = (np.arange(t)[:, None] == owner[None, :])
        hot = np.concatenate([hot] * 3, 0).reshape(3 * t, m["blocks"], P)
        out[name] = bf16_bits(hot.transpose(1, 0, 2).reshape(m["blocks"] * 3 * t, P).astype(np.float32))
    return out


def lay_out(x):
    g = {k: np.asarray(v) for k, v in x.items()}
    w = {n: Wall() for n in ("L0", "L1", "L2", "L3")}
    rows = Wall()
    ho = HEAD_ORDER

    def qkv(wall, tag, wm, bv):
        wall.put(tag + "_wq", wm[:, 0:D][:, ho])
        wall.put(tag + "_wk", wm[:, D:2 * D][:, ho])
        wall.put(tag + "_wv", wm[:, 2 * D:])
        wall.put(tag + "_bq", bv[0:D][ho])
        wall.put(tag + "_bk", bv[D:2 * D][ho])
        rows.put(tag + "_bv", bv[2 * D:][None])

    a = w["L0"]
    qkv(a, "a", g["L0_attn_Wqkv_a"], g["L0_attn_bqkv_a"])
    qkv(a, "s", g["L0_attn_Wqkv_s"], g["L0_attn_bqkv_s"])
    for n in ("g1", "b1", "gm", "bm", "bp_a", "bo_s"):
        a.put(n, g["L0_attn_" + n])
    a.put("b1m", columns(P, g["L0_attn_b1m"]))
    a.put("Wp_a", g["L0_attn_Wp_a"])
    a.put("Wo_s", g["L0_attn_Wo_s"])
    a.put("Wo", g["L0_attn_Wo"])
    a.put("W1", g["L0_attn_W1"])
    a.put("W2", g["L0_attn_W2"].reshape(4, P, D).transpose(1, 0, 2).reshape(P, 4 * D))
    a.put("router0", np.concatenate([g["L0_ffn_gate_w"], g["L0_ffn_shared_expert_gate_w"]], 0).T)
    rows.put("bo", g["L0_attn_bo"][None])
    rows.put("b2m", g["L0_attn_b2m"][None])

    a = w["L1"]
    qkv(a, "l", g["L1_attn_qkv_w"].T, g["L1_attn_qkv_b"])
    a.put("gate_w", g["L1_attn_gate_w"].T[:, ho])
    a.put("gate_b", g["L1_attn_gate_b"][ho])
    a.put("ln_g", g["L1_attn_ln_g"])
    a.put("ln_b", g["L1_attn_ln_b"])
    a.put("proj_w", g["L1_attn_proj_w"].T)
    a.put("router1", g["L1_ffn_gate_w"].T)
    a.put("router1_b", np.broadcast_to(g["L1_ffn_gate_bias"][None], (P, 16)))
    rows.put("proj_b", g["L1_attn_proj_b"][None])

    a = w["L2"]
    for n in ("Wi", "Wf", "Wz", "Wo"):
        a.put(n, g["L2_attn_" + n].T)
    for n in ("bi", "bf", "bz", "bo"):
        a.put(n, np.tile(g["L2_attn_" + n], 2))
    a.put("Wp", np.tile(g["L2_attn_Wp"].T, (2, 1)))
    a.put("ln_w", g["L2_attn_ln_w"])
    a.put("ln_b", g["L2_attn_ln_b"])
    a.put("W_fc", g["L2_ffn_W_fc"].T)
    a.put("W_proj", g["L2_ffn_W_proj"].T.reshape(4, P, D).transpose(1, 0, 2).reshape(P, 4 * D))
    rows.put("bp", g["L2_attn_bp"][None])

    a = w["L3"]
    a.put("f_wq", g["L3_attn_wq"][:, ho])
    a.put("f_wk", g["L3_attn_wk"][:, ho])
    a.put("f_wv", g["L3_attn_wv"])
    a.put("f_bq", g["L3_attn_bq"][ho])
    a.put("f_bk", g["L3_attn_bk"][ho])
    a.put("wo", g["L3_attn_wo"])
    a.put("router3", g["L3_ffn_router_w"])
    a.put("router3_b", np.broadcast_to(g["L3_ffn_router_b"][None], (P, 8)))
    a.put("gate", np.concatenate([columns(P, g["L3_ffn_gate"].reshape(-1)), columns(P, g["L3_ffn_sgate"])], 1))
    a.put("b1", np.concatenate([columns(P, g["L3_ffn_b1"].reshape(-1)), columns(P, g["L3_ffn_sb1"])], 1))
    a.put("b2", np.concatenate([g["L3_ffn_b2"], g["L3_ffn_sb2"][None]], 0))
    a.put("shared_w", np.broadcast_to(g["L3_ffn_shared_weight"].reshape(1, 1), (P, 1)))
    a.put("ln_g3", np.broadcast_to(g["L3_ffn_ln_g"][None], (P, D)))
    a.put("ln_b3", np.broadcast_to(g["L3_ffn_ln_b"][None], (P, D)))
    rows.put("f_bv", g["L3_attn_bv"][None])
    rows.put("bo3", g["L3_attn_bo"][None])
    rows.put("ones", np.ones((1, P), np.float32))

    def blocks_in(m):
        return m.reshape(P, -1, P).transpose(1, 0, 2)

    def padded(m, n):
        out = np.zeros((m.shape[0], n), m.dtype)
        out[:, :m.shape[1]] = m
        return out

    streams = {}
    n0 = MOE["L0"]["blocks"] * P
    gu = g["L0_ffn_experts_gate_up"]
    gate = padded(np.concatenate([gu[:, :176].reshape(-1, D), g["L0_ffn_shared_gate_w"]], 0).T, n0)
    up = padded(np.concatenate([gu[:, 176:].reshape(-1, D), g["L0_ffn_shared_up_w"]], 0).T, n0)
    down = padded(np.concatenate([g["L0_ffn_experts_down"].transpose(1, 0, 2).reshape(D, -1),
                                  g["L0_ffn_shared_down_w"]], 1), n0)
    streams["L0"] = (np.concatenate([blocks_in(gate), blocks_in(up)], 2).reshape(-1, 2 * P), down.T)
    gate = np.concatenate([g["L1_ffn_Wg"].reshape(-1, D), g["L1_ffn_Ws_g"]], 0).T
    up = np.concatenate([g["L1_ffn_Wu"].reshape(-1, D), g["L1_ffn_Ws_u"]], 0).T
    down = np.concatenate([g["L1_ffn_Wd"].transpose(1, 0, 2).reshape(D, -1), g["L1_ffn_Ws_d"]], 1)
    streams["L1"] = (np.concatenate([blocks_in(gate), blocks_in(up)], 2).reshape(-1, 2 * P), down.T)
    w1 = np.concatenate([g["L3_ffn_w1"].transpose(1, 0, 2).reshape(D, -1), g["L3_ffn_sw1"]], 1)
    w2 = np.concatenate([g["L3_ffn_w2"].reshape(-1, D), g["L3_ffn_sw2"]], 0)
    streams["L3"] = (blocks_in(w1).reshape(-1, P), w2)

    arrays = {"x": g["L0_attn_x"].reshape(PASSES, NT, P, D).transpose(0, 2, 1, 3).reshape(PASSES * P, NT * D)}
    at = {}
    for n, wall in w.items():
        arrays["w" + n] = wall.array(P, np.float32)
        at[n] = wall.at
    arrays["rows"] = rows.array(1, np.float32)
    at["rows"] = rows.at
    arrays["cf"], at["cf"], arrays["cb"], at["cb"] = constants()
    arrays["ones_rows"] = bf16_bits(np.ones((3, H * TOK), np.float32))
    for n, hot in expanders().items():
        arrays["in" + n], arrays["down" + n] = streams[n]
        arrays["hot" + n] = hot
    return {k: np.ascontiguousarray(v) for k, v in arrays.items()}, at


def unit_loop(eng, n, body):
    for u in range(4):
        body(u, u)
    last = (n - 1) // 4
    with eng.Fori(1, last) as i:
        for q in range(4):
            body(i * 4 + q, q)
    for u in range(4 * last, n):
        body(u, u % 4)


def program(nc, T, at, shapes, stop=99):
    with ExitStack() as ctx, ExitStack() as ctx_loop:
        def sb(name, shape, dt=F32):
            return ctx.enter_context(nc.sbuf_tensor(name, shape, dt))

        sems = {}

        def S(name):
            if name not in sems:
                sems[name] = phase["sems"].enter_context(nc.semaphore(name.replace(".", "_")))
            return sems[name]

        ONCE = {n: ctx.enter_context(nc.semaphore(n)) for n in
                ("rows_in", "cf_in", "cb_in", "ones_in", "wall_L0", "wall_L1", "wall_L2", "wall_L3",
                 "zero_in", "v_ready", "half_ready", "stack_zero", "q_zero")}

        PS = ctx.enter_context(nc.psum_tensor("PS", [P, 8, 512], F32))
        X = sb("X", [P, NT, D])
        A = sb("A", [P, NT, D])
        A2 = sb("A2", [P, NT, D])
        AT = sb("AT", [P, TOK])
        NTT = sb("NTT", [P, TOK])
        T0 = sb("T0", [P, TOK])
        T1 = sb("T1", [P, TOK])
        T2 = sb("T2", [P, TOK])
        T3 = sb("T3", [P, TOK])
        OT = sb("OT", [P, TOK])
        QS = sb("QS", [P, H, TOK], BF16)
        KS = sb("KS", [P, H, TOK], BF16)
        V = sb("V", [P, NT, H, VW])
        BIG = sb("BIG", [P, GROUPS, TOK])
        PR = sb("PR", [P, 8, 512])
        SM = PR[:, 4:6, :]
        WALL = {n: sb("wall_" + n, [P, shapes["w" + n][1]]) for n in ("L0", "L1", "L2", "L3")}
        CF = sb("CF", [P, shapes["cf"][1]])
        CB = sb("CB", [P, shapes["cb"][1]], BF16)
        ROWS = sb("ROWS", [1, shapes["rows"][1]])
        GU = sb("GU", [P, 2, 2 * P])
        DN = sb("DN", [P, 2, P])
        HOT = sb("HOT", [51, 2, P], BF16)
        CT = sb("CT", [51, TOK], BF16)
        C32 = sb("C32", [17, TOK])
        GM = sb("GM", [P, NT])
        DEN = sb("DEN", [P, 2, 64])
        stats = sb("stats", [P, NT, 6])
        moments = sb("moments", [P, NT, 2])
        small = sb("small", [P, 8, NT])
        MX = sb("MX", [P, 2, 16])
        MXR = sb("MXR", [P, 2, 16])
        MP = sb("MP", [P, 2, 4, 3, 4], BF16)
        MR = sb("MR", [48, 512], BF16)
        CW = sb("CW", [P, NT, 17])
        CWR = sb("CWR", [P, NT, 17])
        CP = sb("CP", [P, NT, 3, 17], BF16)
        b1g = sb("b1g", [P, 34, 2])
        GB = sb("GB", [P, 2, 2])
        zero = sb("zero", [1, 512], BF16)
        vec = sb("vec", [P, 4])

        def parts_of(which, i):
            n = 3 * which + i
            return BIG[:, n // 2, :].bitcast(BF16)[:, (n % 2) * TOK:(n % 2 + 1) * TOK]

        def w(layer, name, a=0, b=None):
            o, n, r = at[layer][name]
            return WALL[layer][0:r, o + a:o + (n if b is None else b)]

        def cf(name, a=0, b=None):
            o, n, r = at["cf"][name]
            return CF[:, o + a:o + (n if b is None else b)]

        def cb(name):
            o, n, r = at["cb"][name]
            return CB[:, o:o + n]

        def row(name):
            o, n, r = at["rows"][name]
            return ROWS[0:1, o:o + n]

        def row4(name):
            return row(name).unsqueeze(1).to_broadcast([1, 4, P])

        def half(h):
            return slice(HALF * h, HALF * (h + 1))

        def tile(t):
            return slice(P * t, P * (t + 1))

        def bank(i, n=1):
            return PS[:, i, :] if n == 1 else PS[:, i:i + n, :].rearrange("p a b -> p (a b)")

        def tok(buf):
            return buf[:, :].rearrange("p (t d) -> p t d", t=NT)

        def flat(buf):
            return buf[:, :, :].rearrange("p t d -> p (t d)")

        with nc.Block() as once:
            @once.sync
            def _(sp):
                sp.dma_start(WALL["L0"][:, :], T["wL0"]).then_inc(ONCE["wall_L0"], 16)
                sp.dma_start(ROWS[:, :], T["rows"]).then_inc(ONCE["rows_in"], 16)
                sp.dma_start(CF[:, :], T["cf"]).then_inc(ONCE["cf_in"], 16)
                sp.dma_start(CB[:, :], T["cb"]).then_inc(ONCE["cb_in"], 16)
                for n in ("L1", "L2", "L3"):
                    sp.dma_start(WALL[n][:, :], T["w" + n]).then_inc(ONCE["wall_" + n], 16)
                sp.wait_ge(ONCE["stack_zero"], 1)
                sp.dma_start(KS[M_ROW:M_ROW + 3, :, :].rearrange("p h t -> p (h t)"), T["ones_rows"]
                             ).then_inc(ONCE["ones_in"], 16)

            @once.vector
            def _(v):
                v.memset(QS[:, :, :].rearrange("p h t -> p (h t)").bitcast(F32), 0.0).then_inc(ONCE["q_zero"], 1)

            @once.gpsimd
            def _(g):
                g.memset(KS[:, :, :].rearrange("p h t -> p (h t)").bitcast(F32), 0.0).then_inc(ONCE["stack_zero"], 1)
                g.memset(small[:, 7, :], -0.5).then_inc(ONCE["half_ready"], 1)
                g.memset(zero[:, :], 0.0).then_inc(ONCE["zero_in"], 1)
                g.memset(V[:, :, :, :], 0.0).then_inc(ONCE["v_ready"], 1)
                g.wait_ge(ONCE["v_ready"], 1)
                g.memset(V[:, :, :, E], 1.0).then_inc(ONCE["v_ready"], 1)

        NORMS = {
            "n0": (X, True, [(A2, NTT, (w("L0", "g1"), w("L0", "b1")))]),
            "n0m": (tok(T0), False, [(tok(T1), T2, (w("L0", "gm"), w("L0", "bm")))]),
            "n0f": (X, False, [(A, AT, None)]),
            "n1": (X, True, [(A, AT, None), (A2, NTT, (w("L1", "ln_g"), w("L1", "ln_b")))]),
            "n1f": (X, False, [(A, AT, None)]),
            "n2": (X, True, [(A2, NTT, (w("L2", "ln_w"), w("L2", "ln_b")))]),
            "n2f": (X, False, [(A, AT, None)]),
            "n3": (X, False, [(A, NTT, None)]),
            "n3f": (X, False, [(A, AT, None)]),
        }

        NORM_AT = {k: i if i < 5 else i - 5 for i, k in enumerate(NORMS)}

        def vector_norm(v, k):
            src, second, turns = NORMS[k]
            for t in range(NT):
                v.bn_stats(stats[:, t, :], src[:, t, :]).then_inc(S("norm_stats"), 1)
            v.wait_ge(S("norm_stats"), NT * (NORM_AT[k] + 1))
            for t in range(NT):
                v.bn_aggr(moments[:, t, :], stats[:, t, :]).then_inc(S("norm_moments"), 1)
            v.wait_ge(S("norm_rstd"), NORM_AT[k] + 1)
            if not second or k == "n0" or len(turns) == 2:
                a = tok(T1) if k == "n0m" else A
                for t in range(NT):
                    v.tensor_scalar(a[:, t, :], src[:, t, :], moments[:, t, 0:1], small[:, 1, t:t + 1],
                                    ALU.subtract, ALU.mult).then_inc(S(k + "_first"), 1)
            if second:
                for t in range(NT):
                    v.tensor_scalar(A2[:, t, :], src[:, t, :], moments[:, t, 0:1], small[:, 5, t:t + 1],
                                    ALU.subtract, ALU.mult).then_inc(S(k + "_second"), 1)

        def gpsimd_norm(g, k, chain):
            n = NORM_AT[k] + 1
            g.wait_ge(S("norm_moments"), NT * n)
            var = moments[:, :, 1]
            first = not NORMS[k][1] or k != "n2"
            if first:
                chain(g.tensor_scalar(small[:, 0, :], var, EPS, None, ALU.add))
            if NORMS[k][1]:
                chain(g.tensor_scalar(small[:, 4, :], var, 1.0 + EPS, EPS * EPS, ALU.mult, ALU.add))
            if first:
                last = g.tensor_tensor(small[:, 1, :], small[:, 0, :], small[:, 7, :], ALU.pow)
            if NORMS[k][1]:
                last = g.tensor_tensor(small[:, 5, :], small[:, 4, :], small[:, 7, :], ALU.pow)
            last.then_inc(S("norm_rstd"), 1)

        def tensor_norm(pe, k):
            for s, (src, _, affine) in enumerate(NORMS[k][2]):
                for hf in range(2):
                    pe.wait_ge(S(k + ("_second" if src is A2 else "_first")), TPB * (hf + 1))
                    for t in range(TPB):
                        last = pe.transpose(PS[:, 2 * s + hf, tile(t)], src[:, TPB * hf + t, :], cf("ident"))
                    last.then_inc(S(k + "_turned"), 1)

        def scalar_norm(act, k):
            for s, (_, dst, affine) in enumerate(NORMS[k][2]):
                for hf in range(2):
                    act.wait_ge(S(k + "_turned"), 2 * s + hf + 1)
                    if affine is None:
                        i = act.activation(dst[:, half(hf)], bank(2 * s + hf), ACT.Copy)
                    else:
                        i = act.activation(dst[:, half(hf)], bank(2 * s + hf), ACT.Identity,
                                           bias=affine[1], scale=affine[0])
                    i.then_inc(S(k + "_in"), 1)

        LAYER = {"a": "L0", "s": "L0", "l": "L1", "f": "L3"}
        FROM = {"a": "n0", "s": "n0", "l": "n1", "f": "n3"}
        LINEAR = {"s": (SCALE, 1.0, 1e-4, 1e-6), "l": (None, None, 0.0, 1e-5)}

        def tensor_qkv(pe, a):
            lay = LAYER[a]
            pe.wait_ge(S(FROM[a] + "_in"), 4 if a == "l" else 2)
            pe.wait_ge(ONCE["wall_" + lay], 16)
            if a == "a":
                pe.wait_ge(ONCE["rows_in"], 16)
            if a == "s":
                pe.wait_ge(S("a.ot"), 2)
            for i, m in enumerate(("_wq", "_wk")):
                for hf in range(2):
                    pe.matmul(bank(2 * i + hf), w(lay, a + m), NTT[:, half(hf)], start=True, stop=True
                              ).then_inc(S(a + ".qk"), 1)
            if a == "l":
                for hf in range(2):
                    pe.matmul(bank(4 + hf), w(lay, "gate_w"), AT[:, half(hf)], start=True, stop=True
                              ).then_inc(S("l.gate"), 1)
                pe.wait_ge(S("l.gate_sig"), 1)
                for t in range(NT):
                    last = pe.matmul(PS[:, 6, t:t + 1], T2[:, tile(t)], cf("ones"), start=(t == 0), stop=True,
                                     skip_group_check=True)
                last.then_inc(S("l.gate_mean"), 1)
                pe.wait_ge(S("l.gate_inverse"), 1)
                for hf in range(2):
                    for t in range(TPB):
                        last = pe.transpose(PS[:, 6 + hf, tile(t)], GM[:, TPB * hf + t:TPB * hf + t + 1]
                                            .to_broadcast([P, P]), cf("ident"))
                    last.then_inc(S("l.gate_row"), 1)
            for hf in range(2):
                pe.matmul(bank(4 + hf), row("ones"), row4(a + "_bv"), start=True, stop=True, skip_group_check=True)
                for t in range(TPB):
                    last = pe.matmul(PS[:, 4 + hf, tile(t)], NTT[:, tile(TPB * hf + t)], w(lay, a + "_wv"),
                                     start=False, stop=True, skip_group_check=True)
                last.then_inc(S(a + ".v"), 1)

        def vector_v(v, a):
            for hf in range(2):
                v.wait_ge(S(a + ".v"), hf + 1)
                if a == "a":
                    v.wait_ge(ONCE["v_ready"], 2)
                v.tensor_copy(V[:, TPB * hf:TPB * (hf + 1), :, 0:E],
                              bank(4 + hf).rearrange("p (t h e) -> p t h e", t=TPB, h=H)
                              ).then_inc(S(a + ".v_in"), 1)

        def scalar_qk(act, a):
            lay = LAYER[a]
            if a in "af":
                for i, (dst, bias) in enumerate(((T0, "_bq"), (T1, "_bk"))):
                    act.wait_ge(S(a + ".qk"), 2 * i + 2)
                    act.activation(dst[:, :], bank(2 * i, 2), ACT.Identity, bias=w(lay, a + bias)
                                   ).then_inc(S(a + ".f"), 1)
            else:
                if a == "l":
                    act.wait_ge(S("l.gate"), 2)
                    act.activation(T2[:, :], bank(4, 2), ACT.Sigmoid, bias=w("L1", "gate_b")
                                   ).then_inc(S("l.gate_sig"), 1)
                for i, dst in enumerate((T0, T1)):
                    act.wait_ge(S(a + ".z"), i + 1)
                    act.activation((T2 if i == 0 else T3)[:, :], dst[:, :], ACT.Exp).then_inc(S(a + ".e"), 1)
            for i, dst in enumerate((T0, T1)):
                act.wait_ge(S(a + ".f"), i + 1)
                act.activation(parts_of(i, 0), dst[:, :], ACT.Copy).then_inc(S(a + ".p0"), 1)
            for i in range(2):
                act.wait_ge(S(a + ".r"), i + 1)
                act.activation(parts_of(i, 1), (T2, T3)[i][:, :], ACT.Copy).then_inc(S(a + ".p1"), 1)

        def vector_qk(v, a, link):
            lay = LAYER[a]
            if a in LINEAR:
                sq, sk, plus, _ = LINEAR[a]
                if a == "l":
                    v.wait_ge(S("l.gate_mean"), 1)
                    link(v.tensor_scalar(GM[:, :], PS[:, 6, 0:NT], EPS, None, ALU.add))
                    v.reciprocal(GM[:, :], GM[:, :]).then_inc(S("l.gate_inverse"), 1)
                    v.wait_ge(S("l.gate_row"), 2)
                    link(v.tensor_tensor(T3[:, :], bank(6, 2), T2[:, :], ALU.mult))
                for i, (dst, bias, s) in enumerate(((T0, "_bq", sq), (T1, "_bk", sk))):
                    v.wait_ge(S(a + ".qk"), 2 * i + 2)
                    if a == "l":
                        z = v.scalar_tensor_tensor(out=dst[:, :], in0=bank(2 * i, 2), scalar=w(lay, a + bias),
                                                   in1=T3[:, :], op0=ALU.add, op1=ALU.mult)
                    else:
                        z = v.tensor_scalar(dst[:, :], bank(2 * i, 2), w(lay, a + bias), s, ALU.add, ALU.mult)
                    z.then_inc(S(a + ".z"), 1)
                for i, dst in enumerate((T0, T1)):
                    e = (T2, T3)[i]
                    v.wait_ge(S(a + ".e"), i + 1)
                    link(v.tensor_scalar(e[:, :], e[:, :], 1.0, plus, ALU.min, ALU.add))
                    v.scalar_tensor_tensor(out=dst[:, :], in0=dst[:, :], scalar=0.0, in1=e[:, :],
                                           op0=ALU.max, op1=ALU.add).then_inc(S(a + ".f"), 1)
                v.wait_ge(S(a + ".f"), 2)
            for i, (src, left) in enumerate(((T0, T2), (T1, T3))):
                v.wait_ge(S(a + ".p0"), i + 1)
                v.tensor_tensor(left[:, :], src[:, :], parts_of(i, 0), ALU.subtract).then_inc(S(a + ".r"), 1)
            vector_v(v, a)
            for i, left in enumerate((T2, T3)):
                v.wait_ge(S(a + ".p1"), i + 1)
                v.tensor_tensor(parts_of(i, 2), left[:, :], parts_of(i, 1), ALU.subtract
                                ).then_inc(S(a + ".p2"), 1)

        def sync_stacks(sp, a):
            sp.wait_ge(ONCE["stack_zero"], 1)
            sp.wait_ge(ONCE["q_zero"], 1)
            for part in range(3):
                for i, (dst, groups) in enumerate(((QS, Q_PARTS), (KS, K_PARTS))):
                    sp.wait_ge(S(a + f".p{part}"), i + 1)
                    for g, p in enumerate(groups):
                        if p == part:
                            sp.dma_start(dst[E * g:E * (g + 1), :, :], parts_of(i, part)
                                         ).then_inc(S(a + ".stacked"), 16)
        STACK_DMAS = 16 * (len(Q_PARTS) + len(K_PARTS))

        def plan(a):
            u = 8 if a == "a" else 16
            return dict(units=u, per=2 if a == "a" else 4, lead=u + u // 2)

        def score_1(pe, a, n):
            pl = plan(a)
            G, u = divmod(n, pl["units"])
            b = n % 3
            if n >= 3:
                pe.wait_ge(S(a + ".max"), n - 2)
            if a == "a":
                first = G % TPB == 0
                pe.matmul(bank(b), cb("ident"), cb("mask_q0" if first else "mask_q"), start=True, stop=True, skip_group_check=True)
                for j in range(2):
                    h = 2 * u + j
                    lo = 1 if first else 0
                    last = pe.matmul(PS[:, b, 256 * j + 128 * lo:256 * (j + 1)], QS[0:STACK, h, tile(G)],
                                     KS[0:STACK, h, P * (G - 1 + lo):P * (G + 1)], start=False, stop=True,
                                     skip_group_check=True)
            else:
                bt, g = divmod(G, GROUPS)
                qt, j = divmod(u, 4)
                last = pe.matmul(bank(b), QS[0:STACK, 4 * g + j, tile(TPB * bt + qt)],
                                 KS[0:STACK, 4 * g + j, half(bt)], start=True, stop=True)
            last.then_inc(S(a + ".s1"), 1)

        def max_1(v, a, n):
            pl = plan(a)
            G, u = divmod(n, pl["units"])
            v.wait_ge(S(a + ".s1"), n + 1)
            if a == "a":
                v.tensor_reduce(MX[:, G % 2, 2 * u:2 * u + 2], bank(n % 3).rearrange("p (h k) -> p h k", h=2),
                                AX.X, ALU.max, negate=True).then_inc(S(a + ".max"), 1)
            else:
                v.tensor_reduce(MX[:, G % 2, u:u + 1], bank(n % 3), AX.X, ALU.max, negate=True
                                ).then_inc(S(a + ".max"), 1)

        def max_parts(v, a, G, link):
            pl = plan(a)
            v.wait_ge(S(a + ".max"), (G + 1) * pl["units"])
            if G >= 2:
                v.wait_ge(S(a + ".m_turned"), G - 1)
            m, left = MX[:, G % 2, :], MXR[:, G % 2, :]
            if a == "a":
                out = [MP[:, G % 2, :, :, :].rearrange("p a b c -> p (a b c)")[:, 16 * i:16 * (i + 1)]
                       for i in range(3)]
            else:
                m, left = (y.rearrange("p (t h) -> p t h", t=4) for y in (m, left))
                out = [MP[:, G % 2, :, i, :] for i in range(3)]
            link(v.tensor_copy(out[0], m))
            link(v.tensor_tensor(left, m, out[0], ALU.subtract))
            link(v.tensor_copy(out[1], left))
            v.tensor_tensor(out[2], left, out[1], ALU.subtract).then_inc(S(a + ".m_parts"), 1)

        def turn_max(pe, a, G):
            pe.wait_ge(S(a + ".m_parts"), G + 1)
            if G >= 1:
                pe.wait_ge(S(a + ".m_rows"), G)
            out = bank(7).bitcast(BF16)
            mp = MP[:, G % 2, :, :, :].rearrange("p a b c -> p (a b c)")
            if a == "a":
                last = pe.transpose(out[0:48, 0:P], mp, cb("ident"))
            else:
                for t in range(4):
                    last = pe.transpose(out[0:12, tile(t)], mp[:, 12 * t:12 * (t + 1)], cb("ident"))
            last.then_inc(S(a + ".m_turned"), 1)

        def copy_max(act, a, G):
            act.wait_ge(S(a + ".m_turned"), G + 1)
            if G >= 1:
                act.wait_ge(S(a + ".m_in"), 16 * G)
            r, n = (48, P) if a == "a" else (12, 512)
            act.activation(MR[0:r, 0:n], bank(7).bitcast(BF16)[0:r, 0:n], ACT.Copy
                           ).then_inc(S(a + ".m_rows"), 1)

        def sync_max(sp, a):
            for G in range(8):
                sp.wait_ge(S(a + ".m_rows"), G + 1)
                if a == "a":
                    sp.dma_start(QS[M_ROW:M_ROW + 3, :, tile(G)], MR[0:48, 0:P]).then_inc(S(a + ".m_in"), 16)
                else:
                    bt, g = divmod(G, GROUPS)
                    sp.dma_start(QS[M_ROW:M_ROW + 3, 4 * g:4 * g + 4, half(bt)], MR[0:12, :]
                                 ).then_inc(S(a + ".m_in"), 16)

        def score_2(pe, a, n):
            pl = plan(a)
            G, u = divmod(n, pl["units"])
            b = 3 + n % 3
            if u == 0:
                pe.wait_ge(S(a + ".m_in"), 16 * (G + 1))
            if n >= 3:
                pe.wait_ge(S(a + ".exp"), n - 2)
            if a == "a":
                first = G % TPB == 0
                pe.matmul(bank(b), cb("ident"), cb("mask_k0" if first else "mask_k"), start=True, stop=True, skip_group_check=True)
                for j in range(2):
                    h = 2 * u + j
                    for c in range(1 if first else 0, 2):
                        last = pe.matmul(PS[:, b, 256 * j + 128 * c:256 * j + 128 * (c + 1)],
                                         KS[:, h, tile(G - 1 + c)], QS[:, h, tile(G)],
                                         start=False, stop=True, skip_group_check=True)
            else:
                bt, g = divmod(G, GROUPS)
                kt, j = divmod(u, 4)
                last = pe.matmul(bank(b), KS[:, 4 * g + j, tile(TPB * bt + kt)],
                                 QS[:, 4 * g + j, half(bt)], start=True, stop=True)
            last.then_inc(S(a + ".s2"), 1)

        def exp_2(act, a, n):
            pl = plan(a)
            act.wait_ge(S(a + ".s2"), n + 1)
            if n >= 8:
                act.wait_ge(S(a + ".pv"), (n - 8) // pl["per"] + 1)
            act.activation(PR[:, n % 8, :], bank(3 + n % 3), ACT.Exp, scale=SCALE).then_inc(S(a + ".exp"), 1)

        def values(pe, a, i):
            pl = plan(a)
            per = pl["per"]
            G, k = divmod(i, pl["units"] // per)
            pe.wait_ge(S(a + ".exp"), (i + 1) * per)
            if i == 0:
                pe.wait_ge(S(a + ".v_in"), 2)
            if k == 0 and G >= 1:
                pe.wait_ge(S(a + ".out"), G)
            if a == "a":
                first = G % TPB == 0
                for c in range(1 if first else 0, 2):
                    for j in range(4):
                        u = i * per + j // 2
                        last = pe.matmul(PS[32 * j:32 * j + 32, 6, tile(k)], V[:, G - 1 + c, 4 * k + j, :],
                                         PR[:, u % 8, 256 * (j % 2) + 128 * c:256 * (j % 2) + 128 * (c + 1)],
                                         start=(c == 1 if first else c == 0), stop=(c == 1),
                                         tile_position=(0, 32 * j))
            else:
                bt, g = divmod(G, GROUPS)
                for j in range(4):
                    last = pe.matmul(PS[32 * j:32 * j + 32, 6, :], V[:, TPB * bt + k, 4 * g + j, :],
                                     PR[:, (i * per + j) % 8, :], start=(k == 0), stop=(k == 3),
                                     tile_position=(0, 32 * j))
            last.then_inc(S(a + ".pv"), 1)

        def copy_out(act, a, G):
            pl = plan(a)
            act.wait_ge(S(a + ".pv"), (G + 1) * (pl["units"] // pl["per"]))
            if a == "a":
                i = act.activation(BIG[:, :, tile(G)], bank(6).rearrange("p (g q) -> p g q", g=GROUPS), ACT.Copy)
            else:
                bt, g = divmod(G, GROUPS)
                i = act.activation(BIG[:, g, half(bt)], bank(6), ACT.Copy)
            i.then_inc(S(a + ".out"), 1)

        def steps(a):
            pl = plan(a)
            n, u = 8 * pl["units"], pl["units"]
            for s in range(-pl["lead"], n):
                one = s + pl["lead"]
                turn = one // u - 1 if one % u == 2 and one >= u and one // u <= 8 else None
                yield s, (one if one < n else None), turn

        def tensor_softmax(pe, a):
            pl = plan(a)
            pe.wait_ge(S(a + ".stacked"), STACK_DMAS)
            pe.wait_ge(ONCE["ones_in"], 16)
            pe.wait_ge(ONCE["cb_in"], 16)
            for s, one, turn in steps(a):
                if one is not None:
                    score_1(pe, a, one)
                if turn is not None:
                    turn_max(pe, a, turn)
                if s >= 0:
                    score_2(pe, a, s)
                    if s % pl["per"] == pl["per"] - 1 and s >= pl["per"]:
                        values(pe, a, s // pl["per"] - 1)
            values(pe, a, 8 * pl["units"] // pl["per"] - 1)

        def scalar_softmax(act, a):
            pl = plan(a)
            for s, _, turn in steps(a):
                if turn is not None:
                    copy_max(act, a, turn)
                if s >= 0:
                    exp_2(act, a, s)
                    if s % pl["units"] == pl["per"] + 1 and s >= pl["units"]:
                        copy_out(act, a, s // pl["units"] - 1)
            copy_out(act, a, 7)

        def vector_softmax(v, a, link):
            pl = plan(a)
            for n in range(8 * pl["units"]):
                max_1(v, a, n)
                if n % pl["units"] == pl["units"] - 1:
                    max_parts(v, a, n // pl["units"], link)

        def tensor_linear(pe, a):
            pe.wait_ge(S(a + ".f"), 2)
            pe.wait_ge(S(a + ".v_in"), 2)
            for hf in range(2):
                for t in range(TPB):
                    last = pe.transpose(PS[:, 4 + hf, tile(t)], T1[:, tile(TPB * hf + t)], cf("ident"))
                last.then_inc(S(a + ".k_turned"), 1)
            pe.wait_ge(S(a + ".k_in"), 2)
            pe.wait_ge(S(a + ".stacked"), STACK_DMAS)

            def products(n, g):
                i = GROUPS * n + g
                if i >= 2:
                    pe.wait_ge(S(a + ".masked"), i - 1)
                for j in range(4):
                    h = 4 * g + j
                    last = pe.matmul(PS[:, i % 2, tile(j)], KS[0:STACK, h, tile(n)], QS[0:STACK, h, tile(n)],
                                     start=True, stop=True)
                last.then_inc(S(a + ".s"), 1)

            def through(n, g):
                i = GROUPS * n + g
                o = 2 + n % 2
                t = n % TPB
                if g == 0 and n >= 2:
                    pe.wait_ge(S(a + ".out"), n - 1)
                if t:
                    if g == 0:
                        pe.wait_ge(S(a + ".state_in"), n - n // TPB)
                    pe.matmul(PS[:, o, tile(g)], SM[:, n % 2, tile(g)], T0[:, tile(n)], start=True, stop=True, skip_group_check=True)
                pe.wait_ge(S(a + ".masked"), i + 1)
                for j in range(4):
                    last = pe.matmul(PS[32 * j:32 * j + 32, o, tile(g)], V[:, n, 4 * g + j, :],
                                     PR[:, i % 4, tile(j)], start=(t == 0), stop=True,
                                     tile_position=(0, 32 * j), skip_group_check=True)
                last.then_inc(S(a + ".pv"), 1)

            def state(n):
                t = n % TPB
                if n // TPB or t:
                    pe.wait_ge(S(a + ".state_in"), n - n // TPB)
                pe.matmul(bank(4), T2[:, tile(n)], V[:, n, :, :].rearrange("p h c -> p (h c)"),
                          start=(t == 0), stop=True, skip_group_check=True
                          ).then_inc(S(a + ".state"), 1)

            products(0, 0)
            for n in range(NT):
                if n % TPB < TPB - 1:
                    state(n)
                for g in range(GROUPS):
                    i = GROUPS * n + g + 1
                    if i < GROUPS * NT:
                        products(*divmod(i, GROUPS))
                    through(n, g)

        def vector_linear(v, a):
            for hf in range(2):
                v.wait_ge(S(a + ".k_turned"), hf + 1)
                if hf == 0:
                    v.wait_ge(S(a + ".p2"), 2)
                v.tensor_copy(T2[:, half(hf)], bank(4 + hf)).then_inc(S(a + ".k_in"), 1)
            mask = cf("causal").unsqueeze(1).to_broadcast([P, 4, P])
            for n in range(NT):
                if n % TPB < TPB - 1:
                    v.wait_ge(S(a + ".state"), n - n // TPB + 1)
                    if n >= 1:
                        v.wait_ge(S(a + ".pv"), GROUPS * n)
                    v.tensor_tensor(SM[:, (n + 1) % 2, :], bank(4), cf("block"), ALU.mult
                                    ).then_inc(S(a + ".state_in"), 1)
                for g in range(GROUPS):
                    i = GROUPS * n + g
                    v.wait_ge(S(a + ".s"), i + 1)
                    if i >= 4:
                        v.wait_ge(S(a + ".pv"), i - 3)
                    v.tensor_tensor(PR[:, i % 4, :].rearrange("p (j q) -> p j q", j=4),
                                    bank(i % 2).rearrange("p (j q) -> p j q", j=4), mask, ALU.mult
                                    ).then_inc(S(a + ".masked"), 1)

        def scalar_linear(act, a):
            act.wait_ge(S(a + ".stacked"), STACK_DMAS)
            for n in range(NT):
                act.wait_ge(S(a + ".pv"), GROUPS * (n + 1))
                act.activation(BIG[:, :, tile(n)], bank(2 + n % 2).rearrange("p (g q) -> p g q", g=GROUPS),
                               ACT.Copy).then_inc(S(a + ".out"), 1)

        def tensor_gather(pe, a):
            pe.wait_ge(S(a + ".out"), 8)
            for hf in range(2):
                for t in range(TPB):
                    for g in range(GROUPS):
                        last = pe.matmul(PS[:, 2 * hf + t // 2, (t % 2) * 4 * PICK + g * PICK:
                                            (t % 2) * 4 * PICK + (g + 1) * PICK],
                                         BIG[:, g, tile(TPB * hf + t)], cf("pick"), start=True, stop=True,
                                         skip_group_check=True)
                last.then_inc(S(a + ".gathered"), 1)
            for hf in range(2):
                pe.wait_ge(S(a + ".divided"), hf + 1)
                for t in range(TPB):
                    last = pe.transpose(PS[:, 4 + hf, tile(t)], T3[:, tile(TPB * hf + t)], cf("ident"))
                last.then_inc(S(a + ".ot_turned"), 1)

        def vector_gather(v, a, link):
            for hf in range(2):
                v.wait_ge(S(a + ".gathered"), hf + 1)
                got = PS[:, 2 * hf:2 * hf + 2, 0:8 * PICK].rearrange("p b (t c) -> p b t c", c=PICK)
                den = DEN[:, hf, :].rearrange("p (b t j) -> p b t j", b=2, j=4)
                if a in LINEAR:
                    link(v.tensor_scalar(den, got[:, :, :, 4 * E:PICK], LINEAR[a][3], None, ALU.add))
                    link(v.reciprocal(DEN[:, hf, :], DEN[:, hf, :]))
                else:
                    link(v.reciprocal(den, got[:, :, :, 4 * E:PICK]))
                for b in range(2):
                    n = TPB * hf + 2 * b
                    i = v.tensor_tensor(T3[:, P * n:P * (n + 2)].rearrange("p (t j e) -> p t j e", t=8, e=E),
                                        got[:, b, :, 0:4 * E].rearrange("p t (j e) -> p t j e", e=E),
                                        DEN[:, hf, 32 * b:32 * (b + 1)].rearrange("p (t j) -> p t j", t=8)
                                        .unsqueeze(3).to_broadcast([P, 8, 4, E]), ALU.mult)
                i.then_inc(S(a + ".divided"), 1)

        def scalar_gather(act, a):
            for hf in range(2):
                act.wait_ge(S(a + ".ot_turned"), hf + 1)
                act.activation(OT[:, half(hf)], bank(4 + hf), ACT.Copy).then_inc(S(a + ".ot"), 1)

        def tensor_back(pe, name, bias, lhs, rhs, depth=1, ready=None):
            for hf in range(2):
                if ready:
                    ready(hf)
                if bias:
                    pe.matmul(bank(4 + hf), row("ones"), row4(bias), start=True, stop=True, skip_group_check=True)
                for t in range(TPB):
                    for k in range(depth):
                        last = pe.matmul(PS[:, 4 + hf, tile(t)], lhs(k, TPB * hf + t), rhs(k, TPB * hf + t),
                                         start=(not bias and t == 0 and k == 0), stop=True,
                                         skip_group_check=True)
                last.then_inc(S(name), 1)

        def vector_back(v, name, dst, other, done):
            for hf in range(2):
                v.wait_ge(S(name), hf + 1)
                ts = slice(TPB * hf, TPB * (hf + 1))
                v.tensor_tensor(dst[:, ts, :], bank(4 + hf).rearrange("p (t d) -> p t d", t=TPB),
                                other[:, ts, :], ALU.add).then_inc(S(done), 1)
            v.wait_ge(S(done), 2)

        FFN = {"L0": "n0f", "L1": "n1f", "L3": "n3f"}

        def sync_experts(sp, m):
            c = MOE[m]
            gu, dn, hot, t3 = T["in" + m], T["down" + m], T["hot" + m], 3 * c["table"]
            wide = 2 * P if c["glu"] else P

            def load(b, s):
                sp.dma_start(GU[:, s, 0:wide], gu[bass.ds(b * P, P), :]).then_inc(S(f"{m}.gu{s}"), 16)
                sp.dma_start(HOT[0:t3, s, :], hot[bass.ds(b * t3, t3), :]).then_inc(S(f"{m}.gu{s}"), 16)

            def load_down(b, s):
                sp.dma_start(DN[:, s, :], dn[bass.ds(b * P, P), :]).then_inc(S(f"{m}.dn{s}"), 16)

            for s in range(2):
                load(s, s)
                load_down(s, s)
            pairs = c["blocks"] // 2
            with sp.Fori(1, pairs) as i:
                for s in range(2):
                    sp.wait_ge(S(m + ".front"), i * 4 + (2 * s - 2))
                    load(i * 2 + s, s)
                    sp.wait_ge(S(m + ".down"), i * 4 + (2 * s - 2))
                    load_down(i * 2 + s, s)
            if c["blocks"] % 2:
                sp.wait_ge(S(m + ".front"), 4 * pairs - 2)
                load(2 * pairs, 0)
                sp.wait_ge(S(m + ".down"), 4 * pairs - 2)
                load_down(2 * pairs, 0)

        def tensor_experts(pe, m):
            c = MOE[m]
            units, t3, E1 = 2 * c["blocks"], 3 * c["table"], c["table"]
            lay = m
            NR = {"L0": 9, "L1": 16, "L3": 8}[m]
            pe.wait_ge(S(FFN[m] + "_in"), 2)
            for t in range(NT):
                last = pe.matmul(PS[:, 7, 32 * t:32 * t + NR], AT[:, tile(t)], w(lay, "router" + m[1]),
                                 start=(t == 0), stop=True, skip_group_check=True)
            last.then_inc(S(m + ".logits"), 1)
            for hf in range(2):
                pe.matmul(bank(6 if hf == 0 else 5), zero[:, 0:P], zero[:, :], start=True, stop=True,
                          skip_group_check=True)

            pe.wait_ge(S(m + ".cp"), 1)
            out = bank(4).bitcast(BF16)
            for t in range(NT):
                last = pe.transpose(out[0:t3, tile(t)], CP[:, t, :, 0:E1].rearrange("p a b -> p (a b)")
                                    if E1 == 17 else CPV(m)[:, t, :], cb("ident"))
            last.then_inc(S(m + ".ct_turned"), 1)
            if m == "L3":
                for hf in range(2):
                    for t in range(TPB):
                        last = pe.transpose(PS[0:E1, 2 + hf, tile(t)], CW[:, TPB * hf + t, 0:E1], cf("ident"))
                last.then_inc(S("L3.c_turned"), 1)
                pe.wait_ge(S("L3.c_in"), 1)
                for t in range(NT):
                    pe.matmul(PS[:, 6 if t < TPB else 5, tile(t % TPB)], C32[0:E1, tile(t)], w("L3", "b2"),
                              start=False, stop=True, skip_group_check=True)
            pe.wait_ge(S(m + ".ct_in"), 1)

            G0 = (0, 2)
            W0 = (4, 7)

            def front(n, q):
                s = (q // 2) % 2
                hf = q % 2
                if q % 2 == 0:
                    if isinstance(n, int):
                        pe.wait_ge(S(f"{m}.gu{s}"), 32 * (n // 4 + 1))
                    else:
                        i4, _ = n_parts[0]
                        pe.wait_ge(S(f"{m}.gu{s}"), i4)
                if not (isinstance(n, int) and n < 2):
                    pe.wait_ge(S(m + ".hid"), n - 1)
                pe.matmul(bank(G0[hf]), GU[:, s, 0:P], AT[:, half(hf)], start=True, stop=True)
                if c["glu"]:
                    pe.matmul(bank(G0[hf] + 1), GU[:, s, P:2 * P], AT[:, half(hf)], start=True, stop=True)
                pe.matmul(bank(W0[hf]), HOT[0:t3, s, :], CT[0:t3, half(hf)], start=True, stop=True
                          ).then_inc(S(m + ".front"), 1)

            def down(n, q):
                s = (q // 2) % 2
                hf = q % 2
                if q % 2 == 0:
                    if isinstance(n, int):
                        pe.wait_ge(S(f"{m}.dn{s}"), 16 * (n // 4 + 1))
                    else:
                        pe.wait_ge(S(f"{m}.dn{s}"), n_parts[0][1])
                pe.wait_ge(S(m + ".hid"), n + 1)
                for t in range(TPB):
                    last = pe.matmul(PS[:, 6 - hf, tile(t)], HID(q % 2)[:, tile(t)], DN[:, s, :],
                                     start=False, stop=True, skip_group_check=True)
                last.then_inc(S(m + ".down"), 1)

            n_parts = [None]
            front(0, 0)
            for u in range(4):
                front(u + 1, (u + 1) % 4)
                down(u, u)
            last4 = (units - 1) // 4
            with pe.Fori(1, last4) as i:
                for q in range(4):
                    ahead = (i + 2) if q == 3 else (i + 1)
                    n_parts[0] = (ahead * 32, (i + 1) * 16)
                    front(i * 4 + (q + 1), (q + 1) % 4)
                    down(i * 4 + q, q)
            for u in range(4 * last4, units):
                if u + 1 < units:
                    front(u + 1, (u + 1) % 4)
                down(u, u % 4)

        def HID(s):
            return PR[:, s, :]

        def CPV(m):
            n = 3 * MOE[m]["table"]
            return CP[:, :, :, :].rearrange("p t a b -> p (t a b)")[:, 0:NT * n].rearrange("p (t n) -> p t n", t=NT)

        def scalar_experts(act, m, link):
            c = MOE[m]
            E1, t3 = c["table"], 3 * c["table"]
            act.wait_ge(S(m + ".ct_turned"), 1)
            act.activation(CT[0:t3, :], bank(4).bitcast(BF16)[0:t3, :], ACT.Copy).then_inc(S(m + ".ct_in"), 1)
            if m == "L3":
                act.wait_ge(S("L3.c_turned"), 1)
                act.activation(C32[0:E1, :], PS[0:E1, 2:4, :].rearrange("p a b -> p (a b)"), ACT.Copy
                               ).then_inc(S("L3.c_in"), 1)
                act.wait_ge(S("L3.b1g"), 1)

            def unit(n, q):
                s = q // 2
                if not c["glu"] and q % 2 == 0:
                    b = n // 2 if isinstance(n, int) else base[0] * 2 + s
                    act.activation(GB[:, s, :], b1g[:, :, :].rearrange("p b c -> p (b c)")[:, bass.ds(b * 2, 2)],
                                   ACT.Copy).then_inc(S("L3.gb"), 1)
                    act.wait_ge(S("L3.gb"), b + 1)
                act.wait_ge(S(m + ".front"), n + 1)
                if not (isinstance(n, int) and n < 2):
                    act.wait_ge(S(m + ".hid"), n - 1)
                o, i = PR[:, 2 + q % 2, :], bank(2 * (q % 2))
                if c["glu"]:
                    act.activation(o, i, ACT.Silu).then_inc(S(m + ".act"), 1)
                else:
                    act.activation(o, i, ACT.Gelu, bias=GB[:, s, 0:1], scale=GB[:, s, 1:2]
                                   ).then_inc(S(m + ".act"), 1)

            base = [None]
            for u in range(4):
                unit(u, u)
            units = 2 * c["blocks"]
            last4 = (units - 1) // 4
            with act.Fori(1, last4) as i:
                base[0] = i
                for q in range(4):
                    unit(i * 4 + q, q)
            for u in range(4 * last4, units):
                unit(u, u % 4)

        def vector_experts(v, m, link):
            c = MOE[m]

            def unit(n, q):
                s = q % 2
                v.wait_ge(S(m + ".act"), n + 1)
                if not (isinstance(n, int) and n < 2):
                    v.wait_ge(S(m + ".down"), n - 1)
                src = PR[:, 2 + s, :]
                if c["glu"]:
                    v.tensor_tensor(PR[:, 4 + s, :], src, bank(2 * s + 1), ALU.mult).then_inc(S(m + ".gated"), 1)
                    v.wait_ge(S(m + ".gated"), n + 1)
                    src = PR[:, 4 + s, :]
                v.tensor_tensor(HID(s), src, bank((4, 7)[s]), ALU.mult).then_inc(S(m + ".hid"), 1)

            unit_loop(v, 2 * c["blocks"], unit)
            v.wait_ge(S(m + ".down"), 2 * c["blocks"])

        def rank_of(v, link, s, n, k, before, out, scratch, scratch2):
            G = s.shape[1]
            big = [P, G, n, n]
            sj = s.unsqueeze(2).to_broadcast(big)
            si = s.unsqueeze(3).to_broadcast(big)
            bf = before.rearrange("p (i j) -> p i j", i=n).unsqueeze(1).to_broadcast(big)
            s1 = scratch[:, 0:G * n * n].rearrange("p (g i j) -> p g i j", g=G, i=n)
            s2 = scratch2[:, 0:G * n * n].rearrange("p (g i j) -> p g i j", g=G, i=n)
            v.tensor_tensor(s1, sj, si, ALU.is_gt).then_inc(link.sem, 1)
            link.n += 1
            link(v.tensor_tensor(s2, sj, si, ALU.is_equal))
            link(v.tensor_tensor(s2, s2, bf, ALU.mult))
            link(v.tensor_tensor(s1, s1, s2, ALU.add))
            link(v.tensor_reduce(out, s1, AX.X, ALU.add))
            link(v.tensor_scalar(out, out, float(k) - 0.5, None, ALU.is_lt))

        def bc(ap, n):
            return ap.unsqueeze(2).to_broadcast([P, NT, n])

        def vector_route(v, m, link):
            c = MOE[m]
            n, E1 = c["experts"], c["table"]
            lg = T0[:, 0:NT * 32].rearrange("p (t e) -> p t e", t=NT)
            sc = T0[:, 256:256 + NT * n].rearrange("p (t e) -> p t e", t=NT)
            sel = T0[:, 512:512 + NT * n].rearrange("p (t e) -> p t e", t=NT)
            tmp = T0[:, 768:768 + NT * n].rearrange("p (t e) -> p t e", t=NT)
            r1 = small[:, 2, :]
            v.wait_ge(S(m + ".logits"), 1)
            lp = bank(7)[:, 0:NT * 32].rearrange("p (t e) -> p t e", t=NT)
            NR = {"L0": 9, "L1": 16, "L3": 8}[m]
            if m == "L3":
                link(v.tensor_tensor(lg[:, :, 0:8], lp[:, :, 0:8],
                                     w("L3", "router3_b").unsqueeze(1).to_broadcast([P, NT, 8]), ALU.add))
            else:
                link(v.tensor_copy(lg[:, :, 0:NR], lp[:, :, 0:NR]))
            if m == "L1":
                v.engine_nop().then_inc(S(m + ".lg"), 1) if False else \
                    v.tensor_copy(tmp, lg[:, :, 0:16]).then_inc(S(m + ".lg"), 1)
                v.wait_ge(S(m + ".sg"), 1)
                sfc = T1[:, 0:128].rearrange("p (t e) -> p t e", t=NT)
                link(v.tensor_tensor(sfc, sc, w("L1", "router1_b").unsqueeze(1).to_broadcast([P, NT, 16]), ALU.add))
                g4 = T1[:, 0:128].rearrange("p (g e) -> p g e", e=4)
                top = T1[:, 128:256].rearrange("p (g e) -> p g e", e=4)
                rank_of(v, link, g4, 4, 2, cf("before4"), top, T2, T3)
                link(v.tensor_tensor(top, top, g4, ALU.mult))
                gs = T1[:, 256:288]
                link(v.tensor_reduce(gs, top, AX.X, ALU.add))
                gsel = T1[:, 288:320].rearrange("p (t g) -> p t g", t=NT)
                rank_of(v, link, gs.rearrange("p (t g) -> p t g", t=NT), 4, 2, cf("before4"), gsel, T2, T3)
                chosen = T1[:, 288:320].unsqueeze(2).to_broadcast([P, 32, 4])
                mk = T1[:, 320:448].rearrange("p (g e) -> p g e", e=4)
                link(v.tensor_tensor(mk, g4, chosen, ALU.mult))
                low = T1[:, 448:480]
                link(v.tensor_scalar(low, T1[:, 288:320], -NEG, NEG, ALU.mult, ALU.add))
                link(v.tensor_tensor(mk, mk, low.unsqueeze(2).to_broadcast([P, 32, 4]), ALU.add))
                mt = T1[:, 320:448].rearrange("p (t e) -> p t e", t=NT)
                for hf in range(2):
                    ts = slice(4 * hf, 4 * hf + 4)
                    rank_of(v, link, mt[:, ts, :], 16, 4, cf("before16"), sel[:, ts, :], T2, T3)
                link(v.tensor_tensor(sel, sel, sc, ALU.mult))
                link(v.tensor_reduce(r1, sel, AX.X, ALU.add))
                link(v.tensor_scalar(r1, r1, 1e-20, None, ALU.add))
                link(v.reciprocal(r1, r1))
                link(v.tensor_tensor(sel, sel, bc(r1, 16), ALU.mult))
                link(v.tensor_scalar(CW[:, :, 0:16], sel, 2.5, None, ALU.mult))
                link(v.memset(CW[:, :, 16], 1.0))
            else:
                link(v.tensor_reduce(r1, lg[:, :, 0:8], AX.X, ALU.max))
                v.tensor_tensor(tmp, lg[:, :, 0:8], bc(r1, 8), ALU.subtract).then_inc(S(m + ".lg"), 1)
                v.wait_ge(S(m + ".sg"), 1)
                link(v.tensor_reduce(r1, sc, AX.X, ALU.add))
                link(v.reciprocal(r1, r1))
                link(v.tensor_tensor(sc, sc, bc(r1, 8), ALU.mult))
                rank_of(v, link, sc, 8, 2, cf("before8"), sel, T2, T3)
                if m == "L0":
                    link(v.tensor_tensor(CW[:, :, 0:8], sel, sc, ALU.mult))
                    v.wait_ge(S("L0.sw"), 1)
                    link(v.tensor_copy(CW[:, :, 8], small[:, 6, :]))
                else:
                    link(v.tensor_tensor(sel, sel, sc, ALU.mult))
                    link(v.tensor_reduce(r1, sel, AX.X, ALU.add))
                    link(v.reciprocal(r1, r1))
                    link(v.tensor_tensor(CW[:, :, 0:8], sel, bc(r1, 8), ALU.mult))
                    v.wait_ge(S("L3.sw"), 1)
                    link(v.tensor_copy(CW[:, :, 8], vec[:, 0:1].to_broadcast([P, NT])))
                    link(v.tensor_tensor(b1g[:, :, 0], w("L3", "b1"), w("L3", "gate"), ALU.mult))
                    v.tensor_copy(b1g[:, :, 1], w("L3", "gate")).then_inc(S("L3.b1g"), 1)
            n3 = 3 * E1
            cp = CPV(m).rearrange("p t (a e) -> p t a e", a=3)
            cw, left = CW[:, :, 0:E1], CWR[:, :, 0:E1]
            link(v.tensor_copy(cp[:, :, 0, :], cw))
            link(v.tensor_tensor(left, cw, cp[:, :, 0, :], ALU.subtract))
            link(v.tensor_copy(cp[:, :, 1, :], left))
            v.tensor_tensor(cp[:, :, 2, :], left, cp[:, :, 1, :], ALU.subtract).then_inc(S(m + ".cp"), 1)

        def scalar_route(act, m):
            c = MOE[m]
            n = c["experts"]
            act.wait_ge(S(m + ".lg"), 1)
            fn = ACT.Sigmoid if m == "L1" else ACT.Exp
            act.activation(T0[:, 256:256 + NT * n], T0[:, 768:768 + NT * n], fn).then_inc(S(m + ".sg"), 1)
            if m == "L0":
                act.activation(small[:, 6, :], T0[:, 0:NT * 32].rearrange("p (t e) -> p t e", t=NT)[:, :, 8],
                               ACT.Sigmoid).then_inc(S("L0.sw"), 1)
            if m == "L3":
                act.activation(vec[:, 0:1], w("L3", "shared_w"), ACT.Sigmoid).then_inc(S("L3.sw"), 1)

        def vector_add_experts(v, m, link):
            for hf in range(2):
                ts = slice(TPB * hf, TPB * (hf + 1))
                y = bank(6 - hf).rearrange("p (t d) -> p t d", t=TPB)
                if m == "L1":
                    link(v.tensor_tensor(A[:, ts, :], A[:, ts, :], y, ALU.add))
                    link(v.tensor_tensor(X[:, ts, :], X[:, ts, :], A[:, ts, :], ALU.add))
                else:
                    link(v.tensor_tensor(X[:, ts, :], X[:, ts, :], y, ALU.add))

        pass_ = ctx_loop.enter_context(nc.Fori(0, PASSES))
        phase = {}

        def begin_phase():
            phase["sems"], phase["block"] = ExitStack(), ExitStack()
            return phase["block"].enter_context(nc.Block())

        def end_phase():
            phase["block"].close()
            numbers = sorted(x.num for x in sems.values())
            assert numbers == list(range(numbers[0], numbers[0] + len(numbers)))
            nc.all_engine_barrier(sems_to_clear=range(numbers[0], numbers[-1] + 1))
            phase["sems"].close()
            sems.clear()

        block = begin_phase()

        @block.sync
        def _(sp):
            sp.dma_start(flat(X), T["x"][bass.ds(pass_ * P, P), :]).then_inc(S("x_in"), 16)
            sync_stacks(sp, "a")
            sync_max(sp, "a")
            sync_stacks(sp, "s")
            if stop > 1:
                sync_experts(sp, "L0")
            if stop > 2:
                sync_stacks(sp, "l")
            if stop > 3:
                sync_experts(sp, "L1")

        @block.gpsimd
        def _(g):
            chain = Link(g, S("gpsimd_chain"))
            g.wait_ge(ONCE["half_ready"], 1)
            for i, k in enumerate(("n0", "n0m", "n0f", "n1", "n1f")):
                if stop >= i:
                    gpsimd_norm(g, k, chain)

        @block.scalar
        def _(act):
            link = Link(act, S("scalar_chain"))
            act.wait_ge(ONCE["wall_L0"], 16)
            scalar_norm(act, "n0")
            scalar_qk(act, "a")
            scalar_softmax(act, "a")
            scalar_gather(act, "a")
            scalar_qk(act, "s")
            scalar_linear(act, "s")
            scalar_gather(act, "s")
            scalar_norm(act, "n0m")
            for m in range(4):
                for hf in range(2):
                    act.wait_ge(S("mlp.up"), 2 * m + hf + 1)
                    act.activation(BIG[:, m, half(hf)], bank((2 * m + hf) % 4), ACT.Gelu,
                                   bias=w("L0", "b1m", m, m + 1)).then_inc(S("mlp.gelu"), 1)
            if stop > 1:
                scalar_norm(act, "n0f")
                scalar_route(act, "L0")
                scalar_experts(act, "L0", link)
            if stop > 2:
                act.wait_ge(ONCE["wall_L1"], 16)
                scalar_norm(act, "n1")
                scalar_qk(act, "l")
                scalar_linear(act, "l")
                scalar_gather(act, "l")
            if stop > 3:
                scalar_norm(act, "n1f")
                scalar_route(act, "L1")
                scalar_experts(act, "L1", link)

        @block.vector
        def _(v):
            link = Link(v, S("vector_chain"))
            v.wait_ge(S("x_in"), 16)
            v.wait_ge(ONCE["wall_L0"], 16)
            v.wait_ge(ONCE["cf_in"], 16)
            vector_norm(v, "n0")
            vector_qk(v, "a", link)
            vector_softmax(v, "a", link)
            vector_gather(v, "a", link)
            v.wait_ge(S("a.proj"), 2)
            link(v.tensor_scalar(flat(A2), bank(6, 2), w("L0", "bp_a"), None, ALU.add))
            vector_qk(v, "s", link)
            vector_linear(v, "s")
            vector_gather(v, "s", link)
            v.wait_ge(S("s.proj"), 2)
            v.scalar_tensor_tensor(out=flat(A2), in0=bank(6, 2), scalar=w("L0", "bo_s"), in1=flat(A2),
                                   op0=ALU.add, op1=ALU.add).then_inc(S("s.sum"), 1)
            vector_back(v, "mixed", tok(T0), A, "x1")
            vector_norm(v, "n0m")
            vector_back(v, "mlp.back", tok(T0), tok(T0), "mlp.done")
            link(v.tensor_tensor(flat(X), flat(X), T0[:, :], ALU.add))
            if stop > 1:
                vector_norm(v, "n0f")
                vector_route(v, "L0", link)
                vector_experts(v, "L0", link)
                vector_add_experts(v, "L0", link)
            if stop > 2:
                v.wait_ge(ONCE["wall_L1"], 16)
                vector_norm(v, "n1")
                vector_qk(v, "l", link)
                vector_linear(v, "l")
                vector_gather(v, "l", link)
                vector_back(v, "l.back", X, X, "l.done")
            if stop > 3:
                vector_norm(v, "n1f")
                vector_route(v, "L1", link)
                vector_experts(v, "L1", link)
                vector_add_experts(v, "L1", link)

        @block.tensor
        def _(pe):
            pe.wait_ge(ONCE["cf_in"], 16)
            pe.wait_ge(ONCE["zero_in"], 1)
            tensor_norm(pe, "n0")
            tensor_qkv(pe, "a")
            tensor_softmax(pe, "a")
            tensor_gather(pe, "a")
            for hf in range(2):
                pe.wait_ge(S("a.ot"), hf + 1)
                pe.matmul(bank(6 + hf), w("L0", "Wp_a"), OT[:, half(hf)], start=True, stop=True
                          ).then_inc(S("a.proj"), 1)
            tensor_qkv(pe, "s")
            tensor_linear(pe, "s")
            tensor_gather(pe, "s")
            for hf in range(2):
                pe.wait_ge(S("s.ot"), hf + 1)
                pe.matmul(bank(6 + hf), w("L0", "Wo_s"), OT[:, half(hf)], start=True, stop=True
                          ).then_inc(S("s.proj"), 1)
            pe.wait_ge(S("s.sum"), 1)
            tensor_back(pe, "mixed", "bo", lambda k, t: flat(A2)[:, tile(t)], lambda k, t: w("L0", "Wo"))
            tensor_norm(pe, "n0m")
            pe.wait_ge(S("n0m_in"), 2)
            for m in range(4):
                for hf in range(2):
                    n = 2 * m + hf
                    if n >= 4:
                        pe.wait_ge(S("mlp.gelu"), n - 3)
                    pe.matmul(bank(n % 4), w("L0", "W1", P * m, P * (m + 1)), T2[:, half(hf)],
                              start=True, stop=True).then_inc(S("mlp.up"), 1)
            pe.wait_ge(S("mlp.gelu"), 8)
            tensor_back(pe, "mlp.back", "b2m", lambda k, t: BIG[:, k, tile(t)],
                        lambda k, t: w("L0", "W2", P * k, P * (k + 1)), depth=4)
            if stop > 1:
                tensor_norm(pe, "n0f")
                tensor_experts(pe, "L0")
            if stop > 2:
                tensor_norm(pe, "n1")
                tensor_qkv(pe, "l")
                tensor_linear(pe, "l")
                tensor_gather(pe, "l")
                tensor_back(pe, "l.back", "proj_b", lambda k, t: OT[:, tile(t)], lambda k, t: w("L1", "proj_w"),
                            ready=lambda hf: pe.wait_ge(S("l.ot"), hf + 1))
            if stop > 3:
                tensor_norm(pe, "n1f")
                tensor_experts(pe, "L1")

        end_phase()

        block = begin_phase()

        @block.sync
        def _(sp):
            if stop > 6:
                sync_stacks(sp, "f")
                sync_max(sp, "f")
            if stop > 7:
                sync_experts(sp, "L3")
            sp.wait_ge(S("x_final"), 1)
            sp.dma_start(T["out"][bass.ds(pass_ * P, P), :], flat(X)).then_inc(S("out_done"), 16)
            sp.wait_ge(S("out_done"), 16)

        @block.gpsimd
        def _(g):
            chain = Link(g, S("gpsimd_chain"))
            for i, k in enumerate(("n2", "n2f", "n3", "n3f")):
                if stop > i + 4:
                    gpsimd_norm(g, k, chain)
            if stop > 7:
                g.wait_ge(S("y_moments"), NT)
                chain(g.tensor_scalar(small[:, 0, :], moments[:, :, 1], EPS, None, ALU.add))
                g.tensor_tensor(small[:, 1, :], small[:, 0, :], small[:, 7, :], ALU.pow).then_inc(S("y_rstd"), 1)

        @block.scalar
        def _(act):
            link = Link(act, S("scalar_chain"))
            if stop > 4:
                act.wait_ge(ONCE["wall_L2"], 16)
                scalar_norm(act, "n2")
                act.wait_ge(S("g.proj"), 4)
                act.activation(T1[:, half(0)], bank(2), ACT.Tanh, bias=w("L2", "bz")).then_inc(S("g.z"), 1)
                act.activation(T1[:, half(1)], bank(3), ACT.Sigmoid, bias=w("L2", "bo")).then_inc(S("g.z"), 1)
                act.wait_ge(S("g.arg"), 1)
                act.activation(T2[:, :], T2[:, :], ACT.Exp).then_inc(S("g.exp"), 1)
                act.wait_ge(S("g.c"), 1)
                act.activation(T3[:, half(1)], T3[:, half(0)], ACT.Tanh).then_inc(S("g.tanh"), 1)
            if stop > 5:
                scalar_norm(act, "n2f")
                for m in range(4):
                    for hf in range(2):
                        n = 2 * m + hf
                        act.wait_ge(S("spk.up"), n + 1)
                        if n >= 4:
                            act.wait_ge(S("spk.h"), n - 3)
                        act.activation(PR[:, n % 4, :], bank(n % 4), ACT.Relu).then_inc(S("spk.relu"), 1)
            if stop > 6:
                act.wait_ge(ONCE["wall_L3"], 16)
                scalar_norm(act, "n3")
                scalar_qk(act, "f")
                scalar_softmax(act, "f")
                scalar_gather(act, "f")
            if stop > 7:
                scalar_norm(act, "n3f")
                scalar_route(act, "L3")
                scalar_experts(act, "L3", link)

        @block.vector
        def _(v):
            link = Link(v, S("vector_chain"))
            if stop > 4:
                v.wait_ge(ONCE["wall_L2"], 16)
                vector_norm(v, "n2")
                li, lf = T0[:, half(0)], T0[:, half(1)]
                v.wait_ge(S("g.proj"), 2)
                link(v.tensor_scalar(li, bank(0), w("L2", "bi"), 20.0, ALU.add, ALU.min))
                link(v.tensor_scalar(lf, bank(1), w("L2", "bf"), 20.0, ALU.add, ALU.min))
                link(v.tensor_scalar(T0[:, :], T0[:, :], -20.0, None, ALU.max))
                ms = BIG[:, 0, 0:513]
                link(v.memset(BIG[:, 0, 0:1], 0.0))
                link(v.tensor_tensor_scan(ms[:, 1:513], lf, li, 0.0, ALU.add, ALU.max))
                link(v.tensor_tensor(lf, lf, ms[:, 0:512], ALU.add))
                link(v.tensor_tensor(T2[:, half(0)], li, ms[:, 1:513], ALU.subtract))
                v.tensor_tensor(T2[:, half(1)], lf, ms[:, 1:513], ALU.subtract).then_inc(S("g.arg"), 1)
                v.wait_ge(S("g.exp"), 1)
                v.wait_ge(S("g.z"), 2)
                link(v.tensor_tensor(T2[:, half(0)], T2[:, half(0)], T1[:, half(0)], ALU.mult))
                v.tensor_tensor_scan(T3[:, half(0)], T2[:, half(1)], T2[:, half(0)], 0.0, ALU.mult, ALU.add
                                     ).then_inc(S("g.c"), 1)
                v.wait_ge(S("g.tanh"), 1)
                v.tensor_tensor(OT[:, half(0)], T1[:, half(1)], T3[:, half(1)], ALU.mult).then_inc(S("g.h"), 1)
                vector_back(v, "g.back", X, X, "g.done")
            if stop > 5:
                vector_norm(v, "n2f")
                for n in range(8):
                    v.wait_ge(S("spk.relu"), n + 1)
                    v.scalar_tensor_tensor(out=BIG[:, n // 2, half(n % 2)], in0=bank(n % 4), scalar=0.0,
                                           in1=PR[:, n % 4, :], op0=ALU.max, op1=ALU.mult
                                           ).then_inc(S("spk.h"), 1)
                v.wait_ge(S("spk.back"), 2)
                y = bank(4, 2)
                link(v.tensor_copy(T0[:, :], y))
                link(v.tensor_scalar(T1[:, :], T0[:, :], 1.0, None, ALU.is_gt))
                link(v.tensor_copy(T2[:, :], T1[:, :]))
                for _ in range(4):
                    link(v.scalar_tensor_tensor(out=T0[:, :], in0=T0[:, :], scalar=0.9, in1=y,
                                                op0=ALU.mult, op1=ALU.add))
                    link(v.tensor_tensor(T0[:, :], T0[:, :], T1[:, :], ALU.subtract))
                    link(v.tensor_scalar(T1[:, :], T0[:, :], 1.0, None, ALU.is_gt))
                    link(v.tensor_tensor(T2[:, :], T2[:, :], T1[:, :], ALU.add))
                link(v.scalar_tensor_tensor(out=flat(X), in0=T2[:, :], scalar=0.2, in1=flat(X),
                                            op0=ALU.mult, op1=ALU.add))
            if stop > 6:
                v.wait_ge(ONCE["wall_L3"], 16)
                vector_norm(v, "n3")
                vector_qk(v, "f", link)
                vector_softmax(v, "f", link)
                vector_gather(v, "f", link)
                vector_back(v, "f.back", X, X, "f.done")
            if stop > 7:
                vector_norm(v, "n3f")
                vector_route(v, "L3", link)
                vector_experts(v, "L3", link)
                for hf in range(2):
                    link(v.tensor_copy(T0[:, half(hf)], bank(6 - hf)))
                y = tok(T0)
                for t in range(NT):
                    v.bn_stats(stats[:, t, :], y[:, t, :]).then_inc(S("y_stats"), 1)
                v.wait_ge(S("y_stats"), NT)
                for t in range(NT):
                    v.bn_aggr(moments[:, t, :], stats[:, t, :]).then_inc(S("y_moments"), 1)
                v.wait_ge(S("y_rstd"), 1)
                for t in range(NT):
                    last = v.tensor_scalar(y[:, t, :], y[:, t, :], moments[:, t, 0:1], small[:, 1, t:t + 1],
                                           ALU.subtract, ALU.mult)
                    last.then_inc(S("y_normed"), 1)
                v.wait_ge(S("y_normed"), NT)
                link(v.tensor_tensor(y, y, w("L3", "ln_g3").unsqueeze(1).to_broadcast([P, NT, D]), ALU.mult))
                link(v.tensor_tensor(y, y, w("L3", "ln_b3").unsqueeze(1).to_broadcast([P, NT, D]), ALU.add))
                link(v.tensor_tensor(flat(X), flat(X), T0[:, :], ALU.add))
            v.memset(vec[:, 3:4], 0.0).then_inc(S("x_final"), 1)

        @block.tensor
        def _(pe):
            if stop > 4:
                tensor_norm(pe, "n2")
                pe.wait_ge(S("n2_in"), 2)
                for i, m in enumerate(("Wi", "Wf", "Wz", "Wo")):
                    for b in range(B):
                        last = pe.matmul(PS[64 * b:64 * b + 64, i, :], w("L2", m), NTT[:, half(b)],
                                         start=True, stop=True, tile_position=(0, 64 * b))
                    last.then_inc(S("g.proj"), 1)
                pe.wait_ge(S("g.h"), 1)
                tensor_back(pe, "g.back", "bp", lambda k, t: OT[64 * (t // TPB):64 * (t // TPB) + 64, tile(t % TPB)],
                            lambda k, t: w("L2", "Wp")[64 * (t // TPB):64 * (t // TPB) + 64, :])
            if stop > 5:
                tensor_norm(pe, "n2f")
                pe.wait_ge(S("n2f_in"), 2)
                for n in range(8):
                    m, hf = divmod(n, 2)
                    if n >= 4:
                        pe.wait_ge(S("spk.h"), n - 3)
                    pe.matmul(bank(n % 4), w("L2", "W_fc", P * m, P * (m + 1)), AT[:, half(hf)],
                              start=True, stop=True).then_inc(S("spk.up"), 1)
                pe.wait_ge(S("spk.h"), 8)
                tensor_back(pe, "spk.back", None, lambda k, t: BIG[:, k, tile(t)],
                            lambda k, t: w("L2", "W_proj", P * k, P * (k + 1)), depth=4)
            if stop > 6:
                tensor_norm(pe, "n3")
                tensor_qkv(pe, "f")
                tensor_softmax(pe, "f")
                tensor_gather(pe, "f")
                tensor_back(pe, "f.back", "bo3", lambda k, t: OT[:, tile(t)], lambda k, t: w("L3", "wo"),
                            ready=lambda hf: pe.wait_ge(S("f.ot"), hf + 1))
            if stop > 7:
                tensor_norm(pe, "n3f")
                tensor_experts(pe, "L3")

        end_phase()


class Link:

    def __init__(self, eng, sem):
        self.eng, self.sem, self.n = eng, sem, 0

    def __call__(self, instruction):
        self.n += 1
        instruction.then_inc(self.sem, 1)
        self.eng.wait_ge(self.sem, self.n)


STOP = 99


def kernel(**inputs):
    import concourse.bacc as _bacc
    from concourse.bass_utils import run_bass_kernel_spmd as _run

    nc = _bacc.Bacc("TRN2", target_bir_lowering=False, num_devices=1)
    arrays, at = lay_out(inputs)
    T = {n: nc.dram_tensor("in_" + n, a.shape, mybir.dt.from_np(a.dtype), kind="ExternalInput").ap()
         for n, a in arrays.items()}
    T = {n: ap.bitcast(BF16) if arrays[n].dtype == np.uint16 else ap for n, ap in T.items()}
    T["out"] = nc.dram_tensor("out", (PASSES * P, NT * D), F32, kind="ExternalOutput").ap()
    program(nc, T, at, {n: a.shape for n, a in arrays.items()}, STOP)
    r = _run(nc, [{"in_" + n: a for n, a in arrays.items()}], core_ids=[0])
    out = np.asarray(r.results[0]["out"])
    return np.ascontiguousarray(out.reshape(PASSES, P, NT, D).transpose(0, 2, 1, 3).reshape(PASSES * B, L, D))
```

```python
from contextlib import ExitStack

import numpy as np
import concourse.bass as bass
from concourse import mybir

F32 = mybir.dt.float32
BF16 = mybir.dt.bfloat16
ALU = mybir.AluOpType
ACT = mybir.ActivationFunctionType
AX = mybir.AxisListType

P = 128
B, L, D, H = 2, 512, 128, 16
E = D // H
NT = B * L // P
TPB = L // P
TOK = B * L
PASSES = 2
HALF = 512
VW = 32
PICK = 4 * E + 4
GROUPS = H // 4
SCALE = float(E) ** -0.5
NEG = -1e30
EPS = 1e-5
SPIKE_STEPS = 5

Q_PARTS = (0, 0, 1, 1, 0, 2)
K_PARTS = (0, 1, 0, 1, 2, 0)
STACK = 96
M_ROW = 96

MOE = {"L0": dict(blocks=14, experts=8, table=9, topk=2, glu=True),
       "L1": dict(blocks=9, experts=16, table=17, topk=4, glu=True),
       "L3": dict(blocks=34, experts=8, table=9, topk=2, glu=False)}
PER_EXPERT = 4

HEAD_ORDER = np.array([h * E + e for e in range(E) for h in range(H)])


class Wall:

    def __init__(self):
        self.at, self.parts, self.n = {}, [], 0

    def put(self, name, array):
        array = np.asarray(array)
        if array.ndim == 1:
            array = array[:, None]
        self.at[name] = (self.n, array.shape[1], array.shape[0])
        self.parts.append(array)
        self.n += array.shape[1]

    def array(self, rows, dtype):
        out = np.zeros((rows, self.n), dtype)
        for (at, n, r), a in zip(self.at.values(), self.parts):
            out[:r, at:at + n] = a
        return out


def columns(n_rows, x):
    return np.asarray(x).reshape(-1, n_rows).T


def bf16_bits(constant):
    return (np.ascontiguousarray(constant).view(np.uint32) >> 16).astype(np.uint16)


def constants():
    f = Wall()
    f.put("ident", np.eye(P, dtype=np.float32))
    r, c = np.arange(P)[:, None], np.arange(P)[None, :]
    f.put("causal", (r <= c).astype(np.float32))
    block = np.zeros((P, H, VW), np.float32)
    for row in range(P):
        block[row, row % H, :] = 1.0
    f.put("block", block.reshape(P, H * VW))
    pick = np.zeros((P, PICK), np.float32)
    for j in range(4):
        for e in range(E):
            pick[32 * j + e, j * E + e] = 1.0
        pick[32 * j + E, 4 * E + j] = 1.0
    f.put("pick", pick)
    f.put("ones", np.full((P, 1), 1.0 / P, np.float32))
    below = (np.arange(4)[None, :] < np.arange(4)[:, None]).astype(np.float32)
    f.put("before4", np.broadcast_to(below.reshape(1, 16), (P, 16)))
    for n in (8, 16):
        f.put(f"keep{n}", np.broadcast_to((np.arange(NT * n) % n > 0).astype(np.float32)[None], (P, NT * n)))
    b = Wall()
    b.put("ident", np.eye(P))
    q, k = r, c
    previous = np.where(k > q, 0.0, NEG)
    current = np.where(k <= q, 0.0, NEG)
    nothing = np.full((P, P), NEG)
    b.put("mask_q", np.tile(np.concatenate([previous, current], 1), 2))
    b.put("mask_q0", np.tile(np.concatenate([nothing, current], 1), 2))
    b.put("mask_k", np.tile(np.concatenate([previous.T, current.T], 1), 2))
    b.put("mask_k0", np.tile(np.concatenate([nothing, current.T], 1), 2))
    return f.array(P, np.float32), f.at, bf16_bits(b.array(P, np.float32)), b.at


def expanders():
    out = {}
    for name in ("L0", "L1"):
        m = MOE[name]
        t = m["table"]
        if name == "L0":
            owner = np.concatenate([np.repeat(np.arange(8), 176), np.full(352, 8), np.full(32, -1)])
        else:
            owner = np.concatenate([np.repeat(np.arange(16), 64), np.full(128, 16)])
        hot = (np.arange(t)[:, None] == owner[None, :])
        hot = np.concatenate([hot] * 3, 0).reshape(3 * t, m["blocks"], P)
        out[name] = bf16_bits(hot.transpose(1, 0, 2).reshape(m["blocks"] * 3 * t, P).astype(np.float32))
    return out


def lay_out(x):
    g = {k: np.asarray(v) for k, v in x.items()}
    w = {n: Wall() for n in ("L0", "L1", "L2", "L3")}
    rows = Wall()
    ho = HEAD_ORDER

    def qkv(wall, tag, wm, bv):
        wall.put(tag + "_wq", wm[:, 0:D][:, ho])
        wall.put(tag + "_wk", wm[:, D:2 * D][:, ho])
        wall.put(tag + "_wv", wm[:, 2 * D:])
        wall.put(tag + "_bq", bv[0:D][ho])
        wall.put(tag + "_bk", bv[D:2 * D][ho])
        rows.put(tag + "_bv", bv[2 * D:][None])

    a = w["L0"]
    qkv(a, "a", g["L0_attn_Wqkv_a"], g["L0_attn_bqkv_a"])
    qkv(a, "s", g["L0_attn_Wqkv_s"], g["L0_attn_bqkv_s"])
    for n in ("g1", "b1", "gm", "bm", "bp_a", "bo_s"):
        a.put(n, g["L0_attn_" + n])
    a.put("b1m", columns(P, g["L0_attn_b1m"]))
    a.put("Wp_a", g["L0_attn_Wp_a"])
    a.put("Wo_s", g["L0_attn_Wo_s"])
    a.put("Wo", g["L0_attn_Wo"])
    a.put("W1", g["L0_attn_W1"])
    a.put("W2", g["L0_attn_W2"].reshape(4, P, D).transpose(1, 0, 2).reshape(P, 4 * D))
    a.put("router0", np.concatenate([g["L0_ffn_gate_w"], g["L0_ffn_shared_expert_gate_w"]], 0).T)
    rows.put("bo", g["L0_attn_bo"][None])
    rows.put("b2m", g["L0_attn_b2m"][None])

    a = w["L1"]
    qkv(a, "l", g["L1_attn_qkv_w"].T, g["L1_attn_qkv_b"])
    a.put("gate_w", g["L1_attn_gate_w"].T[:, ho])
    a.put("gate_b", g["L1_attn_gate_b"][ho])
    a.put("ln_g", g["L1_attn_ln_g"])
    a.put("ln_b", g["L1_attn_ln_b"])
    a.put("proj_w", g["L1_attn_proj_w"].T)
    a.put("router1", g["L1_ffn_gate_w"].T)
    a.put("router1_b", np.broadcast_to(g["L1_ffn_gate_bias"][None], (P, 16)))
    rows.put("proj_b", g["L1_attn_proj_b"][None])

    a = w["L2"]
    for n in ("Wi", "Wf", "Wz", "Wo"):
        a.put(n, g["L2_attn_" + n].T)
    for n in ("bi", "bf", "bz", "bo"):
        a.put(n, np.tile(g["L2_attn_" + n], 2))
    a.put("Wp", np.tile(g["L2_attn_Wp"].T, (2, 1)))
    a.put("ln_w", g["L2_attn_ln_w"])
    a.put("ln_b", g["L2_attn_ln_b"])
    a.put("W_fc", g["L2_ffn_W_fc"].T)
    a.put("W_proj", g["L2_ffn_W_proj"].T.reshape(4, P, D).transpose(1, 0, 2).reshape(P, 4 * D))
    rows.put("bp", g["L2_attn_bp"][None])

    a = w["L3"]
    a.put("f_wq", g["L3_attn_wq"][:, ho])
    a.put("f_wk", g["L3_attn_wk"][:, ho])
    a.put("f_wv", g["L3_attn_wv"])
    a.put("f_bq", g["L3_attn_bq"][ho])
    a.put("f_bk", g["L3_attn_bk"][ho])
    a.put("wo", g["L3_attn_wo"])
    a.put("router3", g["L3_ffn_router_w"])
    a.put("router3_b", np.broadcast_to(g["L3_ffn_router_b"][None], (P, 8)))
    a.put("gate", np.concatenate([columns(P, g["L3_ffn_gate"].reshape(-1)), columns(P, g["L3_ffn_sgate"])], 1))
    a.put("b1", np.concatenate([columns(P, g["L3_ffn_b1"].reshape(-1)), columns(P, g["L3_ffn_sb1"])], 1))
    a.put("b2", np.concatenate([g["L3_ffn_b2"], g["L3_ffn_sb2"][None]], 0))
    a.put("shared_w", np.broadcast_to(g["L3_ffn_shared_weight"].reshape(1, 1), (P, 1)))
    a.put("ln_g3", np.broadcast_to(g["L3_ffn_ln_g"][None], (P, D)))
    a.put("ln_b3", np.broadcast_to(g["L3_ffn_ln_b"][None], (P, D)))
    rows.put("f_bv", g["L3_attn_bv"][None])
    rows.put("bo3", g["L3_attn_bo"][None])
    rows.put("ones", np.ones((1, P), np.float32))

    def blocks_in(m):
        return m.reshape(P, -1, P).transpose(1, 0, 2)

    def padded(m, n):
        out = np.zeros((m.shape[0], n), m.dtype)
        out[:, :m.shape[1]] = m
        return out

    streams = {}
    n0 = MOE["L0"]["blocks"] * P
    gu = g["L0_ffn_experts_gate_up"]
    gate = padded(np.concatenate([gu[:, :176].reshape(-1, D), g["L0_ffn_shared_gate_w"]], 0).T, n0)
    up = padded(np.concatenate([gu[:, 176:].reshape(-1, D), g["L0_ffn_shared_up_w"]], 0).T, n0)
    down = padded(np.concatenate([g["L0_ffn_experts_down"].transpose(1, 0, 2).reshape(D, -1),
                                  g["L0_ffn_shared_down_w"]], 1), n0)
    streams["L0"] = (np.concatenate([blocks_in(gate), blocks_in(up)], 2).reshape(-1, 2 * P), down.T)
    gate = np.concatenate([g["L1_ffn_Wg"].reshape(-1, D), g["L1_ffn_Ws_g"]], 0).T
    up = np.concatenate([g["L1_ffn_Wu"].reshape(-1, D), g["L1_ffn_Ws_u"]], 0).T
    down = np.concatenate([g["L1_ffn_Wd"].transpose(1, 0, 2).reshape(D, -1), g["L1_ffn_Ws_d"]], 1)
    streams["L1"] = (np.concatenate([blocks_in(gate), blocks_in(up)], 2).reshape(-1, 2 * P), down.T)
    w1 = np.concatenate([g["L3_ffn_w1"].transpose(1, 0, 2).reshape(D, -1), g["L3_ffn_sw1"]], 1)
    w2 = np.concatenate([g["L3_ffn_w2"].reshape(-1, D), g["L3_ffn_sw2"]], 0)
    streams["L3"] = (blocks_in(w1).reshape(-1, P), w2)

    arrays = {"x": g["L0_attn_x"].reshape(PASSES, NT, P, D).transpose(0, 2, 1, 3).reshape(PASSES * P, NT * D)}
    at = {}
    for n, wall in w.items():
        arrays["w" + n] = wall.array(P, np.float32)
        at[n] = wall.at
    arrays["rows"] = rows.array(1, np.float32)
    at["rows"] = rows.at
    arrays["cf"], at["cf"], arrays["cb"], at["cb"] = constants()
    arrays["ones_rows"] = bf16_bits(np.ones((3, H * TOK), np.float32))
    for n, stream in streams.items():
        arrays["in" + n], arrays["down" + n] = stream
    for n, hot in expanders().items():
        arrays["hot" + n] = hot
    return {k: np.ascontiguousarray(v) for k, v in arrays.items()}, at


def unit_loop(eng, n, body):
    for u in range(4):
        body(u, u)
    last = (n - 1) // 4
    with eng.Fori(1, last) as i:
        for q in range(4):
            body(i * 4 + q, q)
    for u in range(4 * last, n):
        body(u, u % 4)


def program(nc, T, at, shapes, stop=99):
    with ExitStack() as ctx, ExitStack() as ctx_loop:
        def sb(name, shape, dt=F32):
            return ctx.enter_context(nc.sbuf_tensor(name, shape, dt))

        sems = {}

        def S(name):
            if name not in sems:
                sems[name] = phase["sems"].enter_context(nc.semaphore(name.replace(".", "_")))
            return sems[name]

        ONCE = {n: ctx.enter_context(nc.semaphore(n)) for n in
                ("rows_in", "cf_in", "cb_in", "ones_in", "wall_L0", "wall_L1", "wall_L2", "wall_L3",
                 "zero_in", "v_ready", "half_ready", "stack_zero", "q_zero")}

        PS = ctx.enter_context(nc.psum_tensor("PS", [P, 8, 512], F32))
        X = sb("X", [P, NT, D])
        A = sb("A", [P, NT, D])
        A2 = sb("A2", [P, NT, D])
        AT = sb("AT", [P, TOK])
        NTT = sb("NTT", [P, TOK])
        T0 = sb("T0", [P, TOK])
        T1 = sb("T1", [P, TOK])
        T2 = sb("T2", [P, TOK])
        T3 = sb("T3", [P, TOK])
        OT = sb("OT", [P, TOK])
        QS = sb("QS", [P, H, TOK], BF16)
        KS = sb("KS", [P, H, TOK], BF16)
        V = sb("V", [P, NT, H, VW])
        BIG = sb("BIG", [P, GROUPS, TOK])
        PR = sb("PR", [P, 8, 512])
        SM = PR[:, 4:6, :]
        WALL = {n: sb("wall_" + n, [P, shapes["w" + n][1]]) for n in ("L0", "L1", "L2", "L3")}
        CF = sb("CF", [P, shapes["cf"][1]])
        CB = sb("CB", [P, shapes["cb"][1]], BF16)
        ROWS = sb("ROWS", [1, shapes["rows"][1]])
        GU = sb("GU", [P, 2, 2 * P])
        DN = sb("DN", [P, 2, P])
        HOT = sb("HOT", [51, 2, P], BF16)
        CT = sb("CT", [51, TOK], BF16)
        C32 = sb("C32", [17, TOK])
        GM = sb("GM", [P, NT])
        DEN = sb("DEN", [P, 2, 64])
        stats = sb("stats", [P, NT, 6])
        moments = sb("moments", [P, NT, 2])
        small = sb("small", [P, 8, NT])
        MX = sb("MX", [P, 2, 16])
        MXR = sb("MXR", [P, 2, 16])
        MP = sb("MP", [P, 2, 4, 3, 4], BF16)
        MR = sb("MR", [48, 512], BF16)
        CW = sb("CW", [P, NT, 17])
        CWR = sb("CWR", [P, NT, 17])
        CP = sb("CP", [P, NT, 3, 17], BF16)
        b1g = sb("b1g", [P, 34, 2])
        GB = sb("GB", [P, PER_EXPERT, 2])
        CE = sb("CE", [P, NT])
        zero = sb("zero", [1, 512], BF16)
        vec = sb("vec", [P, 4])

        def parts_of(which, i):
            n = 3 * which + i
            return BIG[:, n // 2, :].bitcast(BF16)[:, (n % 2) * TOK:(n % 2 + 1) * TOK]

        def w(layer, name, a=0, b=None):
            o, n, r = at[layer][name]
            return WALL[layer][0:r, o + a:o + (n if b is None else b)]

        def cf(name, a=0, b=None):
            o, n, r = at["cf"][name]
            return CF[:, o + a:o + (n if b is None else b)]

        def cb(name):
            o, n, r = at["cb"][name]
            return CB[:, o:o + n]

        def row(name):
            o, n, r = at["rows"][name]
            return ROWS[0:1, o:o + n]

        def row4(name):
            return row(name).unsqueeze(1).to_broadcast([1, 4, P])

        def half(h):
            return slice(HALF * h, HALF * (h + 1))

        def tile(t):
            return slice(P * t, P * (t + 1))

        def bank(i, n=1):
            return PS[:, i, :] if n == 1 else PS[:, i:i + n, :].rearrange("p a b -> p (a b)")

        def tok(buf):
            return buf[:, :].rearrange("p (t d) -> p t d", t=NT)

        def flat(buf):
            return buf[:, :, :].rearrange("p t d -> p (t d)")

        with nc.Block() as once:
            @once.sync
            def _(sp):
                sp.dma_start(WALL["L0"][:, :], T["wL0"]).then_inc(ONCE["wall_L0"], 16)
                sp.dma_start(ROWS[:, :], T["rows"]).then_inc(ONCE["rows_in"], 16)
                sp.dma_start(CF[:, :], T["cf"]).then_inc(ONCE["cf_in"], 16)
                sp.dma_start(CB[:, :], T["cb"]).then_inc(ONCE["cb_in"], 16)
                for n in ("L1", "L2", "L3"):
                    sp.dma_start(WALL[n][:, :], T["w" + n]).then_inc(ONCE["wall_" + n], 16)
                sp.wait_ge(ONCE["stack_zero"], 1)
                sp.dma_start(KS[M_ROW:M_ROW + 3, :, :].rearrange("p h t -> p (h t)"), T["ones_rows"]
                             ).then_inc(ONCE["ones_in"], 16)

            @once.vector
            def _(v):
                v.memset(QS[:, :, :].rearrange("p h t -> p (h t)").bitcast(F32), 0.0).then_inc(ONCE["q_zero"], 1)

            @once.gpsimd
            def _(g):
                g.memset(KS[:, :, :].rearrange("p h t -> p (h t)").bitcast(F32), 0.0).then_inc(ONCE["stack_zero"], 1)
                g.memset(small[:, 7, :], -0.5).then_inc(ONCE["half_ready"], 1)
                g.memset(zero[:, :], 0.0).then_inc(ONCE["zero_in"], 1)
                g.memset(V[:, :, :, :], 0.0).then_inc(ONCE["v_ready"], 1)
                g.wait_ge(ONCE["v_ready"], 1)
                g.memset(V[:, :, :, E], 1.0).then_inc(ONCE["v_ready"], 1)

        NORMS = {
            "n0": (X, True, [(A2, NTT, (w("L0", "g1"), w("L0", "b1")))]),
            "n0m": (tok(T0), False, [(tok(T1), T2, (w("L0", "gm"), w("L0", "bm")))]),
            "n0f": (X, False, [(A, AT, None)]),
            "n1": (X, True, [(A, AT, None), (A2, NTT, (w("L1", "ln_g"), w("L1", "ln_b")))]),
            "n1f": (X, False, [(A, AT, None)]),
            "n2": (X, True, [(A2, NTT, (w("L2", "ln_w"), w("L2", "ln_b")))]),
            "n2f": (X, False, [(A, AT, None)]),
            "n3": (X, False, [(A, NTT, None)]),
            "n3f": (X, False, [(A, AT, None)]),
        }

        PHASE_1 = ("n0", "n0m", "n0f", "n1", "n1f")
        NORM_AT = {k: i if i < len(PHASE_1) else i - len(PHASE_1) for i, k in enumerate(NORMS)}

        TURNED_AT = {k: 2 * sum(len(NORMS[j][2]) for j in NORMS if NORM_AT[j] < NORM_AT[k] and
                                (j in PHASE_1) == (k in PHASE_1)) for k in NORMS}

        def wait_norm(eng, k, n):
            eng.wait_ge(S("norm_in"), TURNED_AT[k] + n)

        def vector_norm(v, k, before=None):
            src, second, turns = NORMS[k]
            for hf in range(2):
                if before:
                    before(hf)
                for t in range(TPB * hf, TPB * (hf + 1)):
                    v.bn_stats(stats[:, t, :], src[:, t, :]).then_inc(S("norm_stats"), 1)
                v.wait_ge(S("norm_stats"), NT * NORM_AT[k] + TPB * (hf + 1))
                for t in range(TPB * hf, TPB * (hf + 1)):
                    v.bn_aggr(moments[:, t, :], stats[:, t, :]).then_inc(S("norm_moments"), 1)

            def normed(dst, rstd, signal):
                for t in range(NT):
                    if t % TPB == 0:
                        v.wait_ge(S("norm_rstd"), 2 * NORM_AT[k] + t // TPB + 1)
                    v.tensor_scalar(dst[:, t, :], src[:, t, :], moments[:, t, 0:1], small[:, rstd, t:t + 1],
                                    ALU.subtract, ALU.mult).then_inc(S(k + signal), 1)
            if k == "n0":
                normed(A2, 5, "_second")
                normed(A, 1, "_first")
            else:
                if not second or len(turns) == 2:
                    normed(tok(T1) if k == "n0m" else A, 1, "_first")
                if second:
                    normed(A2, 5, "_second")

        def gpsimd_norm(g, k, chain):
            first = not NORMS[k][1] or k != "n2"
            for hf in range(2):
                ts = slice(TPB * hf, TPB * (hf + 1))
                g.wait_ge(S("norm_moments"), NT * NORM_AT[k] + TPB * (hf + 1))
                var = moments[:, ts, 1]
                if first:
                    chain(g.tensor_scalar(small[:, 0, ts], var, EPS, None, ALU.add))
                if NORMS[k][1]:
                    chain(g.tensor_scalar(small[:, 4, ts], var, 1.0 + EPS, EPS * EPS, ALU.mult, ALU.add))
                if first:
                    last = g.tensor_tensor(small[:, 1, ts], small[:, 0, ts], small[:, 7, ts], ALU.pow)
                if NORMS[k][1]:
                    last = g.tensor_tensor(small[:, 5, ts], small[:, 4, ts], small[:, 7, ts], ALU.pow)
                last.then_inc(S("norm_rstd"), 1)

        def tensor_norm(pe, k):
            for s, (src, _, affine) in enumerate(NORMS[k][2]):
                for hf in range(2):
                    pe.wait_ge(S(k + ("_second" if src is A2 else "_first")), TPB * (hf + 1))
                    for t in range(TPB):
                        last = pe.transpose(PS[:, 2 * s + hf, tile(t)], src[:, TPB * hf + t, :], cf("ident"))
                    last.then_inc(S("norm_turned"), 1)

        def scalar_norm(act, k):
            for s, (_, dst, affine) in enumerate(NORMS[k][2]):
                for hf in range(2):
                    act.wait_ge(S("norm_turned"), TURNED_AT[k] + 2 * s + hf + 1)
                    if affine is None:
                        i = act.activation(dst[:, half(hf)], bank(2 * s + hf), ACT.Copy)
                    else:
                        i = act.activation(dst[:, half(hf)], bank(2 * s + hf), ACT.Identity,
                                           bias=affine[1], scale=affine[0])
                    i.then_inc(S("norm_in"), 1)

        LAYER = {"a": "L0", "s": "L0", "l": "L1", "f": "L3"}
        FROM = {"a": "n0", "s": "n0", "l": "n1", "f": "n3"}
        LINEAR = {"s": (SCALE, 1.0, 1e-4, 1e-6), "l": (None, None, 0.0, 1e-5)}

        def tensor_qkv(pe, a):
            lay = LAYER[a]
            pe.wait_ge(ONCE["wall_" + lay], 16)
            if a == "a":
                pe.wait_ge(ONCE["rows_in"], 16)
            if a == "s":
                pe.wait_ge(S("a.ot"), 2)
            if a == "l":
                for hf in range(2):
                    wait_norm(pe, "n1", hf + 1)
                    pe.matmul(bank(4 + hf), w(lay, "gate_w"), AT[:, half(hf)], start=True, stop=True
                              ).then_inc(S("l.gate"), 1)

            def heads(hf):
                wait_norm(pe, FROM[a], hf + (3 if a == "l" else 1))
                for i, m in enumerate(("_wq", "_wk")):
                    pe.matmul(bank(2 * i + hf), w(lay, a + m), NTT[:, half(hf)], start=True, stop=True
                              ).then_inc(S(a + ".qk"), 1)

            def gate_mean(hf):
                pe.wait_ge(S("l.gate_sig"), hf + 1)
                for t in range(TPB):
                    last = pe.matmul(PS[:, 6 + hf, t:t + 1], T2[:, tile(TPB * hf + t)], cf("ones"),
                                     start=(t == 0), stop=True, skip_group_check=True)
                last.then_inc(S("l.gate_mean"), 1)

            def gate_row(hf):
                pe.wait_ge(S("l.gate_inverse"), hf + 1)
                for t in range(TPB):
                    last = pe.transpose(PS[:, 6 + hf, tile(t)], GM[:, TPB * hf + t:TPB * hf + t + 1]
                                        .to_broadcast([P, P]), cf("ident"))
                last.then_inc(S("l.gate_row"), 1)

            def values_of(hf):
                pe.matmul(bank(4 + hf), row("ones"), row4(a + "_bv"), start=True, stop=True, skip_group_check=True)
                for t in range(TPB):
                    last = pe.matmul(PS[:, 4 + hf, tile(t)], NTT[:, tile(TPB * hf + t)], w(lay, a + "_wv"),
                                     start=False, stop=True, skip_group_check=True)
                last.then_inc(S(a + ".v"), 1)

            if a == "l":
                heads(0)
                gate_mean(0)
                heads(1)
                gate_mean(1)
                gate_row(0)
                values_of(0)
                gate_row(1)
                values_of(1)
            else:
                for hf in range(2):
                    heads(hf)
                    values_of(hf)

        def vector_v(v, a, hf):
            v.wait_ge(S(a + ".v"), hf + 1)
            if a == "a":
                v.wait_ge(ONCE["v_ready"], 2)
            v.tensor_copy(V[:, TPB * hf:TPB * (hf + 1), :, 0:E],
                          bank(4 + hf).rearrange("p (t h e) -> p t h e", t=TPB, h=H)
                          ).then_inc(S(a + ".v_in"), 1)

        def scalar_qk(act, a):
            lay = LAYER[a]
            if a == "l":
                for hf in range(2):
                    act.wait_ge(S("l.gate"), hf + 1)
                    act.activation(T2[:, half(hf)], bank(4 + hf), ACT.Sigmoid, bias=w("L1", "gate_b")
                                   ).then_inc(S("l.gate_sig"), 1)
            for hf in range(2):
                for i, dst in enumerate((T0, T1)):
                    n, dst, e, src = 2 * hf + i, dst[:, half(hf)], (T2, T3)[i][:, half(hf)], bank(2 * i + hf)
                    bias = w(lay, a + ("_bq", "_bk")[i])
                    if a == "l":
                        act.wait_ge(S("l.z"), n + 1)
                        act.activation(e, dst, ACT.Exp).then_inc(S("l.e"), 1)
                        act.wait_ge(S("l.e"), n + 1)
                        act.activation(dst, dst, ACT.Relu).then_inc(S("l.relu"), 1)
                    elif a == "s":
                        act.wait_ge(S("s.qk"), n + 1)
                        if i == 0:
                            act.wait_ge(S("s.bias"), 1)
                            bias = vec[:, 2:3]
                        act.activation(e, src, ACT.Exp, bias=bias, scale=SCALE if i == 0 else 1.0
                                       ).then_inc(S("s.e"), 1)
                        act.activation(dst, src, ACT.Relu, bias=bias, scale=SCALE if i == 0 else 1.0
                                       ).then_inc(S("s.relu"), 1)
                    else:
                        act.wait_ge(S(a + ".qk"), n + 1)
                        act.activation(dst, src, ACT.Identity, bias=bias).then_inc(S(a + ".f"), 1)
                        act.activation(parts_of(i, 0)[:, half(hf)], src, ACT.Identity, bias=bias
                                       ).then_inc(S(a + ".p0"), 1)
                if a in LINEAR:
                    for i, dst in enumerate((T0, T1)):
                        act.wait_ge(S(a + ".f"), 2 * hf + i + 1)
                        act.activation(parts_of(i, 0)[:, half(hf)], dst[:, half(hf)], ACT.Copy
                                       ).then_inc(S(a + ".p0"), 1)
                for i in range(2):
                    act.wait_ge(S(a + ".r"), 2 * hf + i + 1)
                    act.activation(parts_of(i, 1)[:, half(hf)], (T2, T3)[i][:, half(hf)], ACT.Copy
                                   ).then_inc(S(a + ".p1"), 1)

        def vector_qk(v, a, link):
            lay = LAYER[a]
            if a == "s":
                v.tensor_scalar(vec[:, 2:3], w("L0", "s_bq"), SCALE, None, ALU.mult).then_inc(S("s.bias"), 1)
            for hf in range(2):
                hs, ts = half(hf), slice(TPB * hf, TPB * (hf + 1))
                if a == "l":
                    v.wait_ge(S("l.gate_mean"), hf + 1)
                    link(v.tensor_scalar(GM[:, ts], PS[:, 6 + hf, 0:TPB], EPS, None, ALU.add))
                    v.reciprocal(GM[:, ts], GM[:, ts]).then_inc(S("l.gate_inverse"), 1)
                    v.wait_ge(S("l.gate_row"), hf + 1)
                    link(v.tensor_tensor(T3[:, hs], bank(6 + hf), T2[:, hs], ALU.mult))
                    for i, (dst, bias) in enumerate(((T0, "_bq"), (T1, "_bk"))):
                        v.wait_ge(S("l.qk"), 2 * hf + i + 1)
                        v.scalar_tensor_tensor(out=dst[:, hs], in0=bank(2 * i + hf), scalar=w(lay, a + bias),
                                               in1=T3[:, hs], op0=ALU.add, op1=ALU.mult).then_inc(S("l.z"), 1)
                if a in LINEAR:
                    for i, dst in enumerate((T0, T1)):
                        e = (T2, T3)[i][:, hs]
                        if a == "s":
                            v.wait_ge(S("s.e"), 2 * hf + i + 1)
                            link(v.tensor_scalar(e, e, 1.0, LINEAR[a][2], ALU.min, ALU.add))
                        v.wait_ge(S(a + ".relu"), 2 * hf + i + 1)
                        v.scalar_tensor_tensor(out=dst[:, hs], in0=e, scalar=1.0 + LINEAR[a][2], in1=dst[:, hs],
                                               op0=ALU.min, op1=ALU.add).then_inc(S(a + ".f"), 1)
                    v.wait_ge(S(a + ".f"), 2 * hf + 2)
                for i, (src, left) in enumerate(((T0, T2), (T1, T3))):
                    v.wait_ge(S(a + ".p0"), 2 * hf + i + 1)
                    v.tensor_tensor(left[:, hs], src[:, hs], parts_of(i, 0)[:, hs], ALU.subtract
                                    ).then_inc(S(a + ".r"), 1)
                vector_v(v, a, hf)
                for i, left in enumerate((T2, T3)):
                    v.wait_ge(S(a + ".p1"), 2 * hf + i + 1)
                    v.tensor_tensor(parts_of(i, 2)[:, hs], left[:, hs], parts_of(i, 1)[:, hs], ALU.subtract
                                    ).then_inc(S(a + ".p2"), 1)

        STACK_DMAS = 16 * (len(Q_PARTS) + len(K_PARTS))

        def sync_stacks(sp, a):
            sp.wait_ge(ONCE["stack_zero"], 1)
            sp.wait_ge(ONCE["q_zero"], 1)
            for hf in range(2):
                for part in range(3):
                    for i, (dst, groups) in enumerate(((QS, Q_PARTS), (KS, K_PARTS))):
                        sp.wait_ge(S(a + f".p{part}"), 2 * hf + i + 1)
                        for g, p in enumerate(groups):
                            if p == part:
                                sp.dma_start(dst[E * g:E * (g + 1), :, half(hf)], parts_of(i, part)[:, half(hf)]
                                             ).then_inc(S(a + f".stacked{hf}"), 16)

        def plan(a):
            u = 8 if a == "a" else 16
            return dict(units=u, per=2 if a == "a" else 4, lead=u + u // 2)

        def score_1(pe, a, n):
            pl = plan(a)
            G, u = divmod(n, pl["units"])
            b = n % 3
            if n >= 3:
                pe.wait_ge(S(a + ".max"), n - 2)
            if a == "a":
                first = G % TPB == 0
                pe.matmul(bank(b), cb("ident"), cb("mask_q0" if first else "mask_q"), start=True, stop=True, skip_group_check=True)
                for j in range(2):
                    h = 2 * u + j
                    lo = 1 if first else 0
                    last = pe.matmul(PS[:, b, 256 * j + 128 * lo:256 * (j + 1)], QS[0:STACK, h, tile(G)],
                                     KS[0:STACK, h, P * (G - 1 + lo):P * (G + 1)], start=False, stop=True,
                                     skip_group_check=True)
            else:
                bt, g = divmod(G, GROUPS)
                qt, j = divmod(u, 4)
                last = pe.matmul(bank(b), QS[0:STACK, 4 * g + j, tile(TPB * bt + qt)],
                                 KS[0:STACK, 4 * g + j, half(bt)], start=True, stop=True)
            last.then_inc(S(a + ".s1"), 1)

        def max_1(v, a, n):
            pl = plan(a)
            G, u = divmod(n, pl["units"])
            v.wait_ge(S(a + ".s1"), n + 1)
            if a == "a":
                v.tensor_reduce(MX[:, G % 2, 2 * u:2 * u + 2], bank(n % 3).rearrange("p (h k) -> p h k", h=2),
                                AX.X, ALU.max, negate=True).then_inc(S(a + ".max"), 1)
            else:
                v.tensor_reduce(MX[:, G % 2, u:u + 1], bank(n % 3), AX.X, ALU.max, negate=True
                                ).then_inc(S(a + ".max"), 1)

        def max_parts(v, a, G, link):
            pl = plan(a)
            v.wait_ge(S(a + ".max"), (G + 1) * pl["units"])
            if G >= 2:
                v.wait_ge(S(a + ".m_turned"), G - 1)
            m, left = MX[:, G % 2, :], MXR[:, G % 2, :]
            if a == "a":
                out = [MP[:, G % 2, :, :, :].rearrange("p a b c -> p (a b c)")[:, 16 * i:16 * (i + 1)]
                       for i in range(3)]
            else:
                m, left = (y.rearrange("p (t h) -> p t h", t=4) for y in (m, left))
                out = [MP[:, G % 2, :, i, :] for i in range(3)]
            link(v.tensor_copy(out[0], m))
            link(v.tensor_tensor(left, m, out[0], ALU.subtract))
            link(v.tensor_copy(out[1], left))
            v.tensor_tensor(out[2], left, out[1], ALU.subtract).then_inc(S(a + ".m_parts"), 1)

        def turn_max(pe, a, G):
            pe.wait_ge(S(a + ".m_parts"), G + 1)
            if G >= 1:
                pe.wait_ge(S(a + ".m_rows"), G)
            out = bank(7).bitcast(BF16)
            mp = MP[:, G % 2, :, :, :].rearrange("p a b c -> p (a b c)")
            if a == "a":
                last = pe.transpose(out[0:48, 0:P], mp, cb("ident"))
            else:
                for t in range(4):
                    last = pe.transpose(out[0:12, tile(t)], mp[:, 12 * t:12 * (t + 1)], cb("ident"))
            last.then_inc(S(a + ".m_turned"), 1)

        def copy_max(act, a, G):
            act.wait_ge(S(a + ".m_turned"), G + 1)
            if G >= 1:
                act.wait_ge(S(a + ".m_in"), 16 * G)
            r, n = (48, P) if a == "a" else (12, 512)
            act.activation(MR[0:r, 0:n], bank(7).bitcast(BF16)[0:r, 0:n], ACT.Copy
                           ).then_inc(S(a + ".m_rows"), 1)

        def sync_max(sp, a):
            for G in range(8):
                sp.wait_ge(S(a + ".m_rows"), G + 1)
                if a == "a":
                    sp.dma_start(QS[M_ROW:M_ROW + 3, :, tile(G)], MR[0:48, 0:P]).then_inc(S(a + ".m_in"), 16)
                else:
                    bt, g = divmod(G, GROUPS)
                    sp.dma_start(QS[M_ROW:M_ROW + 3, 4 * g:4 * g + 4, half(bt)], MR[0:12, :]
                                 ).then_inc(S(a + ".m_in"), 16)

        def score_2(pe, a, n):
            pl = plan(a)
            G, u = divmod(n, pl["units"])
            b = 3 + n % 3
            if u == 0:
                pe.wait_ge(S(a + ".m_in"), 16 * (G + 1))
            if n >= 3:
                pe.wait_ge(S(a + ".exp"), n - 2)
            if a == "a":
                first = G % TPB == 0
                pe.matmul(bank(b), cb("ident"), cb("mask_k0" if first else "mask_k"), start=True, stop=True, skip_group_check=True)
                for j in range(2):
                    h = 2 * u + j
                    for c in range(1 if first else 0, 2):
                        last = pe.matmul(PS[:, b, 256 * j + 128 * c:256 * j + 128 * (c + 1)],
                                         KS[:, h, tile(G - 1 + c)], QS[:, h, tile(G)],
                                         start=False, stop=True, skip_group_check=True)
            else:
                bt, g = divmod(G, GROUPS)
                kt, j = divmod(u, 4)
                last = pe.matmul(bank(b), KS[:, 4 * g + j, tile(TPB * bt + kt)],
                                 QS[:, 4 * g + j, half(bt)], start=True, stop=True)
            last.then_inc(S(a + ".s2"), 1)

        def exp_2(act, a, n):
            pl = plan(a)
            act.wait_ge(S(a + ".s2"), n + 1)
            if n >= 8:
                act.wait_ge(S(a + ".pv"), (n - 8) // pl["per"] + 1)
            act.activation(PR[:, n % 8, :], bank(3 + n % 3), ACT.Exp, scale=SCALE).then_inc(S(a + ".exp"), 1)

        def values(pe, a, i):
            pl = plan(a)
            per = pl["per"]
            G, k = divmod(i, pl["units"] // per)
            pe.wait_ge(S(a + ".exp"), (i + 1) * per)
            if i == 0:
                pe.wait_ge(S(a + ".v_in"), 2)
            if k == 0 and G >= 1:
                pe.wait_ge(S(a + ".out"), G)
            if a == "a":
                first = G % TPB == 0
                for c in range(1 if first else 0, 2):
                    for j in range(4):
                        u = i * per + j // 2
                        last = pe.matmul(PS[32 * j:32 * j + 32, 6, tile(k)], V[:, G - 1 + c, 4 * k + j, :],
                                         PR[:, u % 8, 256 * (j % 2) + 128 * c:256 * (j % 2) + 128 * (c + 1)],
                                         start=(c == 1 if first else c == 0), stop=(c == 1),
                                         tile_position=(0, 32 * j))
            else:
                bt, g = divmod(G, GROUPS)
                for j in range(4):
                    last = pe.matmul(PS[32 * j:32 * j + 32, 6, :], V[:, TPB * bt + k, 4 * g + j, :],
                                     PR[:, (i * per + j) % 8, :], start=(k == 0), stop=(k == 3),
                                     tile_position=(0, 32 * j))
            last.then_inc(S(a + ".pv"), 1)

        def copy_out(act, a, G):
            pl = plan(a)
            act.wait_ge(S(a + ".pv"), (G + 1) * (pl["units"] // pl["per"]))
            if G == 0:
                act.wait_ge(S(a + ".stacked0"), STACK_DMAS)
                act.wait_ge(S(a + ".stacked1"), STACK_DMAS)
            if a == "a":
                i = act.activation(BIG[:, :, tile(G)], bank(6).rearrange("p (g q) -> p g q", g=GROUPS), ACT.Copy)
            else:
                bt, g = divmod(G, GROUPS)
                i = act.activation(BIG[:, g, half(bt)], bank(6), ACT.Copy)
            i.then_inc(S(a + ".out"), 1)

        def steps(a):
            pl = plan(a)
            n, u = 8 * pl["units"], pl["units"]
            for s in range(-pl["lead"], n):
                one = s + pl["lead"]
                turn = one // u - 1 if one % u == 2 and one >= u and one // u <= 8 else None
                yield s, (one if one < n else None), turn

        def tensor_softmax(pe, a):
            pl = plan(a)
            pe.wait_ge(S(a + ".p0"), 4)
            pe.wait_ge(S(a + ".stacked0"), STACK_DMAS)
            pe.wait_ge(ONCE["ones_in"], 16)
            pe.wait_ge(ONCE["cb_in"], 16)
            for s, one, turn in steps(a):
                if one == 4 * pl["units"]:
                    pe.wait_ge(S(a + ".stacked1"), STACK_DMAS)
                if one is not None:
                    score_1(pe, a, one)
                if turn is not None:
                    turn_max(pe, a, turn)
                if s >= 0:
                    score_2(pe, a, s)
                    if s % pl["per"] == pl["per"] - 1 and s >= pl["per"]:
                        values(pe, a, s // pl["per"] - 1)
            values(pe, a, 8 * pl["units"] // pl["per"] - 1)

        def scalar_softmax(act, a):
            pl = plan(a)
            for s, _, turn in steps(a):
                if turn is not None:
                    copy_max(act, a, turn)
                if s >= 0:
                    exp_2(act, a, s)
                    if s % pl["units"] == pl["per"] + 1 and s >= pl["units"]:
                        copy_out(act, a, s // pl["units"] - 1)
            copy_out(act, a, 7)

        def vector_softmax(v, a, link):
            pl = plan(a)
            for n in range(8 * pl["units"]):
                max_1(v, a, n)
                if n % pl["units"] == pl["units"] - 1:
                    max_parts(v, a, n // pl["units"], link)

        def tensor_linear(pe, a):
            pe.wait_ge(S(a + ".v_in"), 2)
            for hf in range(2):
                pe.wait_ge(S(a + ".f"), 2 * hf + 2)
                for t in range(TPB):
                    last = pe.transpose(PS[:, 4 + hf, tile(t)], T1[:, tile(TPB * hf + t)], cf("ident"))
                last.then_inc(S(a + ".k_turned"), 1)
            pe.wait_ge(S(a + ".k_in"), 2)
            pe.wait_ge(S(a + ".stacked0"), STACK_DMAS)

            def products(n, g):
                i = GROUPS * n + g
                if i == GROUPS * TPB:
                    pe.wait_ge(S(a + ".stacked1"), STACK_DMAS)
                if i >= 2:
                    pe.wait_ge(S(a + ".masked"), i - 1)
                for j in range(4):
                    h = 4 * g + j
                    last = pe.matmul(PS[:, i % 2, tile(j)], KS[0:STACK, h, tile(n)], QS[0:STACK, h, tile(n)],
                                     start=True, stop=True)
                last.then_inc(S(a + ".s"), 1)

            def through(n, g):
                i = GROUPS * n + g
                o = 2 + n % 2
                t = n % TPB
                if g == 0 and n >= 2:
                    pe.wait_ge(S(a + ".out"), n - 1)
                if t:
                    if g == 0:
                        pe.wait_ge(S(a + ".state_in"), n - n // TPB)
                    pe.matmul(PS[:, o, tile(g)], SM[:, n % 2, tile(g)], T0[:, tile(n)], start=True, stop=True, skip_group_check=True)
                pe.wait_ge(S(a + ".masked"), i + 1)
                for j in range(4):
                    last = pe.matmul(PS[32 * j:32 * j + 32, o, tile(g)], V[:, n, 4 * g + j, :],
                                     PR[:, i % 4, tile(j)], start=(t == 0), stop=True,
                                     tile_position=(0, 32 * j), skip_group_check=True)
                last.then_inc(S(a + ".pv"), 1)

            def state(n):
                t = n % TPB
                if n // TPB or t:
                    pe.wait_ge(S(a + ".state_in"), n - n // TPB)
                pe.matmul(bank(4), T2[:, tile(n)], V[:, n, :, :].rearrange("p h c -> p (h c)"),
                          start=(t == 0), stop=True, skip_group_check=True
                          ).then_inc(S(a + ".state"), 1)

            products(0, 0)
            for n in range(NT):
                if n % TPB < TPB - 1:
                    state(n)
                for g in range(GROUPS):
                    i = GROUPS * n + g + 1
                    if i < GROUPS * NT:
                        products(*divmod(i, GROUPS))
                    through(n, g)

        def vector_linear(v, a):
            for hf in range(2):
                v.wait_ge(S(a + ".k_turned"), hf + 1)
                if hf == 0:
                    v.wait_ge(S(a + ".p2"), 4)
                v.tensor_copy(T2[:, half(hf)], bank(4 + hf)).then_inc(S(a + ".k_in"), 1)
            mask = cf("causal").unsqueeze(1).to_broadcast([P, 4, P])
            for n in range(NT):
                if n % TPB < TPB - 1:
                    v.wait_ge(S(a + ".state"), n - n // TPB + 1)
                    if n >= 1:
                        v.wait_ge(S(a + ".pv"), GROUPS * n)
                    v.tensor_tensor(SM[:, (n + 1) % 2, :], bank(4), cf("block"), ALU.mult
                                    ).then_inc(S(a + ".state_in"), 1)
                for g in range(GROUPS):
                    i = GROUPS * n + g
                    v.wait_ge(S(a + ".s"), i + 1)
                    if i >= 4:
                        v.wait_ge(S(a + ".pv"), i - 3)
                    v.tensor_tensor(PR[:, i % 4, :].rearrange("p (j q) -> p j q", j=4),
                                    bank(i % 2).rearrange("p (j q) -> p j q", j=4), mask, ALU.mult
                                    ).then_inc(S(a + ".masked"), 1)

        def scalar_linear(act, a):
            act.wait_ge(S(a + ".stacked0"), STACK_DMAS)
            act.wait_ge(S(a + ".stacked1"), STACK_DMAS)
            for n in range(NT):
                act.wait_ge(S(a + ".pv"), GROUPS * (n + 1))
                act.activation(BIG[:, :, tile(n)], bank(2 + n % 2).rearrange("p (g q) -> p g q", g=GROUPS),
                               ACT.Copy).then_inc(S(a + ".out"), 1)

        def tensor_gather(pe, a):
            pe.wait_ge(S(a + ".out"), 8)
            for hf in range(2):
                for t in range(TPB):
                    for g in range(GROUPS):
                        last = pe.matmul(PS[:, 2 * hf + t // 2, (t % 2) * 4 * PICK + g * PICK:
                                            (t % 2) * 4 * PICK + (g + 1) * PICK],
                                         BIG[:, g, tile(TPB * hf + t)], cf("pick"), start=True, stop=True,
                                         skip_group_check=True)
                last.then_inc(S(a + ".gathered"), 1)
            for hf in range(2):
                pe.wait_ge(S(a + ".divided"), hf + 1)
                for t in range(TPB):
                    last = pe.transpose(PS[:, 4 + hf, tile(t)], T3[:, tile(TPB * hf + t)], cf("ident"))
                last.then_inc(S(a + ".ot_turned"), 1)

        def vector_gather(v, a, link):
            for hf in range(2):
                v.wait_ge(S(a + ".gathered"), hf + 1)
                got = PS[:, 2 * hf:2 * hf + 2, 0:8 * PICK].rearrange("p b (t c) -> p b t c", c=PICK)
                den = DEN[:, hf, :].rearrange("p (b t j) -> p b t j", b=2, j=4)
                if a in LINEAR:
                    link(v.tensor_scalar(den, got[:, :, :, 4 * E:PICK], LINEAR[a][3], None, ALU.add))
                    link(v.reciprocal(DEN[:, hf, :], DEN[:, hf, :]))
                else:
                    link(v.reciprocal(den, got[:, :, :, 4 * E:PICK]))
                for b in range(2):
                    n = TPB * hf + 2 * b
                    i = v.tensor_tensor(T3[:, P * n:P * (n + 2)].rearrange("p (t j e) -> p t j e", t=8, e=E),
                                        got[:, b, :, 0:4 * E].rearrange("p t (j e) -> p t j e", e=E),
                                        DEN[:, hf, 32 * b:32 * (b + 1)].rearrange("p (t j) -> p t j", t=8)
                                        .unsqueeze(3).to_broadcast([P, 8, 4, E]), ALU.mult)
                i.then_inc(S(a + ".divided"), 1)

        def scalar_gather(act, a):
            for hf in range(2):
                act.wait_ge(S(a + ".ot_turned"), hf + 1)
                act.activation(OT[:, half(hf)], bank(4 + hf), ACT.Copy).then_inc(S(a + ".ot"), 1)

        def tensor_back(pe, name, bias, lhs, rhs, depth=1, ready=None):
            for hf in range(2):
                if ready:
                    ready(hf)
                if bias:
                    pe.matmul(bank(4 + hf), row("ones"), row4(bias), start=True, stop=True, skip_group_check=True)
                for t in range(TPB):
                    for k in range(depth):
                        last = pe.matmul(PS[:, 4 + hf, tile(t)], lhs(k, TPB * hf + t), rhs(k, TPB * hf + t),
                                         start=(not bias and t == 0 and k == 0), stop=True,
                                         skip_group_check=True)
                last.then_inc(S(name), 1)

        def vector_back(v, name, dst, other, link, hf):
            v.wait_ge(S(name), hf + 1)
            ts = slice(TPB * hf, TPB * (hf + 1))
            link(v.tensor_tensor(dst[:, ts, :], bank(4 + hf).rearrange("p (t d) -> p t d", t=TPB),
                                 other[:, ts, :], ALU.add))

        FFN = {"L0": "n0f", "L1": "n1f", "L3": "n3f"}

        def sync_experts(sp, m):
            c = MOE[m]
            gu, dn, t3 = T["in" + m], T["down" + m], 3 * c["table"]
            wide = 2 * P if c["glu"] else P

            def load(b, s):
                sp.dma_start(GU[:, s, 0:wide], gu[bass.ds(b * P, P), :]).then_inc(S(f"{m}.gu{s}"), 16)
                if c["glu"]:
                    sp.dma_start(HOT[0:t3, s, :], T["hot" + m][bass.ds(b * t3, t3), :]
                                 ).then_inc(S(f"{m}.gu{s}"), 16)

            def load_down(b, s):
                sp.dma_start(DN[:, s, :], dn[bass.ds(b * P, P), :]).then_inc(S(f"{m}.dn{s}"), 16)

            for s in range(2):
                load(s, s)
                load_down(s, s)
            pairs = c["blocks"] // 2
            with sp.Fori(1, pairs) as i:
                for s in range(2):
                    sp.wait_ge(S(m + ".front"), i * 4 + (2 * s - 2))
                    load(i * 2 + s, s)
                    sp.wait_ge(S(m + ".down"), i * 4 + (2 * s - 2))
                    load_down(i * 2 + s, s)
            if c["blocks"] % 2:
                sp.wait_ge(S(m + ".front"), 4 * pairs - 2)
                load(2 * pairs, 0)
                sp.wait_ge(S(m + ".down"), 4 * pairs - 2)
                load_down(2 * pairs, 0)

        def tensor_router(pe, m):
            NR = {"L0": 9, "L1": 16, "L3": 8}[m]
            for t in range(NT):
                if t % TPB == 0:
                    wait_norm(pe, FFN[m], t // TPB + 1)
                last = pe.matmul(PS[:, 7, 32 * t:32 * t + NR], AT[:, tile(t)], w(m, "router" + m[1]),
                                 start=(t == 0), stop=True, skip_group_check=True)
            last.then_inc(S(m + ".logits"), 1)

        def tensor_experts(pe, m):
            c = MOE[m]
            units, t3, E1 = 2 * c["blocks"], 3 * c["table"], c["table"]
            tensor_router(pe, m)
            for hf in range(2):
                pe.matmul(bank(6 if hf == 0 else 5), zero[:, 0:P], zero[:, :], start=True, stop=True,
                          skip_group_check=True)

            pe.wait_ge(S(m + ".cp"), 1)
            out = bank(4).bitcast(BF16)
            for t in range(NT):
                last = pe.transpose(out[0:t3, tile(t)], CP[:, t, :, 0:E1].rearrange("p a b -> p (a b)")
                                    if E1 == 17 else CPV(m)[:, t, :], cb("ident"))
            last.then_inc(S(m + ".ct_turned"), 1)
            pe.wait_ge(S(m + ".ct_in"), 1)

            G0 = (0, 2)
            W0 = (4, 7)

            def front(n, q):
                s = (q // 2) % 2
                hf = q % 2
                if q % 2 == 0:
                    if isinstance(n, int):
                        pe.wait_ge(S(f"{m}.gu{s}"), 32 * (n // 4 + 1))
                    else:
                        i4, _ = n_parts[0]
                        pe.wait_ge(S(f"{m}.gu{s}"), i4)
                if not (isinstance(n, int) and n < 2):
                    pe.wait_ge(S(m + ".hid"), n - 1)
                pe.matmul(bank(G0[hf]), GU[:, s, 0:P], AT[:, half(hf)], start=True, stop=True)
                pe.matmul(bank(G0[hf] + 1), GU[:, s, P:2 * P], AT[:, half(hf)], start=True, stop=True)
                pe.matmul(bank(W0[hf]), HOT[0:t3, s, :], CT[0:t3, half(hf)], start=True, stop=True
                          ).then_inc(S(m + ".front"), 1)

            def down(n, q):
                s = (q // 2) % 2
                hf = q % 2
                if q % 2 == 0:
                    if isinstance(n, int):
                        pe.wait_ge(S(f"{m}.dn{s}"), 16 * (n // 4 + 1))
                    else:
                        pe.wait_ge(S(f"{m}.dn{s}"), n_parts[0][1])
                pe.wait_ge(S(m + ".hid"), n + 1)
                for t in range(TPB):
                    last = pe.matmul(PS[:, 6 - hf, tile(t)], HID(q % 2)[:, tile(t)], DN[:, s, :],
                                     start=False, stop=True, skip_group_check=True)
                last.then_inc(S(m + ".down"), 1)

            n_parts = [None]
            front(0, 0)
            for u in range(4):
                front(u + 1, (u + 1) % 4)
                down(u, u)
            last4 = (units - 1) // 4
            with pe.Fori(1, last4) as i:
                for q in range(4):
                    ahead = (i + 2) if q == 3 else (i + 1)
                    n_parts[0] = (ahead * 32, (i + 1) * 16)
                    front(i * 4 + (q + 1), (q + 1) % 4)
                    down(i * 4 + q, q)
            for u in range(4 * last4, units):
                if u + 1 < units:
                    front(u + 1, (u + 1) % 4)
                down(u, u % 4)

        def HID(s):
            return PR[:, s, :]

        def CPV(m):
            n = 3 * MOE[m]["table"]
            return CP[:, :, :, :].rearrange("p t a b -> p (t a b)")[:, 0:NT * n].rearrange("p (t n) -> p t n", t=NT)

        def scalar_experts(act, m, link):
            c = MOE[m]
            E1, t3 = c["table"], 3 * c["table"]
            act.wait_ge(S(m + ".ct_turned"), 1)
            act.activation(CT[0:t3, :], bank(4).bitcast(BF16)[0:t3, :], ACT.Copy).then_inc(S(m + ".ct_in"), 1)
            def unit(n, q):
                act.wait_ge(S(m + ".front"), n + 1)
                if not (isinstance(n, int) and n < 2):
                    act.wait_ge(S(m + ".hid"), n - 1)
                act.activation(PR[:, 2 + q % 2, :], bank(2 * (q % 2)), ACT.Silu).then_inc(S(m + ".act"), 1)

            unit_loop(act, 2 * c["blocks"], unit)

        def vector_experts(v, m, link):
            c = MOE[m]

            def unit(n, q):
                s = q % 2
                v.wait_ge(S(m + ".act"), n + 1)
                if not (isinstance(n, int) and n < 2):
                    v.wait_ge(S(m + ".down"), n - 1)
                src = PR[:, 2 + s, :]
                v.tensor_tensor(PR[:, 4 + s, :], src, bank(2 * s + 1), ALU.mult).then_inc(S(m + ".gated"), 1)
                v.wait_ge(S(m + ".gated"), n + 1)
                v.tensor_tensor(HID(s), PR[:, 4 + s, :], bank((4, 7)[s]), ALU.mult).then_inc(S(m + ".hid"), 1)

            unit_loop(v, 2 * c["blocks"], unit)

        UNITS = 2 * PER_EXPERT
        L3_EXPERTS = MOE["L3"]["experts"]
        L3_UNITS = 2 * MOE["L3"]["blocks"]

        def tensor_experts_3(pe):
            E1 = MOE["L3"]["table"]
            tensor_router(pe, "L3")

            def front(e, q):
                s, n = (q // 2) % 2, e * UNITS + q
                if q % 2 == 0:
                    pe.wait_ge(S(f"L3.gu{s}"), e * 32 + 16 * (q // 4 + 1))
                if not (isinstance(e, int) and n < 4):
                    pe.wait_ge(S("L3.hid"), n - 3)
                pe.matmul(bank(q % 4), GU[:, s, 0:P], AT[:, half(q % 2)], start=True, stop=True
                          ).then_inc(S("L3.front"), 1)

            def down(e, q):
                s, n, hf = (q // 2) % 2, e * UNITS + q, q % 2
                if q % 2 == 0:
                    pe.wait_ge(S(f"L3.dn{s}"), e * 32 + 16 * (q // 4 + 1))
                if q < 2 and not (isinstance(e, int) and e == 0):
                    pe.wait_ge(S("L3.mixed"), e * 2 + (hf - 1))
                pe.wait_ge(S("L3.hid"), n + 1)
                for t in range(TPB):
                    last = pe.matmul(PS[:, 6 - hf, tile(t)], PR[:, q % 4, tile(t)], DN[:, s, :],
                                     start=(q < 2 and t == 0), stop=True, skip_group_check=True)
                last.then_inc(S("L3.down"), 1)

            def expert(e, units=UNITS, more=True):
                for q in range(units):
                    if q + 1 < units:
                        front(e, q + 1)
                    elif more:
                        front(e + 1, 0)
                    down(e, q)

            front(0, 0)
            pe.wait_ge(S("L3.cp"), 1)
            for hf in range(2):
                for t in range(TPB):
                    last = pe.transpose(PS[0:E1, 2 + hf, tile(t)], CW[:, TPB * hf + t, 0:E1], cf("ident"))
            last.then_inc(S("L3.c_turned"), 1)
            pe.wait_ge(S("L3.c_in"), 1)
            for hf in range(2):
                for t in range(TPB):
                    last = pe.matmul(PS[:, 4 + 3 * hf, tile(t)], C32[0:E1, tile(TPB * hf + t)], w("L3", "b2"),
                                     start=(t == 0), stop=True, skip_group_check=True)
            last.then_inc(S("L3.shift"), 1)
            expert(0)
            with pe.Fori(1, L3_EXPERTS) as e:
                expert(e)
            expert(L3_EXPERTS, L3_UNITS - UNITS * L3_EXPERTS, more=False)

        def scalar_experts_3(act):
            E1 = MOE["L3"]["table"]
            act.wait_ge(S("L3.b1g"), 1)
            flat_b1g = b1g[:, :, :].rearrange("p b c -> p (b c)")

            def expert(e, units=UNITS):
                for q in range(units):
                    if q % 4 == 0:
                        act.activation(GB[:, q // 2:q // 2 + 2, :].rearrange("p b c -> p (b c)"),
                                       flat_b1g[:, bass.ds(e * UNITS + q, 4)], ACT.Copy).then_inc(S("L3.gb"), 1)
                        act.wait_ge(S("L3.gb"), e * 2 + (q // 4 + 1))
                    n = e * UNITS + q
                    act.wait_ge(S("L3.front"), n + 1)
                    if not (isinstance(e, int) and n < 4):
                        act.wait_ge(S("L3.down"), n - 3)
                    act.activation(PR[:, q % 4, :], bank(q % 4), ACT.Gelu, bias=GB[:, q // 2, 0:1],
                                   scale=GB[:, q // 2, 1:2]).then_inc(S("L3.hid"), 1)

            act.wait_ge(S("L3.c_turned"), 1)
            act.activation(C32[0:E1, :], PS[0:E1, 2:4, :].rearrange("p a b -> p (a b)"), ACT.Copy
                           ).then_inc(S("L3.c_in"), 1)
            expert(0)
            with act.Fori(1, L3_EXPERTS) as e:
                expert(e)
            expert(L3_EXPERTS, L3_UNITS - UNITS * L3_EXPERTS)

        def vector_experts_3(v, link):
            def expert(e, done, before=None):
                if not (isinstance(e, int) and e == 0):
                    v.wait_ge(S("L3.mixed"), e * 2)
                v.tensor_copy(CE[:, :], CW[:, :, bass.ds(e, 1)].rearrange("p t o -> p (t o)")
                              ).then_inc(S("L3.ce"), 1)
                v.wait_ge(S("L3.ce"), e + 1)
                for hf in range(2):
                    v.wait_ge(S("L3.down"), done + hf)
                    for t in range(TPB):
                        to = T0[:, tile(TPB * hf + t)]
                        last = v.scalar_tensor_tensor(out=to, in0=PS[:, 6 - hf, tile(t)],
                                                      scalar=CE[:, TPB * hf + t:TPB * hf + t + 1],
                                                      in1=to, op0=ALU.mult, op1=ALU.add)
                    last.then_inc(S("L3.mixed"), 1)

            v.wait_ge(S("L3.shift"), 1)
            for hf in range(2):
                link(v.tensor_copy(T0[:, half(hf)], bank(4 + 3 * hf)))
            expert(0, UNITS - 1)
            with v.Fori(1, L3_EXPERTS) as e:
                expert(e, e * UNITS + (UNITS - 1))
            expert(L3_EXPERTS, L3_UNITS - 1)

        def rank_of(v, link, s, n, k, before, out, scratch, scratch2):
            G = s.shape[1]
            big = [P, G, n, n]
            sj = s.unsqueeze(2).to_broadcast(big)
            si = s.unsqueeze(3).to_broadcast(big)
            bf = before.rearrange("p (i j) -> p i j", i=n).unsqueeze(1).to_broadcast(big)
            s1 = scratch[:, 0:G * n * n].rearrange("p (g i j) -> p g i j", g=G, i=n)
            s2 = scratch2[:, 0:G * n * n].rearrange("p (g i j) -> p g i j", g=G, i=n)
            v.tensor_tensor(s1, sj, si, ALU.is_gt).then_inc(link.sem, 1)
            link.n += 1
            link(v.tensor_tensor(s2, sj, si, ALU.is_equal))
            link(v.tensor_tensor(s2, s2, bf, ALU.mult))
            link(v.tensor_tensor(s1, s1, s2, ALU.add))
            link(v.tensor_reduce(out, s1, AX.X, ALU.add))
            link(v.tensor_scalar(out, out, float(k) - 0.5, None, ALU.is_lt))

        def top_of(v, link, s, n, k, out):
            top = T2[:, 0:8 * NT].rearrange("p (t e) -> p t e", t=NT)
            above, same, nth = (T2[:, 128 * i:128 * i + NT * n].rearrange("p (t e) -> p t e", t=NT)
                                for i in (1, 2, 3))
            for t in range(NT):
                last = v.max(top[:, t, :], s[:, t, :])
            link(last)
            kth = top[:, :, k - 1].unsqueeze(2).to_broadcast([P, NT, n])
            v.tensor_tensor(same, s, kth, ALU.is_equal)
            link(v.tensor_tensor(above, s, kth, ALU.is_gt))
            v.tensor_reduce(small[:, 3, :], above, AX.X, ALU.add)
            link(v.tensor_tensor_scan(T2[:, 384:384 + NT * n], cf(f"keep{n}"), T2[:, 256:256 + NT * n], 0.0,
                                      ALU.mult, ALU.add))
            link(v.tensor_tensor(nth, nth, small[:, 3, :].unsqueeze(2).to_broadcast([P, NT, n]), ALU.add))
            link(v.scalar_tensor_tensor(out=same, in0=nth, scalar=float(k), in1=same, op0=ALU.is_le, op1=ALU.mult))
            link(v.tensor_tensor(out, above, same, ALU.add))

        def bc(ap, n):
            return ap.unsqueeze(2).to_broadcast([P, NT, n])

        def vector_route(v, m, link):
            c = MOE[m]
            n, E1 = c["experts"], c["table"]
            lg = T0[:, 0:NT * 32].rearrange("p (t e) -> p t e", t=NT)
            sc = T0[:, 256:256 + NT * n].rearrange("p (t e) -> p t e", t=NT)
            sel = T0[:, 512:512 + NT * n].rearrange("p (t e) -> p t e", t=NT)
            tmp = T0[:, 768:768 + NT * n].rearrange("p (t e) -> p t e", t=NT)
            r1 = small[:, 2, :]
            v.wait_ge(S(m + ".logits"), 1)
            lp = bank(7)[:, 0:NT * 32].rearrange("p (t e) -> p t e", t=NT)
            NR = {"L0": 9, "L1": 16, "L3": 8}[m]
            if m == "L3":
                link(v.tensor_tensor(lg[:, :, 0:8], lp[:, :, 0:8],
                                     w("L3", "router3_b").unsqueeze(1).to_broadcast([P, NT, 8]), ALU.add))
            else:
                link(v.tensor_copy(lg[:, :, 0:NR], lp[:, :, 0:NR]))
            if m == "L1":
                v.engine_nop().then_inc(S(m + ".lg"), 1) if False else \
                    v.tensor_copy(tmp, lg[:, :, 0:16]).then_inc(S(m + ".lg"), 1)
                v.wait_ge(S(m + ".sg"), 1)
                sfc = T1[:, 0:128].rearrange("p (t e) -> p t e", t=NT)
                link(v.tensor_tensor(sfc, sc, w("L1", "router1_b").unsqueeze(1).to_broadcast([P, NT, 16]), ALU.add))
                g4 = T1[:, 0:128].rearrange("p (g e) -> p g e", e=4)
                pairs = T1[:, 0:128].rearrange("p (g c e) -> p g c e", c=2, e=2)
                high = T1[:, 128:192].rearrange("p (g c) -> p g c", c=2)
                low = T1[:, 192:256].rearrange("p (g c) -> p g c", c=2)
                best, second, gs = T1[:, 480:512], T1[:, 448:480], T1[:, 256:288]
                v.tensor_tensor(high, pairs[:, :, :, 0], pairs[:, :, :, 1], ALU.max)
                link(v.tensor_tensor(low, pairs[:, :, :, 0], pairs[:, :, :, 1], ALU.min))
                v.tensor_tensor(best, high[:, :, 0], high[:, :, 1], ALU.max)
                v.tensor_tensor(second, high[:, :, 0], high[:, :, 1], ALU.min)
                link(v.tensor_tensor(gs, low[:, :, 0], low[:, :, 1], ALU.max))
                link(v.tensor_tensor(second, second, gs, ALU.max))
                link(v.tensor_tensor(gs, best, second, ALU.add))
                gsel = T1[:, 288:320].rearrange("p (t g) -> p t g", t=NT)
                rank_of(v, link, gs.rearrange("p (t g) -> p t g", t=NT), 4, 2, cf("before4"), gsel, T2, T3)
                chosen = T1[:, 288:320].unsqueeze(2).to_broadcast([P, 32, 4])
                mk = T1[:, 320:448].rearrange("p (g e) -> p g e", e=4)
                link(v.tensor_tensor(mk, g4, chosen, ALU.mult))
                low = T1[:, 448:480]
                link(v.tensor_scalar(low, T1[:, 288:320], -NEG, NEG, ALU.mult, ALU.add))
                link(v.tensor_tensor(mk, mk, low.unsqueeze(2).to_broadcast([P, 32, 4]), ALU.add))
                mt = T1[:, 320:448].rearrange("p (t e) -> p t e", t=NT)
                top_of(v, link, mt, 16, 4, sel)
                link(v.tensor_tensor(sel, sel, sc, ALU.mult))
                link(v.tensor_reduce(r1, sel, AX.X, ALU.add))
                link(v.tensor_scalar(r1, r1, 1e-20, None, ALU.add))
                link(v.reciprocal(r1, r1))
                link(v.tensor_tensor(sel, sel, bc(r1, 16), ALU.mult))
                link(v.tensor_scalar(CW[:, :, 0:16], sel, 2.5, None, ALU.mult))
                link(v.memset(CW[:, :, 16], 1.0))
            else:
                link(v.tensor_reduce(r1, lg[:, :, 0:8], AX.X, ALU.max))
                v.tensor_tensor(tmp, lg[:, :, 0:8], bc(r1, 8), ALU.subtract).then_inc(S(m + ".lg"), 1)
                v.wait_ge(S(m + ".sg"), 1)
                link(v.tensor_reduce(r1, sc, AX.X, ALU.add))
                link(v.reciprocal(r1, r1))
                link(v.tensor_tensor(sc, sc, bc(r1, 8), ALU.mult))
                top_of(v, link, sc, 8, 2, sel)
                if m == "L0":
                    link(v.tensor_tensor(CW[:, :, 0:8], sel, sc, ALU.mult))
                    v.wait_ge(S("L0.sw"), 1)
                    link(v.tensor_copy(CW[:, :, 8], small[:, 6, :]))
                else:
                    link(v.tensor_tensor(sel, sel, sc, ALU.mult))
                    link(v.tensor_reduce(r1, sel, AX.X, ALU.add))
                    link(v.reciprocal(r1, r1))
                    link(v.tensor_tensor(CW[:, :, 0:8], sel, bc(r1, 8), ALU.mult))
                    v.wait_ge(S("L3.sw"), 1)
                    v.tensor_copy(CW[:, :, 8], vec[:, 0:1].to_broadcast([P, NT])).then_inc(S("L3.cp"), 1)
                    v.wait_ge(S("L3.cp"), 1)
                    return
            n3 = 3 * E1
            cp = CPV(m).rearrange("p t (a e) -> p t a e", a=3)
            cw, left = CW[:, :, 0:E1], CWR[:, :, 0:E1]
            link(v.tensor_copy(cp[:, :, 0, :], cw))
            link(v.tensor_tensor(left, cw, cp[:, :, 0, :], ALU.subtract))
            link(v.tensor_copy(cp[:, :, 1, :], left))
            v.tensor_tensor(cp[:, :, 2, :], left, cp[:, :, 1, :], ALU.subtract).then_inc(S(m + ".cp"), 1)

        def scalar_route(act, m):
            c = MOE[m]
            n = c["experts"]
            act.wait_ge(S(m + ".lg"), 1)
            fn = ACT.Sigmoid if m == "L1" else ACT.Exp
            act.activation(T0[:, 256:256 + NT * n], T0[:, 768:768 + NT * n], fn).then_inc(S(m + ".sg"), 1)
            if m == "L0":
                act.activation(small[:, 6, :], T0[:, 0:NT * 32].rearrange("p (t e) -> p t e", t=NT)[:, :, 8],
                               ACT.Sigmoid).then_inc(S("L0.sw"), 1)
            if m == "L3":
                act.activation(vec[:, 0:1], w("L3", "shared_w"), ACT.Sigmoid).then_inc(S("L3.sw"), 1)

        def vector_add_experts(v, m, link, hf):
            v.wait_ge(S(m + ".down"), 2 * MOE[m]["blocks"] - 1 + hf)
            ts = slice(TPB * hf, TPB * (hf + 1))
            y = bank(6 - hf).rearrange("p (t d) -> p t d", t=TPB)
            if m == "L1":
                link(v.tensor_tensor(A[:, ts, :], A[:, ts, :], y, ALU.add))
                link(v.tensor_tensor(X[:, ts, :], X[:, ts, :], A[:, ts, :], ALU.add))
            else:
                link(v.tensor_tensor(X[:, ts, :], X[:, ts, :], y, ALU.add))

        pass_ = ctx_loop.enter_context(nc.Fori(0, PASSES))
        phase = {}

        def begin_phase():
            phase["sems"], phase["block"] = ExitStack(), ExitStack()
            return phase["block"].enter_context(nc.Block())

        def end_phase():
            phase["block"].close()
            numbers = sorted(x.num for x in sems.values())
            assert numbers == list(range(numbers[0], numbers[0] + len(numbers)))
            nc.all_engine_barrier(sems_to_clear=range(numbers[0], numbers[-1] + 1))
            phase["sems"].close()
            sems.clear()

        def SPIKES(n):
            return PR[:, 6 + n % 2, :].bitcast(BF16)[:, HALF * (n // 2 % 2):HALF * (n // 2 % 2 + 1)]

        block = begin_phase()

        @block.sync
        def _(sp):
            sp.dma_start(flat(X), T["x"][bass.ds(pass_ * P, P), :]).then_inc(S("x_in"), 16)
            sync_stacks(sp, "a")
            sync_max(sp, "a")
            sync_stacks(sp, "s")
            if stop > 1:
                sync_experts(sp, "L0")
            if stop > 2:
                sync_stacks(sp, "l")
            if stop > 3:
                sync_experts(sp, "L1")

        @block.gpsimd
        def _(g):
            chain = Link(g, S("gpsimd_chain"))
            g.wait_ge(ONCE["half_ready"], 1)
            for i, k in enumerate(("n0", "n0m", "n0f", "n1", "n1f")):
                if stop >= i:
                    gpsimd_norm(g, k, chain)

        @block.scalar
        def _(act):
            link = Link(act, S("scalar_chain"))
            act.wait_ge(ONCE["wall_L0"], 16)
            scalar_norm(act, "n0")
            scalar_qk(act, "a")
            scalar_softmax(act, "a")
            scalar_gather(act, "a")
            scalar_qk(act, "s")
            scalar_linear(act, "s")
            scalar_gather(act, "s")
            scalar_norm(act, "n0m")
            for m in range(4):
                for hf in range(2):
                    act.wait_ge(S("mlp.up"), 2 * m + hf + 1)
                    act.activation(BIG[:, m, half(hf)], bank((2 * m + hf) % 4), ACT.Gelu,
                                   bias=w("L0", "b1m", m, m + 1)).then_inc(S("mlp.gelu"), 1)
            if stop > 1:
                scalar_norm(act, "n0f")
                scalar_route(act, "L0")
                scalar_experts(act, "L0", link)
            if stop > 2:
                act.wait_ge(ONCE["wall_L1"], 16)
                scalar_norm(act, "n1")
                scalar_qk(act, "l")
                scalar_linear(act, "l")
                scalar_gather(act, "l")
            if stop > 3:
                scalar_norm(act, "n1f")
                scalar_route(act, "L1")
                scalar_experts(act, "L1", link)

        @block.vector
        def _(v):
            link = Link(v, S("vector_chain"))
            v.wait_ge(S("x_in"), 16)
            v.wait_ge(ONCE["wall_L0"], 16)
            v.wait_ge(ONCE["cf_in"], 16)
            vector_norm(v, "n0")
            vector_qk(v, "a", link)
            vector_softmax(v, "a", link)
            vector_gather(v, "a", link)
            v.wait_ge(S("a.proj"), 2)
            link(v.tensor_scalar(flat(A2), bank(6, 2), w("L0", "bp_a"), None, ALU.add))
            vector_qk(v, "s", link)
            vector_linear(v, "s")
            vector_gather(v, "s", link)
            v.wait_ge(S("s.proj"), 2)
            v.scalar_tensor_tensor(out=flat(A2), in0=bank(6, 2), scalar=w("L0", "bo_s"), in1=flat(A2),
                                   op0=ALU.add, op1=ALU.add).then_inc(S("s.sum"), 1)
            vector_norm(v, "n0m", lambda hf: vector_back(v, "mixed", tok(T0), A, link, hf))
            link(v.tensor_tensor(flat(X), flat(X), T0[:, :], ALU.add))
            if stop > 1:
                vector_norm(v, "n0f", lambda hf: vector_back(v, "mlp.back", X, X, link, hf))
                vector_route(v, "L0", link)
                vector_experts(v, "L0", link)
            if stop > 2:
                v.wait_ge(ONCE["wall_L1"], 16)
                vector_norm(v, "n1", lambda hf: vector_add_experts(v, "L0", link, hf))
                vector_qk(v, "l", link)
                vector_linear(v, "l")
                vector_gather(v, "l", link)
            if stop > 3:
                vector_norm(v, "n1f", lambda hf: vector_back(v, "l.back", X, X, link, hf))
                vector_route(v, "L1", link)
                vector_experts(v, "L1", link)
                for hf in range(2):
                    vector_add_experts(v, "L1", link, hf)

        @block.tensor
        def _(pe):
            pe.wait_ge(ONCE["cf_in"], 16)
            pe.wait_ge(ONCE["zero_in"], 1)
            tensor_norm(pe, "n0")
            tensor_qkv(pe, "a")
            tensor_softmax(pe, "a")
            tensor_gather(pe, "a")
            for hf in range(2):
                pe.wait_ge(S("a.ot"), hf + 1)
                pe.matmul(bank(6 + hf), w("L0", "Wp_a"), OT[:, half(hf)], start=True, stop=True
                          ).then_inc(S("a.proj"), 1)
            tensor_qkv(pe, "s")
            tensor_linear(pe, "s")
            tensor_gather(pe, "s")
            for hf in range(2):
                pe.wait_ge(S("s.ot"), hf + 1)
                pe.matmul(bank(6 + hf), w("L0", "Wo_s"), OT[:, half(hf)], start=True, stop=True
                          ).then_inc(S("s.proj"), 1)
            pe.wait_ge(S("s.sum"), 1)
            tensor_back(pe, "mixed", "bo", lambda k, t: flat(A2)[:, tile(t)], lambda k, t: w("L0", "Wo"))
            tensor_norm(pe, "n0m")
            wait_norm(pe, "n0m", 2)
            for m in range(4):
                for hf in range(2):
                    n = 2 * m + hf
                    if n >= 4:
                        pe.wait_ge(S("mlp.gelu"), n - 3)
                    pe.matmul(bank(n % 4), w("L0", "W1", P * m, P * (m + 1)), T2[:, half(hf)],
                              start=True, stop=True).then_inc(S("mlp.up"), 1)
            pe.wait_ge(S("mlp.gelu"), 8)
            tensor_back(pe, "mlp.back", "b2m", lambda k, t: BIG[:, k, tile(t)],
                        lambda k, t: w("L0", "W2", P * k, P * (k + 1)), depth=4)
            if stop > 1:
                tensor_norm(pe, "n0f")
                tensor_experts(pe, "L0")
            if stop > 2:
                tensor_norm(pe, "n1")
                tensor_qkv(pe, "l")
                tensor_linear(pe, "l")
                tensor_gather(pe, "l")
                tensor_back(pe, "l.back", "proj_b", lambda k, t: OT[:, tile(t)], lambda k, t: w("L1", "proj_w"),
                            ready=lambda hf: pe.wait_ge(S("l.ot"), hf + 1))
            if stop > 3:
                tensor_norm(pe, "n1f")
                tensor_experts(pe, "L1")

        end_phase()

        block = begin_phase()

        @block.sync
        def _(sp):
            if stop > 6:
                sync_stacks(sp, "f")
                sync_max(sp, "f")
            if stop > 7:
                sync_experts(sp, "L3")
            for hf in range(2):
                sp.wait_ge(S("x_final"), hf + 1)
                sp.dma_start(T["out"][bass.ds(pass_ * P, P), half(hf)], flat(X)[:, half(hf)]
                             ).then_inc(S("out_done"), 16)
            sp.wait_ge(S("out_done"), 32)

        @block.gpsimd
        def _(g):
            chain = Link(g, S("gpsimd_chain"))
            for i, k in enumerate(("n2", "n2f", "n3", "n3f")):
                if stop > i + 4:
                    gpsimd_norm(g, k, chain)
            if stop > 7:
                for hf in range(2):
                    ts = slice(TPB * hf, TPB * (hf + 1))
                    g.wait_ge(S("y_moments"), TPB * (hf + 1))
                    chain(g.tensor_scalar(small[:, 0, ts], moments[:, ts, 1], EPS, None, ALU.add))
                    g.tensor_tensor(small[:, 1, ts], small[:, 0, ts], small[:, 7, ts], ALU.pow
                                    ).then_inc(S("y_rstd"), 1)

        @block.scalar
        def _(act):
            link = Link(act, S("scalar_chain"))
            if stop > 4:
                act.wait_ge(ONCE["wall_L2"], 16)
                scalar_norm(act, "n2")
                act.wait_ge(S("g.proj"), 4)
                act.activation(T1[:, half(0)], bank(2), ACT.Tanh, bias=w("L2", "bz")).then_inc(S("g.z"), 1)
                act.activation(T1[:, half(1)], bank(3), ACT.Sigmoid, bias=w("L2", "bo")).then_inc(S("g.z"), 1)
                act.wait_ge(S("g.arg"), 1)
                act.activation(T2[:, :], T2[:, :], ACT.Exp).then_inc(S("g.exp"), 1)
                act.wait_ge(S("g.c"), 1)
                act.activation(T3[:, half(1)], T3[:, half(0)], ACT.Tanh).then_inc(S("g.tanh"), 1)
            if stop > 5:
                scalar_norm(act, "n2f")
                for m in range(4):
                    for hf in range(2):
                        n = 2 * m + hf
                        act.wait_ge(S("spk.up"), n + 1)
                        if n >= 4:
                            act.wait_ge(S("spk.h"), n - 3)
                        act.activation(PR[:, n % 4, :], bank(n % 4), ACT.Relu).then_inc(S("spk.relu"), 1)

                def spiked(hf):
                    for step in range(SPIKE_STEPS):
                        n = SPIKE_STEPS * hf + step
                        sign = PR[:, 4 + n % 2, :]
                        act.wait_ge(S("spk.step"), n + 1)
                        if n >= 2:
                            act.wait_ge(S("spk.spiked"), n - 1)
                        act.activation(sign, (T0, T1)[step % 2][:, half(hf)], ACT.Sign, scale=-0.5,
                                       bias=small[:, 7, 0:1]).then_inc(S("spk.sign"), 1)
                        act.wait_ge(S("spk.sign"), n + 1)
                        if n >= 4:
                            act.wait_ge(S("spk.counted"), n - 3)
                        act.activation(SPIKES(n), sign, ACT.Relu).then_inc(S("spk.spiked"), 1)

                spiked(0)
                spiked(1)
            if stop > 6:
                act.wait_ge(ONCE["wall_L3"], 16)
                scalar_norm(act, "n3")
                scalar_qk(act, "f")
                scalar_softmax(act, "f")
                scalar_gather(act, "f")
            if stop > 7:
                scalar_norm(act, "n3f")
                scalar_route(act, "L3")
                scalar_experts_3(act)

        @block.vector
        def _(v):
            link = Link(v, S("vector_chain"))
            v.wait_ge(ONCE["wall_L3"], 16)
            v.tensor_tensor(b1g[:, :, 0], w("L3", "b1"), w("L3", "gate"), ALU.mult)
            v.tensor_copy(b1g[:, :, 1], w("L3", "gate")).then_inc(S("L3.b1g"), 1)
            if stop > 4:
                v.wait_ge(ONCE["wall_L2"], 16)
                vector_norm(v, "n2")
                li, lf = T0[:, half(0)], T0[:, half(1)]
                v.wait_ge(S("g.proj"), 2)
                link(v.tensor_scalar(li, bank(0), w("L2", "bi"), 20.0, ALU.add, ALU.min))
                link(v.tensor_scalar(lf, bank(1), w("L2", "bf"), 20.0, ALU.add, ALU.min))
                link(v.tensor_scalar(T0[:, :], T0[:, :], -20.0, None, ALU.max))
                ms = BIG[:, 0, 0:513]
                link(v.memset(BIG[:, 0, 0:1], 0.0))
                link(v.tensor_tensor_scan(ms[:, 1:513], lf, li, 0.0, ALU.add, ALU.max))
                link(v.tensor_tensor(lf, lf, ms[:, 0:512], ALU.add))
                link(v.tensor_tensor(T2[:, half(0)], li, ms[:, 1:513], ALU.subtract))
                v.tensor_tensor(T2[:, half(1)], lf, ms[:, 1:513], ALU.subtract).then_inc(S("g.arg"), 1)
                v.wait_ge(S("g.exp"), 1)
                v.wait_ge(S("g.z"), 2)
                link(v.tensor_tensor(T2[:, half(0)], T2[:, half(0)], T1[:, half(0)], ALU.mult))
                v.tensor_tensor_scan(T3[:, half(0)], T2[:, half(1)], T2[:, half(0)], 0.0, ALU.mult, ALU.add
                                     ).then_inc(S("g.c"), 1)
                v.wait_ge(S("g.tanh"), 1)
                v.tensor_tensor(OT[:, half(0)], T1[:, half(1)], T3[:, half(1)], ALU.mult).then_inc(S("g.h"), 1)
            if stop > 5:
                vector_norm(v, "n2f", lambda hf: vector_back(v, "g.back", X, X, link, hf))
                for n in range(8):
                    v.wait_ge(S("spk.relu"), n + 1)
                    v.scalar_tensor_tensor(out=BIG[:, n // 2, half(n % 2)], in0=bank(n % 4), scalar=0.0,
                                           in1=PR[:, n % 4, :], op0=ALU.max, op1=ALU.mult
                                           ).then_inc(S("spk.h"), 1)

                def spikes(hf):
                    v.wait_ge(S("spk.back"), hf + 1)
                    y, u = bank(4 + hf), T3[:, half(hf)]
                    m = [T0[:, half(hf)], T1[:, half(hf)]]
                    v.tensor_scalar(m[0], y, -1.0, None, ALU.mult).then_inc(S("spk.step"), 1)
                    v.wait_ge(S("spk.step"), SPIKE_STEPS * hf + 1)
                    for step in range(1, SPIKE_STEPS):
                        old, new = m[(step - 1) % 2], m[step % 2]
                        link(v.scalar_tensor_tensor(out=u, in0=old, scalar=0.9, in1=y,
                                                    op0=ALU.mult, op1=ALU.subtract))
                        if step >= 2:
                            v.wait_ge(S("spk.sign"), SPIKE_STEPS * hf + step - 1)
                        v.scalar_tensor_tensor(out=new, in0=old, scalar=-1.0, in1=u,
                                               op0=ALU.is_lt, op1=ALU.add).then_inc(S("spk.step"), 1)
                        v.wait_ge(S("spk.step"), SPIKE_STEPS * hf + step + 1)
                    v.wait_ge(S("spk.counted"), SPIKE_STEPS * (hf + 1))
                    ts = slice(TPB * hf, TPB * (hf + 1))
                    link(v.scalar_tensor_tensor(out=X[:, ts, :], in0=bank(6 + hf).rearrange("p (t d) -> p t d", t=TPB),
                                                scalar=1.0 / SPIKE_STEPS, in1=X[:, ts, :],
                                                op0=ALU.mult, op1=ALU.add))
                if stop == 6:
                    spikes(0)
                    spikes(1)
            if stop > 6:
                v.wait_ge(ONCE["wall_L3"], 16)
                vector_norm(v, "n3", spikes)
                vector_qk(v, "f", link)
                vector_softmax(v, "f", link)
                vector_gather(v, "f", link)
            if stop > 7:
                vector_norm(v, "n3f", lambda hf: vector_back(v, "f.back", X, X, link, hf))
                vector_route(v, "L3", link)
                shift = w("L3", "ln_b3").unsqueeze(1).to_broadcast([P, NT, D])
                link(v.tensor_tensor(X[:, :, :], X[:, :, :], shift, ALU.add))
                vector_experts_3(v, link)
                y = tok(T0)
                for hf in range(2):
                    v.wait_ge(S("L3.mixed"), 2 * L3_EXPERTS + hf + 1)
                    for t in range(TPB * hf, TPB * (hf + 1)):
                        v.bn_stats(stats[:, t, :], y[:, t, :]).then_inc(S("y_stats"), 1)
                    v.wait_ge(S("y_stats"), TPB * (hf + 1))
                    for t in range(TPB * hf, TPB * (hf + 1)):
                        v.bn_aggr(moments[:, t, :], stats[:, t, :]).then_inc(S("y_moments"), 1)
                for hf in range(2):
                    v.wait_ge(S("y_rstd"), hf + 1)
                    for t in range(TPB * hf, TPB * (hf + 1)):
                        v.tensor_scalar(y[:, t, :], y[:, t, :], moments[:, t, 0:1], small[:, 1, t:t + 1],
                                        ALU.subtract, ALU.mult).then_inc(S("y_normed"), 1)
                    v.wait_ge(S("y_normed"), TPB * (hf + 1))
                    ts = slice(TPB * hf, TPB * (hf + 1))
                    scale = w("L3", "ln_g3").unsqueeze(1).to_broadcast([P, TPB, D])
                    link(v.tensor_tensor(y[:, ts, :], y[:, ts, :], scale, ALU.mult))
                    v.tensor_tensor(X[:, ts, :], X[:, ts, :], y[:, ts, :], ALU.add).then_inc(S("x_final"), 1)
            else:
                v.memset(vec[:, 3:4], 0.0).then_inc(S("x_final"), 2)

        @block.tensor
        def _(pe):
            if stop > 4:
                tensor_norm(pe, "n2")
                wait_norm(pe, "n2", 2)
                for i, m in enumerate(("Wi", "Wf", "Wz", "Wo")):
                    for b in range(B):
                        last = pe.matmul(PS[64 * b:64 * b + 64, i, :], w("L2", m), NTT[:, half(b)],
                                         start=True, stop=True, tile_position=(0, 64 * b))
                    last.then_inc(S("g.proj"), 1)
                pe.wait_ge(S("g.h"), 1)
                tensor_back(pe, "g.back", "bp", lambda k, t: OT[64 * (t // TPB):64 * (t // TPB) + 64, tile(t % TPB)],
                            lambda k, t: w("L2", "Wp")[64 * (t // TPB):64 * (t // TPB) + 64, :])
            if stop > 5:
                tensor_norm(pe, "n2f")
                wait_norm(pe, "n2f", 2)
                for n in range(8):
                    m, hf = divmod(n, 2)
                    if n >= 4:
                        pe.wait_ge(S("spk.h"), n - 3)
                    pe.matmul(bank(n % 4), w("L2", "W_fc", P * m, P * (m + 1)), AT[:, half(hf)],
                              start=True, stop=True).then_inc(S("spk.up"), 1)
                pe.wait_ge(S("spk.h"), 8)
                tensor_back(pe, "spk.back", None, lambda k, t: BIG[:, k, tile(t)],
                            lambda k, t: w("L2", "W_proj", P * k, P * (k + 1)), depth=4)

                def counted(hf):
                    for step in range(SPIKE_STEPS):
                        n = SPIKE_STEPS * hf + step
                        pe.wait_ge(S("spk.spiked"), n + 1)
                        pe.matmul(bank(6 + hf), cb("ident"), SPIKES(n), start=(step == 0), stop=True,
                                  skip_group_check=True).then_inc(S("spk.counted"), 1)

                counted(0)
                counted(1)
            if stop > 6:
                tensor_norm(pe, "n3")
                tensor_qkv(pe, "f")
                tensor_softmax(pe, "f")
                tensor_gather(pe, "f")
                tensor_back(pe, "f.back", "bo3", lambda k, t: OT[:, tile(t)], lambda k, t: w("L3", "wo"),
                            ready=lambda hf: pe.wait_ge(S("f.ot"), hf + 1))
            if stop > 7:
                tensor_norm(pe, "n3f")
                tensor_experts_3(pe)

        end_phase()


class Link:

    def __init__(self, eng, sem):
        self.eng, self.sem, self.n = eng, sem, 0

    def __call__(self, instruction):
        self.n += 1
        instruction.then_inc(self.sem, 1)
        self.eng.wait_ge(self.sem, self.n)


STOP = 99


def kernel(**inputs):
    import concourse.bacc as _bacc
    from concourse.bass_utils import run_bass_kernel_spmd as _run

    nc = _bacc.Bacc("TRN2", target_bir_lowering=False, num_devices=1)
    arrays, at = lay_out(inputs)
    T = {n: nc.dram_tensor("in_" + n, a.shape, mybir.dt.from_np(a.dtype), kind="ExternalInput").ap()
         for n, a in arrays.items()}
    T = {n: ap.bitcast(BF16) if arrays[n].dtype == np.uint16 else ap for n, ap in T.items()}
    T["out"] = nc.dram_tensor("out", (PASSES * P, NT * D), F32, kind="ExternalOutput").ap()
    program(nc, T, at, {n: a.shape for n, a in arrays.items()}, STOP)
    r = _run(nc, [{"in_" + n: a for n, a in arrays.items()}], core_ids=[0])
    out = np.asarray(r.results[0]["out"])
    return np.ascontiguousarray(out.reshape(PASSES, P, NT, D).transpose(0, 2, 1, 3).reshape(PASSES * B, L, D))
```

```python
from contextlib import ExitStack

import numpy as np
import concourse.bass as bass
from concourse import mybir

F32 = mybir.dt.float32
BF16 = mybir.dt.bfloat16
ALU = mybir.AluOpType
ACT = mybir.ActivationFunctionType
AX = mybir.AxisListType

P = 128
B, L, D, H = 2, 512, 128, 16
E = D // H
NT = B * L // P
TPB = L // P
TOK = B * L
PASSES = 2
HALF = 512
VW = 32
GROUPS = H // 4
SCALE = float(E) ** -0.5
NEG = -1e30
EPS = 1e-5
SPIKE_STEPS = 5

Q_PARTS = (0, 0, 1, 1, 0, 2)
K_PARTS = (0, 1, 0, 1, 2, 0)
STACK = 96
M_ROW = 96

MOE = {"L0": dict(blocks=14, experts=8, table=9, topk=2, glu=True),
       "L1": dict(blocks=9, experts=16, table=17, topk=4, glu=True),
       "L3": dict(blocks=34, experts=8, table=9, topk=2, glu=False)}
PER_EXPERT = 4

HEAD_ORDER = np.array([h * E + e for e in range(E) for h in range(H)])


class Wall:

    def __init__(self):
        self.at, self.parts, self.n = {}, [], 0

    def put(self, name, array):
        array = np.asarray(array)
        if array.ndim == 1:
            array = array[:, None]
        self.at[name] = (self.n, array.shape[1], array.shape[0])
        self.parts.append(array)
        self.n += array.shape[1]

    def array(self, rows, dtype):
        out = np.zeros((rows, self.n), dtype)
        for (at, n, r), a in zip(self.at.values(), self.parts):
            out[:r, at:at + n] = a
        return out


def columns(n_rows, x):
    return np.asarray(x).reshape(-1, n_rows).T


def bf16_bits(constant):
    return (np.ascontiguousarray(constant).view(np.uint32) >> 16).astype(np.uint16)


def constants():
    f = Wall()
    f.put("ident", np.eye(P, dtype=np.float32))
    r, c = np.arange(P)[:, None], np.arange(P)[None, :]
    f.put("causal", (r <= c).astype(np.float32))
    block = np.zeros((P, H, VW), np.float32)
    for row in range(P):
        block[row, row % H, :] = 1.0
    f.put("block", block.reshape(P, H * VW))
    pick = np.zeros((2, P, 4 * E), np.float32)
    for j in range(4):
        for e in range(E):
            pick[0, 32 * j + e, j * E + e] = 1.0
            pick[1, 32 * j + E, j * E + e] = 1.0
    f.put("pick", pick[0])
    f.put("pick_sum", pick[1])
    f.put("ones", np.full((P, 1), 1.0 / P, np.float32))
    below = (np.arange(4)[None, :] < np.arange(4)[:, None]).astype(np.float32)
    f.put("before4", np.broadcast_to(below.reshape(1, 16), (P, 16)))
    for n in (8, 16):
        f.put(f"keep{n}", np.broadcast_to((np.arange(NT * n) % n > 0).astype(np.float32)[None], (P, NT * n)))
    b = Wall()
    b.put("ident", np.eye(P))
    q, k = r, c
    previous = np.where(k > q, 0.0, NEG)
    current = np.where(k <= q, 0.0, NEG)
    nothing = np.full((P, P), NEG)
    b.put("mask_q", np.concatenate([previous, current], 1))
    b.put("mask_k", np.tile(np.concatenate([previous.T, current.T], 1), 2))
    b.put("mask_k0", np.tile(np.concatenate([nothing, current.T], 1), 2))
    return f.array(P, np.float32), f.at, bf16_bits(b.array(P, np.float32)), b.at


def expanders():
    out = {}
    for name in ("L0", "L1"):
        m = MOE[name]
        t = m["table"]
        if name == "L0":
            owner = np.concatenate([np.repeat(np.arange(8), 176), np.full(352, 8), np.full(32, -1)])
        else:
            owner = np.concatenate([np.repeat(np.arange(16), 64), np.full(128, 16)])
        hot = (np.arange(t)[:, None] == owner[None, :])
        hot = np.concatenate([hot] * 3, 0).reshape(3 * t, m["blocks"], P)
        out[name] = bf16_bits(hot.transpose(1, 0, 2).reshape(m["blocks"] * 3 * t, P).astype(np.float32))
    return out


def lay_out(x):
    g = {k: np.asarray(v) for k, v in x.items()}
    w = {n: Wall() for n in ("L0", "L1", "L2", "L3")}
    rows = Wall()
    ho = HEAD_ORDER

    def qkv(wall, tag, wm, bv):
        wall.put(tag + "_wq", wm[:, 0:D][:, ho])
        wall.put(tag + "_wk", wm[:, D:2 * D][:, ho])
        wall.put(tag + "_wv", wm[:, 2 * D:])
        wall.put(tag + "_bq", bv[0:D][ho])
        wall.put(tag + "_bk", bv[D:2 * D][ho])
        rows.put(tag + "_bv", bv[2 * D:][None])

    a = w["L0"]
    qkv(a, "a", g["L0_attn_Wqkv_a"], g["L0_attn_bqkv_a"])
    qkv(a, "s", g["L0_attn_Wqkv_s"], g["L0_attn_bqkv_s"])
    for n in ("g1", "b1", "gm", "bm", "bp_a", "bo_s"):
        a.put(n, g["L0_attn_" + n])
    a.put("b1m", columns(P, g["L0_attn_b1m"]))
    a.put("Wp_a", g["L0_attn_Wp_a"])
    a.put("Wo_s", g["L0_attn_Wo_s"])
    a.put("Wo", g["L0_attn_Wo"])
    a.put("W1", g["L0_attn_W1"])
    a.put("W2", g["L0_attn_W2"].reshape(4, P, D).transpose(1, 0, 2).reshape(P, 4 * D))
    a.put("router0", np.concatenate([g["L0_ffn_gate_w"], g["L0_ffn_shared_expert_gate_w"]], 0).T)
    rows.put("bo", g["L0_attn_bo"][None])
    rows.put("b2m", g["L0_attn_b2m"][None])

    a = w["L1"]
    qkv(a, "l", g["L1_attn_qkv_w"].T, g["L1_attn_qkv_b"])
    a.put("gate_w", g["L1_attn_gate_w"].T[:, ho])
    a.put("gate_b", g["L1_attn_gate_b"][ho])
    a.put("ln_g", g["L1_attn_ln_g"])
    a.put("ln_b", g["L1_attn_ln_b"])
    a.put("proj_w", g["L1_attn_proj_w"].T)
    a.put("router1", g["L1_ffn_gate_w"].T)
    a.put("router1_b", np.broadcast_to(g["L1_ffn_gate_bias"][None], (P, 16)))
    rows.put("proj_b", g["L1_attn_proj_b"][None])

    a = w["L2"]
    for n in ("Wi", "Wf", "Wz", "Wo"):
        a.put(n, g["L2_attn_" + n].T)
    for n in ("bi", "bf", "bz", "bo"):
        a.put(n, np.tile(g["L2_attn_" + n], 2))
    a.put("Wp", np.tile(g["L2_attn_Wp"].T, (2, 1)))
    a.put("ln_w", g["L2_attn_ln_w"])
    a.put("ln_b", g["L2_attn_ln_b"])
    a.put("W_fc", g["L2_ffn_W_fc"].T)
    a.put("W_proj", g["L2_ffn_W_proj"].T.reshape(4, P, D).transpose(1, 0, 2).reshape(P, 4 * D))
    rows.put("bp", g["L2_attn_bp"][None])

    a = w["L3"]
    a.put("f_wq", g["L3_attn_wq"][:, ho])
    a.put("f_wk", g["L3_attn_wk"][:, ho])
    a.put("f_wv", g["L3_attn_wv"])
    a.put("f_bq", g["L3_attn_bq"][ho])
    a.put("f_bk", g["L3_attn_bk"][ho])
    a.put("wo", g["L3_attn_wo"])
    a.put("router3", g["L3_ffn_router_w"])
    a.put("router3_b", np.broadcast_to(g["L3_ffn_router_b"][None], (P, 8)))
    a.put("gate", np.concatenate([columns(P, g["L3_ffn_gate"].reshape(-1)), columns(P, g["L3_ffn_sgate"])], 1))
    a.put("b1", np.concatenate([columns(P, g["L3_ffn_b1"].reshape(-1)), columns(P, g["L3_ffn_sb1"])], 1))
    a.put("b2", np.concatenate([g["L3_ffn_b2"], g["L3_ffn_sb2"][None]], 0))
    a.put("shared_w", np.broadcast_to(g["L3_ffn_shared_weight"].reshape(1, 1), (P, 1)))
    a.put("ln_g3", np.broadcast_to(g["L3_ffn_ln_g"][None], (P, D)))
    a.put("ln_b3", np.broadcast_to(g["L3_ffn_ln_b"][None], (P, D)))
    rows.put("f_bv", g["L3_attn_bv"][None])
    rows.put("bo3", g["L3_attn_bo"][None])
    rows.put("ones", np.ones((1, P), np.float32))

    def blocks_in(m):
        return m.reshape(P, -1, P).transpose(1, 0, 2)

    def padded(m, n):
        out = np.zeros((m.shape[0], n), m.dtype)
        out[:, :m.shape[1]] = m
        return out

    streams = {}
    n0 = MOE["L0"]["blocks"] * P
    gu = g["L0_ffn_experts_gate_up"]
    gate = padded(np.concatenate([gu[:, :176].reshape(-1, D), g["L0_ffn_shared_gate_w"]], 0).T, n0)
    up = padded(np.concatenate([gu[:, 176:].reshape(-1, D), g["L0_ffn_shared_up_w"]], 0).T, n0)
    down = padded(np.concatenate([g["L0_ffn_experts_down"].transpose(1, 0, 2).reshape(D, -1),
                                  g["L0_ffn_shared_down_w"]], 1), n0)
    streams["L0"] = (np.concatenate([blocks_in(gate), blocks_in(up)], 2).reshape(-1, 2 * P), down.T)
    gate = np.concatenate([g["L1_ffn_Wg"].reshape(-1, D), g["L1_ffn_Ws_g"]], 0).T
    up = np.concatenate([g["L1_ffn_Wu"].reshape(-1, D), g["L1_ffn_Ws_u"]], 0).T
    down = np.concatenate([g["L1_ffn_Wd"].transpose(1, 0, 2).reshape(D, -1), g["L1_ffn_Ws_d"]], 1)
    streams["L1"] = (np.concatenate([blocks_in(gate), blocks_in(up)], 2).reshape(-1, 2 * P), down.T)
    w1 = np.concatenate([g["L3_ffn_w1"].transpose(1, 0, 2).reshape(D, -1), g["L3_ffn_sw1"]], 1)
    w2 = np.concatenate([g["L3_ffn_w2"].reshape(-1, D), g["L3_ffn_sw2"]], 0)
    streams["L3"] = (blocks_in(w1).reshape(-1, P), w2)

    x_tiles = g["L0_attn_x"].reshape(PASSES, NT, P, D).transpose(0, 2, 1, 3).reshape(PASSES * P, NT * D)
    arrays = {"x": np.concatenate([x_tiles, x_tiles[-P:]], 0)}
    at = {}
    for n, wall in w.items():
        arrays["w" + n] = wall.array(P, np.float32)
        at[n] = wall.at
    arrays["rows"] = rows.array(1, np.float32)
    at["rows"] = rows.at
    arrays["cf"], at["cf"], arrays["cb"], at["cb"] = constants()
    arrays["ones_rows"] = bf16_bits(np.ones((3, H * TOK), np.float32))
    for n, stream in streams.items():
        arrays["in" + n], arrays["down" + n] = stream
    for n, hot in expanders().items():
        arrays["hot" + n] = hot
    return {k: np.ascontiguousarray(v) for k, v in arrays.items()}, at


def unit_loop(eng, n, body):
    for u in range(4):
        body(u, u)
    last = (n - 1) // 4
    with eng.Fori(1, last) as i:
        for q in range(4):
            body(i * 4 + q, q)
    for u in range(4 * last, n):
        body(u, u % 4)


def program(nc, T, at, shapes, stop=99):
    with ExitStack() as ctx, ExitStack() as ctx_loop:
        def sb(name, shape, dt=F32):
            return ctx.enter_context(nc.sbuf_tensor(name, shape, dt))

        sems = {}

        def S(name):
            if name not in sems:
                sems[name] = phase["sems"].enter_context(nc.semaphore(name.replace(".", "_")))
            return sems[name]

        ONCE = {n: ctx.enter_context(nc.semaphore(n)) for n in
                ("x_first", "rows_in", "cf_in", "cb_in", "ones_in", "wall_L0", "wall_L1", "wall_L2", "wall_L3",
                 "column_zero", "zero_in", "v_ready", "half_ready", "stack_zero", "q_zero")}

        PS = ctx.enter_context(nc.psum_tensor("PS", [P, 8, 512], F32))
        X = sb("X", [P, NT, D])
        A = sb("A", [P, NT, D])
        A2 = sb("A2", [P, NT, D])
        AT = sb("AT", [P, TOK])
        NTT = sb("NTT", [P, TOK])
        T0 = sb("T0", [P, TOK])
        T1 = sb("T1", [P, TOK])
        T2 = sb("T2", [P, TOK])
        T3 = sb("T3", [P, TOK])
        OT = sb("OT", [P, TOK])
        QS = sb("QS", [P, H, TOK], BF16)
        KS = sb("KS", [P, H, TOK], BF16)
        V = sb("V", [P, NT, H, VW])
        BIG = sb("BIG", [P, GROUPS, TOK])
        PR = sb("PR", [P, 8, 512])
        SM = PR[:, 4:6, :]
        WALL = {n: sb("wall_" + n, [P, shapes["w" + n][1]]) for n in ("L0", "L1", "L2", "L3")}
        CF = sb("CF", [P, shapes["cf"][1]])
        CB = sb("CB", [P, shapes["cb"][1]], BF16)
        ROWS = sb("ROWS", [1, shapes["rows"][1]])
        GU = sb("GU", [P, 2, 2 * P])
        DN = sb("DN", [P, 2, P])
        HOT = sb("HOT", [51, 2, P], BF16)
        CT = sb("CT", [51, TOK], BF16)
        C32 = sb("C32", [17, TOK])
        GM = sb("GM", [P, NT])
        stats = sb("stats", [P, NT, 6])
        moments = sb("moments", [P, NT, 2])
        small = sb("small", [P, 8, NT])
        MX = sb("MX", [P, 2, 16])
        MXR = sb("MXR", [P, 2, 16])
        MP = sb("MP", [P, 2, 4, 3, 4], BF16)
        MR = sb("MR", [48, 512], BF16)
        CW = sb("CW", [P, NT, 17])
        CWR = sb("CWR", [P, NT, 17])
        CP = sb("CP", [P, NT, 3, 17], BF16)
        b1g = sb("b1g", [P, 34, 2])
        GB = sb("GB", [P, PER_EXPERT, 2])
        CE = sb("CE", [P, NT])
        zero = sb("zero", [1, 512], BF16)
        vec = sb("vec", [P, 4])

        def parts_of(which, i):
            n = 3 * which + i
            return BIG[:, n // 2, :].bitcast(BF16)[:, (n % 2) * TOK:(n % 2 + 1) * TOK]

        def w(layer, name, a=0, b=None):
            o, n, r = at[layer][name]
            return WALL[layer][0:r, o + a:o + (n if b is None else b)]

        def cf(name, a=0, b=None):
            o, n, r = at["cf"][name]
            return CF[:, o + a:o + (n if b is None else b)]

        def cb(name):
            o, n, r = at["cb"][name]
            return CB[:, o:o + n]

        def row(name):
            o, n, r = at["rows"][name]
            return ROWS[0:1, o:o + n]

        def row4(name):
            return row(name).unsqueeze(1).to_broadcast([1, 4, P])

        def half(h):
            return slice(HALF * h, HALF * (h + 1))

        def tile(t):
            return slice(P * t, P * (t + 1))

        def bank(i, n=1):
            return PS[:, i, :] if n == 1 else PS[:, i:i + n, :].rearrange("p a b -> p (a b)")

        def tok(buf):
            return buf[:, 0:TOK].rearrange("p (t d) -> p t d", t=NT)

        def flat(buf):
            return buf[:, :, :].rearrange("p t d -> p (t d)")

        with nc.Block() as once:
            @once.sync
            def _(sp):
                sp.dma_start(BIG[:, 3, :], T["x"][0:P, :]).then_inc(ONCE["x_first"], 16)
                sp.dma_start(WALL["L0"][:, :], T["wL0"]).then_inc(ONCE["wall_L0"], 16)
                sp.dma_start(ROWS[:, :], T["rows"]).then_inc(ONCE["rows_in"], 16)
                sp.dma_start(CF[:, :], T["cf"]).then_inc(ONCE["cf_in"], 16)
                sp.dma_start(CB[:, :], T["cb"]).then_inc(ONCE["cb_in"], 16)
                for n in ("L1", "L2", "L3"):
                    sp.dma_start(WALL[n][:, :], T["w" + n]).then_inc(ONCE["wall_" + n], 16)
                sp.wait_ge(ONCE["stack_zero"], 1)
                sp.dma_start(KS[M_ROW:M_ROW + 3, :, :].rearrange("p h t -> p (h t)"), T["ones_rows"]
                             ).then_inc(ONCE["ones_in"], 16)

            @once.vector
            def _(v):
                v.memset(QS[:, :, :].rearrange("p h t -> p (h t)").bitcast(F32), 0.0).then_inc(ONCE["q_zero"], 1)

            @once.scalar
            def _(act):
                act.wait_ge(ONCE["column_zero"], 1)
                k = KS[:, :, :].rearrange("p h t -> p (h t)").bitcast(F32)
                act.activation(k, small[:, 6, 0:1].to_broadcast([P, H * TOK // 2]), ACT.Copy
                               ).then_inc(ONCE["stack_zero"], 1)

            @once.gpsimd
            def _(g):
                g.memset(small[:, 6, :], 0.0).then_inc(ONCE["column_zero"], 1)
                g.memset(small[:, 7, :], -0.5).then_inc(ONCE["half_ready"], 1)
                g.memset(zero[:, :], 0.0).then_inc(ONCE["zero_in"], 1)
                g.memset(V[:, :, :, :], 0.0).then_inc(ONCE["v_ready"], 1)
                g.wait_ge(ONCE["v_ready"], 1)
                g.memset(V[:, :, :, E], 1.0).then_inc(ONCE["v_ready"], 1)

        NORMS = {
            "n0": (tok(BIG[:, 3, :]), True, [(A2, NTT, (w("L0", "g1"), w("L0", "b1")))]),
            "n0m": (tok(T0), False, [(tok(T1), T2, (w("L0", "gm"), w("L0", "bm")))]),
            "n0f": (X, False, [(A, AT, None)]),
            "n1": (X, True, [(A, AT, None), (A2, NTT, (w("L1", "ln_g"), w("L1", "ln_b")))]),
            "n1f": (X, False, [(A, AT, None)]),
            "n2": (X, True, [(A2, NTT, (w("L2", "ln_w"), w("L2", "ln_b")))]),
            "n2f": (X, False, [(A, AT, None)]),
            "n3": (X, False, [(A, NTT, None)]),
            "n3f": (X, False, [(A, AT, None)]),
        }

        PHASE_1 = ("n0", "n0m", "n0f", "n1", "n1f")
        NORM_AT = {k: i if i < len(PHASE_1) else i - len(PHASE_1) for i, k in enumerate(NORMS)}

        TURNED_AT = {k: 2 * sum(len(NORMS[j][2]) for j in NORMS if NORM_AT[j] < NORM_AT[k] and
                                (j in PHASE_1) == (k in PHASE_1)) for k in NORMS}

        RSTDS = {k: ("second", "first") if k == "n0" else ("first", "second") if k == "n1" else
                 ("second",) if k == "n2" else ("first",) for k in NORMS}
        RSTD_AT = {k: 2 * sum(len(RSTDS[j]) for j in NORMS if NORM_AT[j] < NORM_AT[k] and
                              (j in PHASE_1) == (k in PHASE_1)) for k in NORMS}

        def wait_norm(eng, k, n):
            eng.wait_ge(S("norm_in"), TURNED_AT[k] + n)

        def vector_norm(v, k, before=None):
            src = NORMS[k][0]
            for hf in range(2):
                if before:
                    before(hf)
                for t in range(TPB * hf, TPB * (hf + 1)):
                    v.bn_stats(stats[:, t, :], src[:, t, :]).then_inc(S("norm_stats"), 1)
                v.wait_ge(S("norm_stats"), NT * NORM_AT[k] + TPB * (hf + 1))
                for t in range(TPB * hf, TPB * (hf + 1)):
                    v.bn_aggr(moments[:, t, :], stats[:, t, :]).then_inc(S("norm_moments"), 1)

            for pos, which in enumerate(RSTDS[k]):
                dst = A2 if which == "second" else tok(T1) if k == "n0m" else A
                rstd = 5 if which == "second" else 1
                for t in range(NT):
                    if t % TPB == 0:
                        v.wait_ge(S("norm_rstd"), RSTD_AT[k] + len(RSTDS[k]) * (t // TPB) + pos + 1)
                    v.tensor_scalar(dst[:, t, :], src[:, t, :], moments[:, t, 0:1], small[:, rstd, t:t + 1],
                                    ALU.subtract, ALU.mult).then_inc(S(k + "_" + which), 1)

        def gpsimd_norm(g, k, chain):
            for hf in range(2):
                ts = slice(TPB * hf, TPB * (hf + 1))
                g.wait_ge(S("norm_moments"), NT * NORM_AT[k] + TPB * (hf + 1))
                var = moments[:, ts, 1]
                for which in RSTDS[k]:
                    if which == "first":
                        chain(g.tensor_scalar(small[:, 0, ts], var, EPS, None, ALU.add))
                        last = g.tensor_tensor(small[:, 1, ts], small[:, 0, ts], small[:, 7, ts], ALU.pow)
                    else:
                        chain(g.tensor_scalar(small[:, 4, ts], var, 1.0 + EPS, EPS * EPS, ALU.mult, ALU.add))
                        last = g.tensor_tensor(small[:, 5, ts], small[:, 4, ts], small[:, 7, ts], ALU.pow)
                    last.then_inc(S("norm_rstd"), 1)

        def tensor_norm(pe, k):
            for s, (src, _, affine) in enumerate(NORMS[k][2]):
                for hf in range(2):
                    pe.wait_ge(S(k + ("_second" if src is A2 else "_first")), TPB * (hf + 1))
                    for t in range(TPB):
                        last = pe.transpose(PS[:, 2 * s + hf, tile(t)], src[:, TPB * hf + t, :], cf("ident"))
                    last.then_inc(S("norm_turned"), 1)

        def scalar_ready(link, fn):
            link(link.eng.activation(vec[:, 1:2], small[:, 7, 0:1], fn))

        def scalar_norm(act, k):
            for s, (_, dst, affine) in enumerate(NORMS[k][2]):
                for hf in range(2):
                    act.wait_ge(S("norm_turned"), TURNED_AT[k] + 2 * s + hf + 1)
                    if affine is None:
                        i = act.activation(dst[:, half(hf)], bank(2 * s + hf), ACT.Copy)
                    else:
                        i = act.activation(dst[:, half(hf)], bank(2 * s + hf), ACT.Identity,
                                           bias=affine[1], scale=affine[0])
                    i.then_inc(S("norm_in"), 1)

        LAYER = {"a": "L0", "s": "L0", "l": "L1", "f": "L3"}
        FROM = {"a": "n0", "s": "n0", "l": "n1", "f": "n3"}
        LINEAR = {"s": (SCALE, 1.0, 1e-4, 1e-6), "l": (None, None, 0.0, 1e-5)}

        def tensor_qkv(pe, a):
            lay = LAYER[a]
            pe.wait_ge(ONCE["wall_" + lay], 16)
            if a == "a":
                pe.wait_ge(ONCE["rows_in"], 16)
            if a == "s":
                pe.wait_ge(S("a.ot"), 2)
            if a == "l":
                for hf in range(2):
                    wait_norm(pe, "n1", hf + 1)
                    pe.matmul(bank(4 + hf), w(lay, "gate_w"), AT[:, half(hf)], start=True, stop=True
                              ).then_inc(S("l.gate"), 1)

            def heads(hf):
                wait_norm(pe, FROM[a], hf + (3 if a == "l" else 1))
                for i, m in enumerate(("_wq", "_wk")):
                    pe.matmul(bank(2 * i + hf), w(lay, a + m), NTT[:, half(hf)], start=True, stop=True
                              ).then_inc(S(a + ".qk"), 1)

            def gate_mean(hf):
                pe.wait_ge(S("l.gate_sig"), hf + 1)
                for t in range(TPB):
                    last = pe.matmul(PS[:, 6 + hf, t:t + 1], T2[:, tile(TPB * hf + t)], cf("ones"),
                                     start=(t == 0), stop=True, skip_group_check=True)
                last.then_inc(S("l.gate_mean"), 1)

            def gate_row(hf):
                pe.wait_ge(S("l.gate_inverse"), hf + 1)
                for t in range(TPB):
                    last = pe.transpose(PS[:, 6 + hf, tile(t)], GM[:, TPB * hf + t:TPB * hf + t + 1]
                                        .to_broadcast([P, P]), cf("ident"))
                last.then_inc(S("l.gate_row"), 1)

            def values_of(hf):
                pe.matmul(bank(4 + hf), row("ones"), row4(a + "_bv"), start=True, stop=True, skip_group_check=True)
                for t in range(TPB):
                    last = pe.matmul(PS[:, 4 + hf, tile(t)], NTT[:, tile(TPB * hf + t)], w(lay, a + "_wv"),
                                     start=False, stop=True, skip_group_check=True)
                last.then_inc(S(a + ".v"), 1)

            if a == "l":
                heads(0)
                gate_mean(0)
                gate_mean(1)
                gate_row(0)
                heads(1)
                values_of(0)
                gate_row(1)
                values_of(1)
            else:
                for hf in range(2):
                    heads(hf)
                    values_of(hf)

        def vector_v(v, a, hf):
            v.wait_ge(S(a + ".v"), hf + 1)
            if a == "a":
                v.wait_ge(ONCE["v_ready"], 2)
            v.tensor_copy(V[:, TPB * hf:TPB * (hf + 1), :, 0:E],
                          bank(4 + hf).rearrange("p (t h e) -> p t h e", t=TPB, h=H)
                          ).then_inc(S(a + ".v_in"), 1)

        def scalar_qk(act, a):
            lay = LAYER[a]
            if a == "l":
                for hf in range(2):
                    act.wait_ge(S("l.gate"), hf + 1)
                    act.activation(T2[:, half(hf)], bank(4 + hf), ACT.Sigmoid, bias=w("L1", "gate_b")
                                   ).then_inc(S("l.gate_sig"), 1)
            def made(hf):
                for i, dst in enumerate((T0, T1)):
                    n, dst, e, src = 2 * hf + i, dst[:, half(hf)], (T2, T3)[i][:, half(hf)], bank(2 * i + hf)
                    bias = w(lay, a + ("_bq", "_bk")[i])
                    if a == "l":
                        act.wait_ge(S("l.z"), n + 1)
                        act.activation(e, dst, ACT.Exp).then_inc(S("l.e"), 1)
                        act.wait_ge(S("l.e"), n + 1)
                        act.activation(dst, dst, ACT.Relu).then_inc(S("l.relu"), 1)
                    elif a == "s":
                        act.wait_ge(S("s.qk"), n + 1)
                        if i == 0:
                            act.wait_ge(S("s.bias"), 1)
                            bias = vec[:, 2:3]
                        act.activation(e, src, ACT.Exp, bias=bias, scale=SCALE if i == 0 else 1.0
                                       ).then_inc(S("s.e"), 1)
                        act.activation(dst, src, ACT.Relu, bias=bias, scale=SCALE if i == 0 else 1.0
                                       ).then_inc(S("s.relu"), 1)
                    else:
                        act.wait_ge(S(a + ".qk"), n + 1)
                        act.activation(dst, src, ACT.Identity, bias=bias).then_inc(S(a + ".f"), 1)
                        act.activation(parts_of(i, 0)[:, half(hf)], src, ACT.Identity, bias=bias
                                       ).then_inc(S(a + ".p0"), 1)

            def first_parts(hf):
                for i, dst in enumerate((T0, T1)):
                    act.wait_ge(S(a + ".f"), 2 * hf + i + 1)
                    act.activation(parts_of(i, 0)[:, half(hf)], dst[:, half(hf)], ACT.Copy
                                   ).then_inc(S(a + ".p0"), 1)

            def second_parts(hf):
                for i in range(2):
                    act.wait_ge(S(a + ".r"), 2 * hf + i + 1)
                    act.activation(parts_of(i, 1)[:, half(hf)], (T2, T3)[i][:, half(hf)], ACT.Copy
                                   ).then_inc(S(a + ".p1"), 1)

            if a in LINEAR:
                made(0)
                first_parts(0)
                made(1)
                second_parts(0)
                first_parts(1)
                second_parts(1)
            else:
                for hf in range(2):
                    made(hf)
                    second_parts(hf)

        def vector_qk(v, a, link):
            lay = LAYER[a]
            if a == "s":
                v.tensor_scalar(vec[:, 2:3], w("L0", "s_bq"), SCALE, None, ALU.mult).then_inc(S("s.bias"), 1)
            def gated(hf):
                hs, ts = half(hf), slice(TPB * hf, TPB * (hf + 1))
                v.wait_ge(S("l.gate_mean"), hf + 1)
                link(v.tensor_scalar(GM[:, ts], PS[:, 6 + hf, 0:TPB], EPS, None, ALU.add))
                v.reciprocal(GM[:, ts], GM[:, ts]).then_inc(S("l.gate_inverse"), 1)
                v.wait_ge(S("l.gate_row"), hf + 1)
                link(v.tensor_tensor(T3[:, hs], bank(6 + hf), T2[:, hs], ALU.mult))
                for i, (dst, bias) in enumerate(((T0, "_bq"), (T1, "_bk"))):
                    v.wait_ge(S("l.qk"), 2 * hf + i + 1)
                    v.scalar_tensor_tensor(out=dst[:, hs], in0=bank(2 * i + hf), scalar=w(lay, a + bias),
                                           in1=T3[:, hs], op0=ALU.add, op1=ALU.mult).then_inc(S("l.z"), 1)

            def elu(hf):
                hs = half(hf)
                for i, dst in enumerate((T0, T1)):
                    e = (T2, T3)[i][:, hs]
                    if a == "s":
                        v.wait_ge(S("s.e"), 2 * hf + i + 1)
                        link(v.tensor_scalar(e, e, 1.0, LINEAR[a][2], ALU.min, ALU.add))
                    v.wait_ge(S(a + ".relu"), 2 * hf + i + 1)
                    v.scalar_tensor_tensor(out=dst[:, hs], in0=e, scalar=1.0 + LINEAR[a][2], in1=dst[:, hs],
                                           op0=ALU.min, op1=ALU.add).then_inc(S(a + ".f"), 1)
                v.wait_ge(S(a + ".f"), 2 * hf + 2)

            def rest(hf):
                hs = half(hf)
                for i, (src, left) in enumerate(((T0, T2), (T1, T3))):
                    v.wait_ge(S(a + ".p0"), 2 * hf + i + 1)
                    v.tensor_tensor(left[:, hs], src[:, hs], parts_of(i, 0)[:, hs], ALU.subtract
                                    ).then_inc(S(a + ".r"), 1)

            def third_parts(hf):
                hs = half(hf)
                for i, left in enumerate((T2, T3)):
                    v.wait_ge(S(a + ".p1"), 2 * hf + i + 1)
                    v.tensor_tensor(parts_of(i, 2)[:, hs], left[:, hs], parts_of(i, 1)[:, hs], ALU.subtract
                                    ).then_inc(S(a + ".p2"), 1)

            if a == "l":
                gated(0)
                gated(1)
            if a in LINEAR:
                elu(0)
                rest(0)
                elu(1)
                vector_v(v, a, 0)
                third_parts(0)
                rest(1)
                vector_v(v, a, 1)
                third_parts(1)
            else:
                for hf in range(2):
                    rest(hf)
                    vector_v(v, a, hf)
                    third_parts(hf)

        STACK_DMAS = 16 * (len(Q_PARTS) + len(K_PARTS))

        def sync_stacks(sp, a):
            sp.wait_ge(ONCE["stack_zero"], 1)
            sp.wait_ge(ONCE["q_zero"], 1)
            for hf in range(2):
                for part in range(3):
                    for i, (dst, groups) in enumerate(((QS, Q_PARTS), (KS, K_PARTS))):
                        sp.wait_ge(S(a + f".p{part}"), 2 * hf + i + 1)
                        for g, p in enumerate(groups):
                            if p == part:
                                sp.dma_start(dst[E * g:E * (g + 1), :, half(hf)], parts_of(i, part)[:, half(hf)]
                                             ).then_inc(S(a + f".stacked{hf}"), 16)

        def plan(a):
            u = 8 if a == "a" else 16
            return dict(units=u, per=2, lead=18, turn=4) if a == "a" else dict(units=u, per=4, lead=24, turn=2)

        def score_1(pe, a, n):
            pl = plan(a)
            G, u = divmod(n, pl["units"])
            b = n % 3
            if n >= 3:
                pe.wait_ge(S(a + ".max"), n - 2)
            if a == "a":
                lo = 1 if G % TPB == 0 else 0
                for j in range(2):
                    h = 2 * u + j
                    last = pe.matmul(PS[:, b, 256 * j + 128 * lo:256 * (j + 1)], QS[0:STACK, h, tile(G)],
                                     KS[0:STACK, h, P * (G - 1 + lo):P * (G + 1)], start=True, stop=True,
                                     skip_group_check=True)
            else:
                bt, g = divmod(G, GROUPS)
                qt, j = divmod(u, 4)
                last = pe.matmul(bank(b), QS[0:STACK, 4 * g + j, tile(TPB * bt + qt)],
                                 KS[0:STACK, 4 * g + j, half(bt)], start=True, stop=True)
            last.then_inc(S(a + ".s1"), 1)

        def max_1(v, a, n):
            pl = plan(a)
            G, u = divmod(n, pl["units"])
            v.wait_ge(S(a + ".s1"), n + 1)
            if a == "a":
                lo = P if G % TPB == 0 else 0
                if n >= 2:
                    v.wait_ge(S(a + ".max"), n - 1)
                for j in range(2):
                    at = 512 * (n % 2) + 256 * j
                    last = v.tensor_tensor_reduce(out=AT[:, at + lo:at + 256],
                                                  in0=PS[:, n % 3, 256 * j + lo:256 * (j + 1)],
                                                  in1=cb("mask_q")[:, lo:256], scale=1.0, scalar=-3e38,
                                                  op0=ALU.add, op1=ALU.max,
                                                  accum_out=MX[:, G % 2, 2 * u + j:2 * u + j + 1])
                last.then_inc(S(a + ".max"), 1)
            else:
                v.tensor_reduce(MX[:, G % 2, u:u + 1], bank(n % 3), AX.X, ALU.max, negate=True
                                ).then_inc(S(a + ".max"), 1)

        def max_parts(v, a, G, link):
            pl = plan(a)
            v.wait_ge(S(a + ".max"), (G + 1) * pl["units"])
            if G >= 2:
                v.wait_ge(S(a + ".m_turned"), G - 1)
            m, left = MX[:, G % 2, :], MXR[:, G % 2, :]
            if a == "a":
                out = [MP[:, G % 2, :, :, :].rearrange("p a b c -> p (a b c)")[:, 16 * i:16 * (i + 1)]
                       for i in range(3)]
            else:
                m, left = (y.rearrange("p (t h) -> p t h", t=4) for y in (m, left))
                out = [MP[:, G % 2, :, i, :] for i in range(3)]
            if a == "a":
                link(v.tensor_scalar(out[0], m, -1.0, None, ALU.mult))
                link(v.scalar_tensor_tensor(out=left, in0=m, scalar=-1.0, in1=out[0], op0=ALU.mult, op1=ALU.subtract))
            else:
                link(v.tensor_copy(out[0], m))
                link(v.tensor_tensor(left, m, out[0], ALU.subtract))
            link(v.tensor_copy(out[1], left))
            v.tensor_tensor(out[2], left, out[1], ALU.subtract).then_inc(S(a + ".m_parts"), 1)

        def turn_max(pe, a, G):
            pe.wait_ge(S(a + ".m_parts"), G + 1)
            if G >= 1:
                pe.wait_ge(S(a + ".m_rows"), G)
            out = bank(7).bitcast(BF16)
            mp = MP[:, G % 2, :, :, :].rearrange("p a b c -> p (a b c)")
            if a == "a":
                last = pe.transpose(out[0:48, 0:P], mp, cb("ident"))
            else:
                for t in range(4):
                    last = pe.transpose(out[0:12, tile(t)], mp[:, 12 * t:12 * (t + 1)], cb("ident"))
            last.then_inc(S(a + ".m_turned"), 1)

        def copy_max(act, a, G):
            act.wait_ge(S(a + ".m_turned"), G + 1)
            if G >= 1:
                act.wait_ge(S(a + ".m_in"), 16 * G)
            r, n = (48, P) if a == "a" else (12, 512)
            act.activation(MR[0:r, 0:n], bank(7).bitcast(BF16)[0:r, 0:n], ACT.Copy
                           ).then_inc(S(a + ".m_rows"), 1)

        def sync_max(sp, a):
            for G in range(8):
                sp.wait_ge(S(a + ".m_rows"), G + 1)
                if a == "a":
                    sp.dma_start(QS[M_ROW:M_ROW + 3, :, tile(G)], MR[0:48, 0:P]).then_inc(S(a + ".m_in"), 16)
                else:
                    bt, g = divmod(G, GROUPS)
                    sp.dma_start(QS[M_ROW:M_ROW + 3, 4 * g:4 * g + 4, half(bt)], MR[0:12, :]
                                 ).then_inc(S(a + ".m_in"), 16)

        def score_2(pe, a, n):
            pl = plan(a)
            G, u = divmod(n, pl["units"])
            b = 3 + n % 3
            if u == 0:
                pe.wait_ge(S(a + ".m_in"), 16 * (G + 1))
            if n >= 3:
                pe.wait_ge(S(a + ".exp"), n - 2)
            if a == "a":
                first = G % TPB == 0
                pe.matmul(bank(b), cb("ident"), cb("mask_k0" if first else "mask_k"), start=True, stop=True, skip_group_check=True)
                for j in range(2):
                    h = 2 * u + j
                    for c in range(1 if first else 0, 2):
                        last = pe.matmul(PS[:, b, 256 * j + 128 * c:256 * j + 128 * (c + 1)],
                                         KS[:, h, tile(G - 1 + c)], QS[:, h, tile(G)],
                                         start=False, stop=True, skip_group_check=True)
            else:
                bt, g = divmod(G, GROUPS)
                kt, j = divmod(u, 4)
                last = pe.matmul(bank(b), KS[:, 4 * g + j, tile(TPB * bt + kt)],
                                 QS[:, 4 * g + j, half(bt)], start=True, stop=True)
            last.then_inc(S(a + ".s2"), 1)

        def exp_2(act, a, n):
            pl = plan(a)
            act.wait_ge(S(a + ".s2"), n + 1)
            if n >= 8:
                act.wait_ge(S(a + ".pv"), (n - 8) // pl["per"] + 1)
            act.activation(PR[:, n % 8, :], bank(3 + n % 3), ACT.Exp, scale=SCALE).then_inc(S(a + ".exp"), 1)

        def values(pe, a, i):
            pl = plan(a)
            per = pl["per"]
            G, k = divmod(i, pl["units"] // per)
            pe.wait_ge(S(a + ".exp"), (i + 1) * per)
            if i == 0:
                pe.wait_ge(S(a + ".v_in"), 2)
            if k == 0 and G >= 1:
                pe.wait_ge(S(a + ".out"), G)
            if a == "a":
                first = G % TPB == 0
                for c in range(1 if first else 0, 2):
                    for j in range(4):
                        u = i * per + j // 2
                        last = pe.matmul(PS[32 * j:32 * j + 32, 6, tile(k)], V[:, G - 1 + c, 4 * k + j, :],
                                         PR[:, u % 8, 256 * (j % 2) + 128 * c:256 * (j % 2) + 128 * (c + 1)],
                                         start=(c == 1 if first else c == 0), stop=(c == 1),
                                         tile_position=(0, 32 * j))
            else:
                bt, g = divmod(G, GROUPS)
                for j in range(4):
                    last = pe.matmul(PS[32 * j:32 * j + 32, 6, :], V[:, TPB * bt + k, 4 * g + j, :],
                                     PR[:, (i * per + j) % 8, :], start=(k == 0), stop=(k == 3),
                                     tile_position=(0, 32 * j))
            last.then_inc(S(a + ".pv"), 1)

        def copy_out(act, a, G):
            pl = plan(a)
            act.wait_ge(S(a + ".pv"), (G + 1) * (pl["units"] // pl["per"]))
            if G == 0:
                act.wait_ge(S(a + ".stacked0"), STACK_DMAS)
                act.wait_ge(S(a + ".stacked1"), STACK_DMAS)
                if a == "a":
                    act.wait_ge(S("x_in"), 16)
            if a == "a":
                i = act.activation(BIG[:, :, tile(G)], bank(6).rearrange("p (g q) -> p g q", g=GROUPS), ACT.Copy)
            else:
                bt, g = divmod(G, GROUPS)
                i = act.activation(BIG[:, g, half(bt)], bank(6), ACT.Copy)
            i.then_inc(S(a + ".out"), 1)

        def steps(a):
            pl = plan(a)
            n, u = 8 * pl["units"], pl["units"]
            for s in range(-pl["lead"], n):
                one = s + pl["lead"]
                turn = one // u - 1 if one % u == pl["turn"] and one >= u and one // u <= 8 else None
                yield s, (one if one < n else None), turn

        def tensor_softmax(pe, a):
            pl = plan(a)
            pe.wait_ge(S(a + ".p0"), 4)
            pe.wait_ge(S(a + ".stacked0"), STACK_DMAS)
            pe.wait_ge(ONCE["ones_in"], 16)
            pe.wait_ge(ONCE["cb_in"], 16)
            for s, one, turn in steps(a):
                if one == 4 * pl["units"]:
                    pe.wait_ge(S(a + ".stacked1"), STACK_DMAS)
                if one is not None:
                    score_1(pe, a, one)
                if turn is not None:
                    turn_max(pe, a, turn)
                if s >= 0:
                    score_2(pe, a, s)
                    if s % pl["per"] == pl["per"] - 1 and s >= pl["per"]:
                        values(pe, a, s // pl["per"] - 1)
                if s == 7 * pl["units"] + 1:
                    tensor_gather(pe, a, 0)
            values(pe, a, 8 * pl["units"] // pl["per"] - 1)
            tensor_gather(pe, a, 1)

        def scalar_softmax(act, a):
            pl = plan(a)
            for s, _, turn in steps(a):
                if turn is not None:
                    copy_max(act, a, turn)
                if s >= 0:
                    exp_2(act, a, s)
                    if s % pl["units"] == pl["per"] + 1 and s >= pl["units"]:
                        copy_out(act, a, s // pl["units"] - 1)
            copy_out(act, a, 7)

        def vector_softmax(v, a, link):
            pl = plan(a)
            for n in range(8 * pl["units"]):
                max_1(v, a, n)
                if n % pl["units"] == pl["units"] - 1:
                    max_parts(v, a, n // pl["units"], link)
            for hf in range(2):
                vector_gather(v, a, hf, link)

        def tensor_linear(pe, a):
            def turn_k(hf):
                pe.wait_ge(S(a + ".v_in"), hf + 1)
                pe.wait_ge(S(a + ".f"), 2 * hf + 2)
                for t in range(TPB):
                    last = pe.transpose(PS[:, 4 + hf, tile(t)], T1[:, tile(TPB * hf + t)], cf("ident"))
                last.then_inc(S(a + ".k_turned"), 1)

            turn_k(0)
            pe.wait_ge(S(a + ".p0"), 4)
            pe.wait_ge(S(a + ".stacked0"), STACK_DMAS)

            def products(n, g):
                i = GROUPS * n + g
                if i == GROUPS * TPB:
                    pe.wait_ge(S(a + ".stacked1"), STACK_DMAS)
                if i >= 2:
                    pe.wait_ge(S(a + ".masked"), i - 1)
                for j in range(4):
                    h = 4 * g + j
                    last = pe.matmul(PS[:, i % 2, tile(j)], KS[0:STACK, h, tile(n)], QS[0:STACK, h, tile(n)],
                                     start=True, stop=True)
                last.then_inc(S(a + ".s"), 1)

            def through(n, g):
                i = GROUPS * n + g
                o = 2 + n % 2
                t = n % TPB
                if g == 0 and n >= 2:
                    pe.wait_ge(S(a + ".out"), n - 1)
                if t:
                    if g == 0:
                        pe.wait_ge(S(a + ".state_in"), n - n // TPB)
                    pe.matmul(PS[:, o, tile(g)], SM[:, n % 2, tile(g)], T0[:, tile(n)], start=True, stop=True, skip_group_check=True)
                pe.wait_ge(S(a + ".masked"), i + 1)
                for j in range(4):
                    last = pe.matmul(PS[32 * j:32 * j + 32, o, tile(g)], V[:, n, 4 * g + j, :],
                                     PR[:, i % 4, tile(j)], start=(t == 0), stop=True,
                                     tile_position=(0, 32 * j), skip_group_check=True)
                last.then_inc(S(a + ".pv"), 1)

            def state(n):
                t = n % TPB
                if t == 0:
                    pe.wait_ge(S(a + ".k_in"), n // TPB + 1)
                if n // TPB or t:
                    pe.wait_ge(S(a + ".state_in"), n - n // TPB)
                pe.matmul(bank(4), T2[:, tile(n)], V[:, n, :, :].rearrange("p h c -> p (h c)"),
                          start=(t == 0), stop=True, skip_group_check=True
                          ).then_inc(S(a + ".state"), 1)

            products(0, 0)
            for n in range(NT):
                if n % TPB < TPB - 1:
                    state(n)
                for g in range(GROUPS):
                    i = GROUPS * n + g + 1
                    if i < GROUPS * NT:
                        products(*divmod(i, GROUPS))
                    through(n, g)
                if n == 0:
                    turn_k(1)
                if n == TPB:
                    if a == "s":
                        pe.wait_ge(S("a.sum"), 1)
                    tensor_gather(pe, a, 0)
            tensor_gather(pe, a, 1)

        def vector_linear(v, a, link):
            def k_turned(hf):
                v.wait_ge(S(a + ".k_turned"), hf + 1)
                v.wait_ge(S(a + ".p2"), 4)
                v.tensor_copy(T2[:, half(hf)], bank(4 + hf)).then_inc(S(a + ".k_in"), 1)

            k_turned(0)
            mask = cf("causal").unsqueeze(1).to_broadcast([P, 4, P])
            for n in range(NT):
                if n % TPB < TPB - 1:
                    v.wait_ge(S(a + ".state"), n - n // TPB + 1)
                    if n >= 1:
                        v.wait_ge(S(a + ".pv"), GROUPS * n)
                    v.tensor_tensor(SM[:, (n + 1) % 2, :], bank(4), cf("block"), ALU.mult
                                    ).then_inc(S(a + ".state_in"), 1)
                for g in range(GROUPS):
                    i = GROUPS * n + g
                    v.wait_ge(S(a + ".s"), i + 1)
                    if i >= 4:
                        v.wait_ge(S(a + ".pv"), i - 3)
                    v.tensor_tensor(PR[:, i % 4, :].rearrange("p (j q) -> p j q", j=4),
                                    bank(i % 2).rearrange("p (j q) -> p j q", j=4), mask, ALU.mult
                                    ).then_inc(S(a + ".masked"), 1)
                    if n == 1 and g == 1:
                        k_turned(1)
                    if n in (TPB + 1, TPB + 2) and g % 2:
                        vector_invert(v, a, 0, tile(2 * (n - TPB - 1) + g // 2), link)
                    if n == TPB + 3 and g == 1:
                        vector_divide(v, a, 0)
            vector_gather(v, a, 1, link)

        def scalar_linear(act, a):
            act.wait_ge(S(a + ".stacked0"), STACK_DMAS)
            act.wait_ge(S(a + ".stacked1"), STACK_DMAS)
            for n in range(NT):
                act.wait_ge(S(a + ".pv"), GROUPS * (n + 1))
                act.activation(BIG[:, :, tile(n)], bank(2 + n % 2).rearrange("p (g q) -> p g q", g=GROUPS),
                               ACT.Copy).then_inc(S(a + ".out"), 1)
                if n == TPB:
                    scalar_denominators(act, a, 0)
            scalar_denominators(act, a, 1)

        def gather_banks(a, hf):
            return (0, 1) if a in LINEAR and hf else (6, 7) if a in LINEAR else (2 * hf, 2 * hf + 1)

        def tensor_gather(pe, a, hf):
            pe.wait_ge(S(a + ".out"), 4 * (hf + 1))
            if a in LINEAR:
                if hf:
                    pe.wait_ge(S(a + ".masked"), GROUPS * NT)
            else:
                pe.wait_ge(S(a + ".exp" if hf else a + ".max"), 8 * plan(a)["units"])
            for b, pick in zip(gather_banks(a, hf), ("pick", "pick_sum")):
                for g in range(GROUPS):
                    last = pe.matmul(PS[32 * g:32 * g + 32, b, :], cf(pick), BIG[:, g, half(hf)],
                                     start=True, stop=True, tile_position=(0, 32 * g))
            last.then_inc(S(a + ".gathered"), 1)

        def scalar_denominators(act, a, hf):
            act.wait_ge(S(a + ".gathered"), hf + 1)
            act.activation(T3[:, half(hf)], bank(gather_banks(a, hf)[1]), ACT.Copy, bias=LINEAR[a][3]
                           ).then_inc(S(a + ".den"), 1)

        def vector_invert(v, a, hf, cols, link):
            if a in LINEAR:
                v.wait_ge(S(a + ".den"), hf + 1)
                src = T3[:, half(hf)][:, cols]
            else:
                v.wait_ge(S(a + ".gathered"), hf + 1)
                src = bank(gather_banks(a, hf)[1])[:, cols]
            link(v.reciprocal(T3[:, half(hf)][:, cols], src))

        def vector_divide(v, a, hf):
            v.tensor_tensor(OT[:, half(hf)], bank(gather_banks(a, hf)[0]), T3[:, half(hf)], ALU.mult
                            ).then_inc(S(a + ".ot"), 1)

        def vector_gather(v, a, hf, link):
            vector_invert(v, a, hf, slice(0, HALF), link)
            vector_divide(v, a, hf)

        def tensor_back(pe, name, bias, lhs, rhs, depth=1, ready=None):
            for hf in range(2):
                if ready:
                    ready(hf)
                if bias:
                    pe.matmul(bank(4 + hf), row("ones"), row4(bias), start=True, stop=True, skip_group_check=True)
                for t in range(TPB):
                    for k in range(depth):
                        last = pe.matmul(PS[:, 4 + hf, tile(t)], lhs(k, TPB * hf + t), rhs(k, TPB * hf + t),
                                         start=(not bias and t == 0 and k == 0), stop=True,
                                         skip_group_check=True)
                last.then_inc(S(name), 1)

        def vector_back(v, name, dst, other, link, hf):
            v.wait_ge(S(name), hf + 1)
            ts = slice(TPB * hf, TPB * (hf + 1))
            link(v.tensor_tensor(dst[:, ts, :], bank(4 + hf).rearrange("p (t d) -> p t d", t=TPB),
                                 other[:, ts, :], ALU.add))

        FFN = {"L0": "n0f", "L1": "n1f", "L3": "n3f"}

        def sync_experts(sp, m):
            c = MOE[m]
            gu, dn, t3 = T["in" + m], T["down" + m], 3 * c["table"]
            wide = 2 * P if c["glu"] else P

            def load(b, s):
                sp.dma_start(GU[:, s, 0:wide], gu[bass.ds(b * P, P), :]).then_inc(S(f"{m}.gu{s}"), 16)
                if c["glu"]:
                    sp.dma_start(HOT[0:t3, s, :], T["hot" + m][bass.ds(b * t3, t3), :]
                                 ).then_inc(S(f"{m}.gu{s}"), 16)

            def load_down(b, s):
                sp.dma_start(DN[:, s, :], dn[bass.ds(b * P, P), :]).then_inc(S(f"{m}.dn{s}"), 16)

            for s in range(2):
                load(s, s)
                load_down(s, s)
            pairs = c["blocks"] // 2
            with sp.Fori(1, pairs) as i:
                for s in range(2):
                    sp.wait_ge(S(m + ".front"), i * 4 + (2 * s - 2))
                    load(i * 2 + s, s)
                    sp.wait_ge(S(m + ".down"), i * 4 + (2 * s - 2))
                    load_down(i * 2 + s, s)
            if c["blocks"] % 2:
                sp.wait_ge(S(m + ".front"), 4 * pairs - 2)
                load(2 * pairs, 0)
                sp.wait_ge(S(m + ".down"), 4 * pairs - 2)
                load_down(2 * pairs, 0)

        def tensor_router(pe, m):
            NR = {"L0": 9, "L1": 16, "L3": 8}[m]
            for t in range(NT):
                if t % TPB == 0:
                    wait_norm(pe, FFN[m], t // TPB + 1)
                last = pe.matmul(PS[:, 7, 32 * t:32 * t + NR], AT[:, tile(t)], w(m, "router" + m[1]),
                                 start=(t == 0), stop=True, skip_group_check=True)
            last.then_inc(S(m + ".logits"), 1)

        def tensor_experts(pe, m):
            c = MOE[m]
            units, t3, E1 = 2 * c["blocks"], 3 * c["table"], c["table"]
            tensor_router(pe, m)
            for hf in range(2):
                pe.matmul(bank(6 if hf == 0 else 5), zero[:, 0:P], zero[:, :], start=True, stop=True,
                          skip_group_check=True)

            G0 = (0, 2)
            W0 = (4, 7)

            def products(n, q):
                s = (q // 2) % 2
                hf = q % 2
                if q % 2 == 0:
                    if isinstance(n, int):
                        pe.wait_ge(S(f"{m}.gu{s}"), 32 * (n // 4 + 1))
                    else:
                        i4, _ = n_parts[0]
                        pe.wait_ge(S(f"{m}.gu{s}"), i4)
                if not (isinstance(n, int) and n < 2):
                    pe.wait_ge(S(m + ".hid"), n - 1)
                pe.matmul(bank(G0[hf]), GU[:, s, 0:P], AT[:, half(hf)], start=True, stop=True)
                pe.matmul(bank(G0[hf] + 1), GU[:, s, P:2 * P], AT[:, half(hf)], start=True, stop=True)

            def front(n, q):
                s, hf = (q // 2) % 2, q % 2
                if not (isinstance(n, int) and n < 2):
                    products(n, q)
                pe.matmul(bank(W0[hf]), HOT[0:t3, s, :], CT[0:t3, half(hf)], start=True, stop=True
                          ).then_inc(S(m + ".front"), 1)

            def down(n, q):
                s = (q // 2) % 2
                hf = q % 2
                if q % 2 == 0:
                    if isinstance(n, int):
                        pe.wait_ge(S(f"{m}.dn{s}"), 16 * (n // 4 + 1))
                    else:
                        pe.wait_ge(S(f"{m}.dn{s}"), n_parts[0][1])
                pe.wait_ge(S(m + ".hid"), n + 1)
                for t in range(TPB):
                    last = pe.matmul(PS[:, 6 - hf, tile(t)], HID(q % 2)[:, tile(t)], DN[:, s, :],
                                     start=False, stop=True, skip_group_check=True)
                last.then_inc(S(m + ".down"), 1)

            products(0, 0)
            products(1, 1)
            pe.wait_ge(S(m + ".cp"), 1)
            out = bank(4).bitcast(BF16)
            for t in range(NT):
                last = pe.transpose(out[0:t3, tile(t)], CP[:, t, :, 0:E1].rearrange("p a b -> p (a b)")
                                    if E1 == 17 else CPV(m)[:, t, :], cb("ident"))
            last.then_inc(S(m + ".ct_turned"), 1)
            pe.wait_ge(S(m + ".ct_in"), 1)

            n_parts = [None]
            front(0, 0)
            for u in range(4):
                front(u + 1, (u + 1) % 4)
                down(u, u)
            last4 = (units - 1) // 4
            with pe.Fori(1, last4) as i:
                for q in range(4):
                    ahead = (i + 2) if q == 3 else (i + 1)
                    n_parts[0] = (ahead * 32, (i + 1) * 16)
                    front(i * 4 + (q + 1), (q + 1) % 4)
                    down(i * 4 + q, q)
            for u in range(4 * last4, units):
                if u + 1 < units:
                    front(u + 1, (u + 1) % 4)
                down(u, u % 4)

        def HID(s):
            return PR[:, s, :]

        def CPV(m):
            n = 3 * MOE[m]["table"]
            return CP[:, :, :, :].rearrange("p t a b -> p (t a b)")[:, 0:NT * n].rearrange("p (t n) -> p t n", t=NT)

        def scalar_experts(act, m, link):
            c = MOE[m]
            E1, t3 = c["table"], 3 * c["table"]
            act.wait_ge(S(m + ".ct_turned"), 1)
            act.activation(CT[0:t3, :], bank(4).bitcast(BF16)[0:t3, :], ACT.Copy).then_inc(S(m + ".ct_in"), 1)
            def unit(n, q):
                act.wait_ge(S(m + ".front"), n + 1)
                if not (isinstance(n, int) and n < 2):
                    act.wait_ge(S(m + ".hid"), n - 1)
                act.activation(PR[:, 2 + q % 2, :], bank(2 * (q % 2)), ACT.Silu).then_inc(S(m + ".act"), 1)

            unit_loop(act, 2 * c["blocks"], unit)

        def vector_experts(v, m, link):
            c = MOE[m]

            def unit(n, q):
                s = q % 2
                v.wait_ge(S(m + ".act"), n + 1)
                if not (isinstance(n, int) and n < 2):
                    v.wait_ge(S(m + ".down"), n - 1)
                src = PR[:, 2 + s, :]
                v.tensor_tensor(PR[:, 4 + s, :], src, bank(2 * s + 1), ALU.mult).then_inc(S(m + ".gated"), 1)
                v.wait_ge(S(m + ".gated"), n + 1)
                v.tensor_tensor(HID(s), PR[:, 4 + s, :], bank((4, 7)[s]), ALU.mult).then_inc(S(m + ".hid"), 1)

            unit_loop(v, 2 * c["blocks"], unit)

        UNITS = 2 * PER_EXPERT
        L3_EXPERTS = MOE["L3"]["experts"]
        L3_UNITS = 2 * MOE["L3"]["blocks"]

        def tensor_experts_3(pe):
            E1 = MOE["L3"]["table"]
            tensor_router(pe, "L3")

            def front(e, q):
                s, n = (q // 2) % 2, e * UNITS + q
                if q % 2 == 0:
                    pe.wait_ge(S(f"L3.gu{s}"), e * 32 + 16 * (q // 4 + 1))
                if not (isinstance(e, int) and n < 4):
                    pe.wait_ge(S("L3.hid"), n - 3)
                pe.matmul(bank(q % 4), GU[:, s, 0:P], AT[:, half(q % 2)], start=True, stop=True
                          ).then_inc(S("L3.front"), 1)

            def down(e, q):
                s, n, hf = (q // 2) % 2, e * UNITS + q, q % 2
                if q % 2 == 0:
                    pe.wait_ge(S(f"L3.dn{s}"), e * 32 + 16 * (q // 4 + 1))
                if q < 2 and not (isinstance(e, int) and e == 0):
                    pe.wait_ge(S("L3.mixed"), e * 2 + (hf - 1))
                pe.wait_ge(S("L3.hid"), n + 1)
                for t in range(TPB):
                    last = pe.matmul(PS[:, 6 - hf, tile(t)], PR[:, q % 4, tile(t)], DN[:, s, :],
                                     start=(q < 2 and t == 0), stop=True, skip_group_check=True)
                last.then_inc(S("L3.down"), 1)

            def expert(e, units=UNITS, more=True):
                for q in range(units):
                    if isinstance(e, int) and e * UNITS + q == 0:
                        pass
                    elif q + 1 < units:
                        front(e, q + 1)
                    elif more:
                        front(e + 1, 0)
                    down(e, q)

            front(0, 0)
            front(0, 1)
            pe.wait_ge(S("L3.cp"), 1)
            for hf in range(2):
                for t in range(TPB):
                    last = pe.transpose(PS[0:E1, 2 + hf, tile(t)], CW[:, TPB * hf + t, 0:E1], cf("ident"))
            last.then_inc(S("L3.c_turned"), 1)
            pe.wait_ge(S("L3.c_in"), 1)
            for hf in range(2):
                for t in range(TPB):
                    last = pe.matmul(PS[:, 4 + 3 * hf, tile(t)], C32[0:E1, tile(TPB * hf + t)], w("L3", "b2"),
                                     start=(t == 0), stop=True, skip_group_check=True)
            last.then_inc(S("L3.shift"), 1)
            expert(0)
            with pe.Fori(1, L3_EXPERTS) as e:
                expert(e)
            expert(L3_EXPERTS, L3_UNITS - UNITS * L3_EXPERTS, more=False)

        def scalar_experts_3(act):
            E1 = MOE["L3"]["table"]
            act.wait_ge(S("L3.b1g"), 1)
            flat_b1g = b1g[:, :, :].rearrange("p b c -> p (b c)")

            def expert(e, first=0, units=UNITS):
                for q in range(first, units):
                    if q % 4 == 0:
                        act.activation(GB[:, q // 2:q // 2 + 2, :].rearrange("p b c -> p (b c)"),
                                       flat_b1g[:, bass.ds(e * UNITS + q, 4)], ACT.Copy).then_inc(S("L3.gb"), 1)
                        act.wait_ge(S("L3.gb"), e * 2 + (q // 4 + 1))
                    n = e * UNITS + q
                    act.wait_ge(S("L3.front"), n + 1)
                    if not (isinstance(e, int) and n < 4):
                        act.wait_ge(S("L3.down"), n - 3)
                    act.activation(PR[:, q % 4, :], bank(q % 4), ACT.Gelu, bias=GB[:, q // 2, 0:1],
                                   scale=GB[:, q // 2, 1:2]).then_inc(S("L3.hid"), 1)

            expert(0, 0, 2)
            act.wait_ge(S("L3.c_turned"), 1)
            act.activation(C32[0:E1, :], PS[0:E1, 2:4, :].rearrange("p a b -> p (a b)"), ACT.Copy
                           ).then_inc(S("L3.c_in"), 1)
            expert(0, 2)
            with act.Fori(1, L3_EXPERTS) as e:
                expert(e)
            expert(L3_EXPERTS, 0, L3_UNITS - UNITS * L3_EXPERTS)

        def vector_experts_3(v, link):
            def expert(e, done, before=None):
                if not (isinstance(e, int) and e == 0):
                    v.wait_ge(S("L3.mixed"), e * 2)
                v.tensor_copy(CE[:, :], CW[:, :, bass.ds(e, 1)].rearrange("p t o -> p (t o)")
                              ).then_inc(S("L3.ce"), 1)
                v.wait_ge(S("L3.ce"), e + 1)
                for hf in range(2):
                    v.wait_ge(S("L3.down"), done + hf)
                    for t in range(TPB):
                        to = T0[:, tile(TPB * hf + t)]
                        last = v.scalar_tensor_tensor(out=to, in0=PS[:, 6 - hf, tile(t)],
                                                      scalar=CE[:, TPB * hf + t:TPB * hf + t + 1],
                                                      in1=to, op0=ALU.mult, op1=ALU.add)
                    last.then_inc(S("L3.mixed"), 1)

            v.wait_ge(S("L3.shift"), 1)
            for hf in range(2):
                link(v.tensor_copy(T0[:, half(hf)], bank(4 + 3 * hf)))
            expert(0, UNITS - 1)
            with v.Fori(1, L3_EXPERTS) as e:
                expert(e, e * UNITS + (UNITS - 1))
            expert(L3_EXPERTS, L3_UNITS - 1)

        def rank_of(v, link, s, n, k, before, out, scratch, scratch2):
            G = s.shape[1]
            big = [P, G, n, n]
            sj = s.unsqueeze(2).to_broadcast(big)
            si = s.unsqueeze(3).to_broadcast(big)
            bf = before.rearrange("p (i j) -> p i j", i=n).unsqueeze(1).to_broadcast(big)
            s1 = scratch[:, 0:G * n * n].rearrange("p (g i j) -> p g i j", g=G, i=n)
            s2 = scratch2[:, 0:G * n * n].rearrange("p (g i j) -> p g i j", g=G, i=n)
            v.tensor_tensor(s1, sj, si, ALU.is_gt).then_inc(link.sem, 1)
            link.n += 1
            link(v.tensor_tensor(s2, sj, si, ALU.is_equal))
            link(v.tensor_tensor(s2, s2, bf, ALU.mult))
            link(v.tensor_tensor(s1, s1, s2, ALU.add))
            link(v.tensor_reduce(out, s1, AX.X, ALU.add))
            link(v.tensor_scalar(out, out, float(k) - 0.5, None, ALU.is_lt))

        def top_of(v, link, s, n, k, out):
            top = T2[:, 0:8 * NT].rearrange("p (t e) -> p t e", t=NT)
            above, same, nth = (T2[:, 128 * i:128 * i + NT * n].rearrange("p (t e) -> p t e", t=NT)
                                for i in (1, 2, 3))
            for t in range(NT):
                last = v.max(top[:, t, :], s[:, t, :])
            link(last)
            kth = top[:, :, k - 1].unsqueeze(2).to_broadcast([P, NT, n])
            v.tensor_tensor(same, s, kth, ALU.is_equal)
            link(v.tensor_tensor(above, s, kth, ALU.is_gt))
            v.tensor_reduce(small[:, 3, :], above, AX.X, ALU.add)
            link(v.tensor_tensor_scan(T2[:, 384:384 + NT * n], cf(f"keep{n}"), T2[:, 256:256 + NT * n], 0.0,
                                      ALU.mult, ALU.add))
            link(v.tensor_tensor(nth, nth, small[:, 3, :].unsqueeze(2).to_broadcast([P, NT, n]), ALU.add))
            link(v.scalar_tensor_tensor(out=same, in0=nth, scalar=float(k), in1=same, op0=ALU.is_le, op1=ALU.mult))
            link(v.tensor_tensor(out, above, same, ALU.add))

        def bc(ap, n):
            return ap.unsqueeze(2).to_broadcast([P, NT, n])

        def vector_route(v, m, link):
            c = MOE[m]
            n, E1 = c["experts"], c["table"]
            lg = T0[:, 0:NT * 32].rearrange("p (t e) -> p t e", t=NT)
            sc = T0[:, 256:256 + NT * n].rearrange("p (t e) -> p t e", t=NT)
            sel = T0[:, 512:512 + NT * n].rearrange("p (t e) -> p t e", t=NT)
            tmp = T0[:, 768:768 + NT * n].rearrange("p (t e) -> p t e", t=NT)
            r1 = small[:, 2, :]
            v.wait_ge(S(m + ".logits"), 1)
            lp = bank(7)[:, 0:NT * 32].rearrange("p (t e) -> p t e", t=NT)
            NR = {"L0": 9, "L1": 16, "L3": 8}[m]
            if m == "L3":
                link(v.tensor_tensor(lg[:, :, 0:8], lp[:, :, 0:8],
                                     w("L3", "router3_b").unsqueeze(1).to_broadcast([P, NT, 8]), ALU.add))
            else:
                link(v.tensor_copy(lg[:, :, 0:NR], lp[:, :, 0:NR]))
            if m == "L1":
                v.engine_nop().then_inc(S(m + ".lg"), 1) if False else \
                    v.tensor_copy(tmp, lg[:, :, 0:16]).then_inc(S(m + ".lg"), 1)
                v.wait_ge(S(m + ".sg"), 1)
                sfc = T1[:, 0:128].rearrange("p (t e) -> p t e", t=NT)
                link(v.tensor_tensor(sfc, sc, w("L1", "router1_b").unsqueeze(1).to_broadcast([P, NT, 16]), ALU.add))
                g4 = T1[:, 0:128].rearrange("p (g e) -> p g e", e=4)
                pairs = T1[:, 0:128].rearrange("p (g c e) -> p g c e", c=2, e=2)
                high = T1[:, 128:192].rearrange("p (g c) -> p g c", c=2)
                low = T1[:, 192:256].rearrange("p (g c) -> p g c", c=2)
                best, second, gs = T1[:, 480:512], T1[:, 448:480], T1[:, 256:288]
                v.tensor_tensor(high, pairs[:, :, :, 0], pairs[:, :, :, 1], ALU.max)
                link(v.tensor_tensor(low, pairs[:, :, :, 0], pairs[:, :, :, 1], ALU.min))
                v.tensor_tensor(best, high[:, :, 0], high[:, :, 1], ALU.max)
                v.tensor_tensor(second, high[:, :, 0], high[:, :, 1], ALU.min)
                link(v.tensor_tensor(gs, low[:, :, 0], low[:, :, 1], ALU.max))
                link(v.tensor_tensor(second, second, gs, ALU.max))
                link(v.tensor_tensor(gs, best, second, ALU.add))
                gsel = T1[:, 288:320].rearrange("p (t g) -> p t g", t=NT)
                rank_of(v, link, gs.rearrange("p (t g) -> p t g", t=NT), 4, 2, cf("before4"), gsel, T2, T3)
                chosen = T1[:, 288:320].unsqueeze(2).to_broadcast([P, 32, 4])
                mk = T1[:, 320:448].rearrange("p (g e) -> p g e", e=4)
                link(v.tensor_tensor(mk, g4, chosen, ALU.mult))
                low = T1[:, 448:480]
                link(v.tensor_scalar(low, T1[:, 288:320], -NEG, NEG, ALU.mult, ALU.add))
                link(v.tensor_tensor(mk, mk, low.unsqueeze(2).to_broadcast([P, 32, 4]), ALU.add))
                mt = T1[:, 320:448].rearrange("p (t e) -> p t e", t=NT)
                top_of(v, link, mt, 16, 4, sel)
                link(v.tensor_tensor(sel, sel, sc, ALU.mult))
                link(v.tensor_reduce(r1, sel, AX.X, ALU.add))
                link(v.tensor_scalar(r1, r1, 1e-20, None, ALU.add))
                link(v.reciprocal(r1, r1))
                link(v.tensor_tensor(sel, sel, bc(r1, 16), ALU.mult))
                link(v.tensor_scalar(CW[:, :, 0:16], sel, 2.5, None, ALU.mult))
                link(v.memset(CW[:, :, 16], 1.0))
            else:
                link(v.tensor_reduce(r1, lg[:, :, 0:8], AX.X, ALU.max))
                v.tensor_tensor(tmp, lg[:, :, 0:8], bc(r1, 8), ALU.subtract).then_inc(S(m + ".lg"), 1)
                v.wait_ge(S(m + ".sg"), 1)
                link(v.tensor_reduce(r1, sc, AX.X, ALU.add))
                link(v.reciprocal(r1, r1))
                link(v.tensor_tensor(sc, sc, bc(r1, 8), ALU.mult))
                top_of(v, link, sc, 8, 2, sel)
                if m == "L0":
                    link(v.tensor_tensor(CW[:, :, 0:8], sel, sc, ALU.mult))
                    v.wait_ge(S("L0.sw"), 1)
                    link(v.tensor_copy(CW[:, :, 8], small[:, 6, :]))
                else:
                    link(v.tensor_tensor(sel, sel, sc, ALU.mult))
                    link(v.tensor_reduce(r1, sel, AX.X, ALU.add))
                    link(v.reciprocal(r1, r1))
                    link(v.tensor_tensor(CW[:, :, 0:8], sel, bc(r1, 8), ALU.mult))
                    v.wait_ge(S("L3.sw"), 1)
                    v.tensor_copy(CW[:, :, 8], vec[:, 0:1].to_broadcast([P, NT])).then_inc(S("L3.cp"), 1)
                    v.wait_ge(S("L3.cp"), 1)
                    return
            n3 = 3 * E1
            cp = CPV(m).rearrange("p t (a e) -> p t a e", a=3)
            cw, left = CW[:, :, 0:E1], CWR[:, :, 0:E1]
            link(v.tensor_copy(cp[:, :, 0, :], cw))
            link(v.tensor_tensor(left, cw, cp[:, :, 0, :], ALU.subtract))
            link(v.tensor_copy(cp[:, :, 1, :], left))
            v.tensor_tensor(cp[:, :, 2, :], left, cp[:, :, 1, :], ALU.subtract).then_inc(S(m + ".cp"), 1)

        def scalar_route(act, m):
            c = MOE[m]
            n = c["experts"]
            act.wait_ge(S(m + ".lg"), 1)
            fn = ACT.Sigmoid if m == "L1" else ACT.Exp
            act.activation(T0[:, 256:256 + NT * n], T0[:, 768:768 + NT * n], fn).then_inc(S(m + ".sg"), 1)
            if m == "L0":
                act.activation(small[:, 6, :], T0[:, 0:NT * 32].rearrange("p (t e) -> p t e", t=NT)[:, :, 8],
                               ACT.Sigmoid).then_inc(S("L0.sw"), 1)
            if m == "L3":
                act.activation(vec[:, 0:1], w("L3", "shared_w"), ACT.Sigmoid).then_inc(S("L3.sw"), 1)

        def vector_add_experts(v, m, link, hf):
            v.wait_ge(S(m + ".down"), 2 * MOE[m]["blocks"] - 1 + hf)
            ts = slice(TPB * hf, TPB * (hf + 1))
            y = bank(6 - hf).rearrange("p (t d) -> p t d", t=TPB)
            if m == "L1":
                v.wait_ge(S("x_plus_norm"), 1)
            link(v.tensor_tensor(X[:, ts, :], X[:, ts, :], y, ALU.add))

        pass_ = ctx_loop.enter_context(nc.Fori(0, PASSES))
        phase = {}

        def begin_phase():
            phase["sems"], phase["block"] = ExitStack(), ExitStack()
            return phase["block"].enter_context(nc.Block())

        def end_phase():
            phase["block"].close()
            numbers = sorted(x.num for x in sems.values())
            assert numbers == list(range(numbers[0], numbers[0] + len(numbers)))
            nc.all_engine_barrier(sems_to_clear=range(numbers[0], numbers[-1] + 1))
            phase["sems"].close()
            sems.clear()

        def SPIKES(n):
            return PR[:, 6 + n % 2, :].bitcast(BF16)[:, HALF * (n // 2 % 2):HALF * (n // 2 % 2 + 1)]

        block = begin_phase()

        @block.sync
        def _(sp):
            sp.wait_ge(ONCE["x_first"], 16)
            sp.dma_start(flat(X), BIG[:, 3, :]).then_inc(S("x_in"), 16)
            sync_stacks(sp, "a")
            sync_max(sp, "a")
            sync_stacks(sp, "s")
            if stop > 1:
                sync_experts(sp, "L0")
            if stop > 2:
                sync_stacks(sp, "l")
            if stop > 3:
                sync_experts(sp, "L1")

        @block.gpsimd
        def _(g):
            chain = Link(g, S("gpsimd_chain"))
            g.wait_ge(ONCE["half_ready"], 1)
            for i, k in enumerate(("n0", "n0m", "n0f", "n1", "n1f")):
                if stop >= i:
                    gpsimd_norm(g, k, chain)
            if stop > 3:
                g.wait_ge(S("n1f_first"), NT)
                g.tensor_tensor(flat(X), flat(X), flat(A), ALU.add).then_inc(S("x_plus_norm"), 1)

        @block.scalar
        def _(act):
            link = Link(act, S("scalar_chain"))
            act.wait_ge(ONCE["wall_L0"], 16)
            act.wait_ge(ONCE["half_ready"], 1)
            scalar_norm(act, "n0")
            scalar_qk(act, "a")
            scalar_softmax(act, "a")
            act.wait_ge(S("a.proj"), 2)
            act.activation(flat(A2), bank(6, 2), ACT.Identity, bias=w("L0", "bp_a")).then_inc(S("a.sum"), 1)
            scalar_qk(act, "s")
            scalar_linear(act, "s")
            scalar_ready(link, ACT.Gelu)
            scalar_norm(act, "n0m")
            for n in range(8):
                hf, m = divmod(n, 4)
                act.wait_ge(S("mlp.up"), n + 1)
                act.activation(BIG[:, m, half(hf)], bank(m), ACT.Gelu,
                               bias=w("L0", "b1m", m, m + 1)).then_inc(S("mlp.gelu"), 1)
            if stop > 1:
                scalar_ready(link, ACT.Exp)
                scalar_norm(act, "n0f")
                scalar_route(act, "L0")
                scalar_experts(act, "L0", link)
            if stop > 2:
                act.wait_ge(ONCE["wall_L1"], 16)
                scalar_ready(link, ACT.Sigmoid)
                scalar_norm(act, "n1")
                scalar_qk(act, "l")
                scalar_linear(act, "l")
            if stop > 3:
                scalar_ready(link, ACT.Sigmoid)
                scalar_norm(act, "n1f")
                scalar_route(act, "L1")
                scalar_experts(act, "L1", link)

        @block.vector
        def _(v):
            link = Link(v, S("vector_chain"))
            v.wait_ge(ONCE["x_first"], 16)
            v.wait_ge(ONCE["wall_L0"], 16)
            v.wait_ge(ONCE["cf_in"], 16)
            vector_norm(v, "n0")
            vector_qk(v, "a", link)
            vector_softmax(v, "a", link)
            vector_qk(v, "s", link)
            vector_linear(v, "s", link)
            v.wait_ge(S("a.sum"), 1)
            for hf in range(2):
                v.wait_ge(S("s.proj"), hf + 1)
                v.scalar_tensor_tensor(out=flat(A2)[:, half(hf)], in0=bank(6 + hf), scalar=w("L0", "bo_s"),
                                       in1=flat(A2)[:, half(hf)], op0=ALU.add, op1=ALU.add
                                       ).then_inc(S("s.sum"), 1)
            vector_norm(v, "n0m", lambda hf: vector_back(v, "mixed", tok(T0), A, link, hf))
            v.wait_ge(S("x_in"), 16)
            link(v.tensor_tensor(flat(X), flat(X), T0[:, :], ALU.add))
            if stop > 1:
                vector_norm(v, "n0f", lambda hf: vector_back(v, "mlp.back", X, X, link, hf))
                vector_route(v, "L0", link)
                vector_experts(v, "L0", link)
            if stop > 2:
                v.wait_ge(ONCE["wall_L1"], 16)
                vector_norm(v, "n1", lambda hf: vector_add_experts(v, "L0", link, hf))
                vector_qk(v, "l", link)
                vector_linear(v, "l", link)
            if stop > 3:
                vector_norm(v, "n1f", lambda hf: vector_back(v, "l.back", X, X, link, hf))
                vector_route(v, "L1", link)
                vector_experts(v, "L1", link)
                for hf in range(2):
                    vector_add_experts(v, "L1", link, hf)

        @block.tensor
        def _(pe):
            pe.wait_ge(ONCE["cf_in"], 16)
            pe.wait_ge(ONCE["zero_in"], 1)
            tensor_norm(pe, "n0")
            tensor_qkv(pe, "a")
            tensor_softmax(pe, "a")
            for hf in range(2):
                pe.wait_ge(S("a.ot"), hf + 1)
                pe.matmul(bank(6 + hf), w("L0", "Wp_a"), OT[:, half(hf)], start=True, stop=True
                          ).then_inc(S("a.proj"), 1)
            tensor_qkv(pe, "s")
            tensor_linear(pe, "s")
            for hf in range(2):
                pe.wait_ge(S("s.ot"), hf + 1)
                pe.matmul(bank(6 + hf), w("L0", "Wo_s"), OT[:, half(hf)], start=True, stop=True
                          ).then_inc(S("s.proj"), 1)
            tensor_back(pe, "mixed", "bo", lambda k, t: flat(A2)[:, tile(t)], lambda k, t: w("L0", "Wo"),
                        ready=lambda hf: pe.wait_ge(S("s.sum"), hf + 1))
            tensor_norm(pe, "n0m")
            for n in range(8):
                hf, m = divmod(n, 4)
                if n < 2:
                    wait_norm(pe, "n0m", n + 1)
                if n >= 4:
                    pe.wait_ge(S("mlp.gelu"), n - 3)
                pe.matmul(bank(m), w("L0", "W1", P * m, P * (m + 1)), T2[:, half(hf)],
                          start=True, stop=True).then_inc(S("mlp.up"), 1)
            tensor_back(pe, "mlp.back", "b2m", lambda k, t: BIG[:, k, tile(t)],
                        lambda k, t: w("L0", "W2", P * k, P * (k + 1)), depth=4,
                        ready=lambda hf: pe.wait_ge(S("mlp.gelu"), 4 * (hf + 1)))
            if stop > 1:
                tensor_norm(pe, "n0f")
                tensor_experts(pe, "L0")
            if stop > 2:
                tensor_norm(pe, "n1")
                tensor_qkv(pe, "l")
                tensor_linear(pe, "l")
                tensor_back(pe, "l.back", "proj_b", lambda k, t: OT[:, tile(t)], lambda k, t: w("L1", "proj_w"),
                            ready=lambda hf: pe.wait_ge(S("l.ot"), hf + 1))
            if stop > 3:
                tensor_norm(pe, "n1f")
                tensor_experts(pe, "L1")

        end_phase()

        block = begin_phase()

        @block.sync
        def _(sp):
            if stop > 6:
                sync_stacks(sp, "f")
                sync_max(sp, "f")
            if stop > 7:
                sync_experts(sp, "L3")
            if stop > 6:
                sp.wait_ge(S("f.gathered"), 2)
                sp.dma_start(BIG[:, 3, :], T["x"][bass.ds((pass_ + 1) * P, P), :]).then_inc(S("next_x"), 16)
                sp.wait_ge(S("next_x"), 16)
            for hf in range(2):
                sp.wait_ge(S("x_final"), TPB * (hf + 1))
                sp.dma_start(T["out"][bass.ds(pass_ * P, P), half(hf)], flat(X)[:, half(hf)]
                             ).then_inc(S("out_done"), 16)
            sp.wait_ge(S("out_done"), 32)

        @block.gpsimd
        def _(g):
            chain = Link(g, S("gpsimd_chain"))
            g.wait_ge(ONCE["wall_L3"], 16)
            chain(g.tensor_tensor(b1g[:, :, 0], w("L3", "b1"), w("L3", "gate"), ALU.mult))
            g.tensor_copy(b1g[:, :, 1], w("L3", "gate")).then_inc(S("L3.b1g"), 1)
            for i, k in enumerate(("n2", "n2f", "n3", "n3f")):
                if stop > i + 4:
                    gpsimd_norm(g, k, chain)
            if stop > 7:
                for hf in range(2):
                    ts = slice(TPB * hf, TPB * (hf + 1))
                    g.wait_ge(S("y_moments"), TPB * (hf + 1))
                    chain(g.tensor_scalar(small[:, 0, ts], moments[:, ts, 1], EPS, None, ALU.add))
                    g.tensor_tensor(small[:, 1, ts], small[:, 0, ts], small[:, 7, ts], ALU.pow
                                    ).then_inc(S("y_rstd"), 1)

        @block.scalar
        def _(act):
            link = Link(act, S("scalar_chain"))
            if stop > 4:
                act.wait_ge(ONCE["wall_L2"], 16)
                act.wait_ge(ONCE["half_ready"], 1)
                scalar_ready(link, ACT.Sigmoid)
                scalar_norm(act, "n2")
                act.wait_ge(S("g.proj"), 4)
                act.activation(T1[:, half(1)], bank(3), ACT.Sigmoid, bias=w("L2", "bo")).then_inc(S("g.z"), 1)
                act.activation(T1[:, half(0)], bank(2), ACT.Tanh, bias=w("L2", "bz")).then_inc(S("g.z"), 1)
                act.wait_ge(S("g.arg"), 1)
                act.activation(T2[:, :], T2[:, :], ACT.Exp).then_inc(S("g.exp"), 1)
                act.wait_ge(S("g.c"), 1)
                act.activation(T3[:, half(1)], T3[:, half(0)], ACT.Tanh).then_inc(S("g.tanh"), 1)
            if stop > 5:
                scalar_norm(act, "n2f")
                for n in range(8):
                    act.wait_ge(S("spk.up"), n + 1)
                    if n >= 4:
                        act.wait_ge(S("spk.h"), n - 3)
                    act.activation(PR[:, n % 4, :], bank(n % 4), ACT.Relu).then_inc(S("spk.relu"), 1)

                def spiked(hf):
                    for step in range(SPIKE_STEPS):
                        n = SPIKE_STEPS * hf + step
                        sign = PR[:, 4 + n % 2, :]
                        act.wait_ge(S("spk.step"), n + 1)
                        if n >= 2:
                            act.wait_ge(S("spk.spiked"), n - 1)
                        act.activation(sign, (T0, T1)[step % 2][:, half(hf)], ACT.Sign, scale=-0.5,
                                       bias=small[:, 7, 0:1]).then_inc(S("spk.sign"), 1)
                        act.wait_ge(S("spk.sign"), n + 1)
                        if n >= 4:
                            act.wait_ge(S("spk.counted"), n - 3)
                        act.activation(SPIKES(n), sign, ACT.Relu).then_inc(S("spk.spiked"), 1)

                spiked(0)
                spiked(1)
            if stop > 6:
                act.wait_ge(ONCE["wall_L3"], 16)
                scalar_norm(act, "n3")
                scalar_qk(act, "f")
                scalar_softmax(act, "f")
            if stop > 7:
                scalar_ready(link, ACT.Exp)
                scalar_norm(act, "n3f")
                scalar_route(act, "L3")
                scalar_experts_3(act)

        @block.vector
        def _(v):
            link = Link(v, S("vector_chain"))
            if stop > 4:
                v.wait_ge(ONCE["wall_L2"], 16)
                vector_norm(v, "n2")
                li, lf = T0[:, half(0)], T0[:, half(1)]
                v.wait_ge(S("g.proj"), 2)
                link(v.tensor_scalar(li, bank(0), w("L2", "bi"), 20.0, ALU.add, ALU.min))
                link(v.tensor_scalar(lf, bank(1), w("L2", "bf"), 20.0, ALU.add, ALU.min))
                link(v.tensor_scalar(T0[:, :], T0[:, :], -20.0, None, ALU.max))
                ms = BIG[:, 0, 0:513]
                link(v.memset(BIG[:, 0, 0:1], 0.0))
                link(v.tensor_tensor_scan(ms[:, 1:513], lf, li, 0.0, ALU.add, ALU.max))
                link(v.tensor_tensor(lf, lf, ms[:, 0:512], ALU.add))
                link(v.tensor_tensor(T2[:, half(0)], li, ms[:, 1:513], ALU.subtract))
                v.tensor_tensor(T2[:, half(1)], lf, ms[:, 1:513], ALU.subtract).then_inc(S("g.arg"), 1)
                v.wait_ge(S("g.exp"), 1)
                v.wait_ge(S("g.z"), 2)
                link(v.tensor_tensor(T2[:, half(0)], T2[:, half(0)], T1[:, half(0)], ALU.mult))
                v.tensor_tensor_scan(T3[:, half(0)], T2[:, half(1)], T2[:, half(0)], 0.0, ALU.mult, ALU.add
                                     ).then_inc(S("g.c"), 1)
                v.wait_ge(S("g.tanh"), 1)
                v.tensor_tensor(OT[:, half(0)], T1[:, half(1)], T3[:, half(1)], ALU.mult).then_inc(S("g.h"), 1)
            if stop > 5:
                vector_norm(v, "n2f", lambda hf: vector_back(v, "g.back", X, X, link, hf))
                for n in range(8):
                    v.wait_ge(S("spk.relu"), n + 1)
                    v.scalar_tensor_tensor(out=BIG[:, n % 4, half(n // 4)], in0=bank(n % 4), scalar=0.0,
                                           in1=PR[:, n % 4, :], op0=ALU.max, op1=ALU.mult
                                           ).then_inc(S("spk.h"), 1)

                def spikes(hf):
                    v.wait_ge(S("spk.back"), hf + 1)
                    y, u = bank(4 + hf), T3[:, half(hf)]
                    m = [T0[:, half(hf)], T1[:, half(hf)]]
                    v.tensor_scalar(m[0], y, -1.0, None, ALU.mult).then_inc(S("spk.step"), 1)
                    v.wait_ge(S("spk.step"), SPIKE_STEPS * hf + 1)
                    for step in range(1, SPIKE_STEPS):
                        old, new = m[(step - 1) % 2], m[step % 2]
                        link(v.scalar_tensor_tensor(out=u, in0=old, scalar=0.9, in1=y,
                                                    op0=ALU.mult, op1=ALU.subtract))
                        if step >= 2:
                            v.wait_ge(S("spk.sign"), SPIKE_STEPS * hf + step - 1)
                        v.scalar_tensor_tensor(out=new, in0=old, scalar=-1.0, in1=u,
                                               op0=ALU.is_lt, op1=ALU.add).then_inc(S("spk.step"), 1)
                        v.wait_ge(S("spk.step"), SPIKE_STEPS * hf + step + 1)
                    v.wait_ge(S("spk.counted"), SPIKE_STEPS * (hf + 1))
                    ts = slice(TPB * hf, TPB * (hf + 1))
                    link(v.scalar_tensor_tensor(out=X[:, ts, :], in0=bank(6 + hf).rearrange("p (t d) -> p t d", t=TPB),
                                                scalar=1.0 / SPIKE_STEPS, in1=X[:, ts, :],
                                                op0=ALU.mult, op1=ALU.add))
                if stop == 6:
                    spikes(0)
                    spikes(1)
            if stop > 6:
                v.wait_ge(ONCE["wall_L3"], 16)
                vector_norm(v, "n3", spikes)
                vector_qk(v, "f", link)
                vector_softmax(v, "f", link)
            if stop > 7:
                vector_norm(v, "n3f", lambda hf: vector_back(v, "f.back", X, X, link, hf))
                vector_route(v, "L3", link)
                shift = w("L3", "ln_b3").unsqueeze(1).to_broadcast([P, NT, D])
                link(v.tensor_tensor(X[:, :, :], X[:, :, :], shift, ALU.add))
                vector_experts_3(v, link)
                y = tok(T0)
                for hf in range(2):
                    v.wait_ge(S("L3.mixed"), 2 * L3_EXPERTS + hf + 1)
                    for t in range(TPB * hf, TPB * (hf + 1)):
                        v.bn_stats(stats[:, t, :], y[:, t, :]).then_inc(S("y_stats"), 1)
                    v.wait_ge(S("y_stats"), TPB * (hf + 1))
                    for t in range(TPB * hf, TPB * (hf + 1)):
                        v.bn_aggr(moments[:, t, :], stats[:, t, :]).then_inc(S("y_moments"), 1)
                v.wait_ge(S("y_moments"), NT)
                for hf in range(2):
                    for t in range(TPB * hf, TPB * (hf + 1)):
                        v.scalar_tensor_tensor(out=tok(T1)[:, t, :], in0=y[:, t, :], scalar=moments[:, t, 0:1],
                                               in1=w("L3", "ln_g3"), op0=ALU.subtract, op1=ALU.mult
                                               ).then_inc(S("y_scaled"), 1)
                    v.wait_ge(S("y_rstd"), hf + 1)
                    v.wait_ge(S("y_scaled"), TPB * (hf + 1))
                    for t in range(TPB * hf, TPB * (hf + 1)):
                        v.scalar_tensor_tensor(out=X[:, t, :], in0=tok(T1)[:, t, :], scalar=small[:, 1, t:t + 1],
                                               in1=X[:, t, :], op0=ALU.mult, op1=ALU.add
                                               ).then_inc(S("x_final"), 1)
            else:
                v.memset(vec[:, 3:4], 0.0).then_inc(S("x_final"), 2 * TPB)

        @block.tensor
        def _(pe):
            if stop > 4:
                tensor_norm(pe, "n2")
                wait_norm(pe, "n2", 2)
                for i, m in enumerate(("Wi", "Wf", "Wz", "Wo")):
                    for b in range(B):
                        last = pe.matmul(PS[64 * b:64 * b + 64, i, :], w("L2", m), NTT[:, half(b)],
                                         start=True, stop=True, tile_position=(0, 64 * b))
                    last.then_inc(S("g.proj"), 1)
                pe.wait_ge(S("g.h"), 1)
                tensor_back(pe, "g.back", "bp", lambda k, t: OT[64 * (t // TPB):64 * (t // TPB) + 64, tile(t % TPB)],
                            lambda k, t: w("L2", "Wp")[64 * (t // TPB):64 * (t // TPB) + 64, :])
            if stop > 5:
                tensor_norm(pe, "n2f")
                for n in range(8):
                    hf, m = divmod(n, 4)
                    if n < 2:
                        wait_norm(pe, "n2f", n + 1)
                    if n >= 4:
                        pe.wait_ge(S("spk.h"), n - 3)
                    pe.matmul(bank(n % 4), w("L2", "W_fc", P * m, P * (m + 1)), AT[:, half(hf)],
                              start=True, stop=True).then_inc(S("spk.up"), 1)
                tensor_back(pe, "spk.back", None, lambda k, t: BIG[:, k, tile(t)],
                            lambda k, t: w("L2", "W_proj", P * k, P * (k + 1)), depth=4,
                            ready=lambda hf: pe.wait_ge(S("spk.h"), 4 * (hf + 1)))

                def counted(hf):
                    for step in range(SPIKE_STEPS):
                        n = SPIKE_STEPS * hf + step
                        pe.wait_ge(S("spk.spiked"), n + 1)
                        pe.matmul(bank(6 + hf), cb("ident"), SPIKES(n), start=(step == 0), stop=True,
                                  skip_group_check=True).then_inc(S("spk.counted"), 1)

                counted(0)
                counted(1)
            if stop > 6:
                tensor_norm(pe, "n3")
                tensor_qkv(pe, "f")
                tensor_softmax(pe, "f")
                tensor_back(pe, "f.back", "bo3", lambda k, t: OT[:, tile(t)], lambda k, t: w("L3", "wo"),
                            ready=lambda hf: pe.wait_ge(S("f.ot"), hf + 1))
            if stop > 7:
                tensor_norm(pe, "n3f")
                tensor_experts_3(pe)

        end_phase()


class Link:

    def __init__(self, eng, sem):
        self.eng, self.sem, self.n = eng, sem, 0

    def __call__(self, instruction):
        self.n += 1
        instruction.then_inc(self.sem, 1)
        self.eng.wait_ge(self.sem, self.n)


STOP = 99


def kernel(**inputs):
    import concourse.bacc as _bacc
    from concourse.bass_utils import run_bass_kernel_spmd as _run

    nc = _bacc.Bacc("TRN2", target_bir_lowering=False, num_devices=1)
    arrays, at = lay_out(inputs)
    T = {n: nc.dram_tensor("in_" + n, a.shape, mybir.dt.from_np(a.dtype), kind="ExternalInput").ap()
         for n, a in arrays.items()}
    T = {n: ap.bitcast(BF16) if arrays[n].dtype == np.uint16 else ap for n, ap in T.items()}
    T["out"] = nc.dram_tensor("out", (PASSES * P, NT * D), F32, kind="ExternalOutput").ap()
    program(nc, T, at, {n: a.shape for n, a in arrays.items()}, STOP)
    r = _run(nc, [{"in_" + n: a for n, a in arrays.items()}], core_ids=[0])
    out = np.asarray(r.results[0]["out"])
    return np.ascontiguousarray(out.reshape(PASSES, P, NT, D).transpose(0, 2, 1, 3).reshape(PASSES * B, L, D))
```
